# Optimizing a Trainium2 kernel written in Bass

```python
import numpy as np
import jax
import jax.numpy as jnp

def _softmax(x, axis=-1):
    return jax.nn.softmax(x, axis=axis)

def _gelu(x):
    return jax.nn.gelu(x, approximate=True)

def _silu(x):
    return jax.nn.silu(x)

def _sigmoid(x):
    return jax.nn.sigmoid(x)

def _layernorm(x, axis=-1, eps=1e-05):
    m = jnp.mean(x, axis=axis, keepdims=True)
    v = jnp.var(x, axis=axis, keepdims=True)
    return (x - m) / jnp.sqrt(v + eps)

def _scatter_add(tgt, idx, src, axis=0):
    return tgt.at[idx].add(src)

def _segment_sum(src, seg, n):
    return jax.ops.segment_sum(src, seg, n)
kernel_name = 'mk_decoder_postln_d4_seqx_r8_c1f794'

def setup_inputs(seed: int=0):
    np.random.seed(seed)
    _w = jnp.asarray

    def _rec_inputs():
        import jax
        import jax.numpy as jnp
        _rk = jax.random.key(seed)
        x = 0.0001212 + 1 * jax.random.normal(jax.random.fold_in(_rk, 1), (32, 64, 256), jnp.float32)
        _lenS = 64 - jax.random.randint(jax.random.fold_in(_rk, 7), (32,), 0, max(1, 64 // 4) + 1, jnp.int32)
        _lenS2 = 64 - jax.random.randint(jax.random.fold_in(_rk, 8), (32,), 0, max(1, 64 // 4) + 1, jnp.int32)
        _ctx_2048P = jax.random.normal(jax.random.fold_in(_rk, 11), (32, 16, 256), jnp.float32)
        _ctx_2048c = jax.random.dirichlet(jax.random.fold_in(_rk, 511), 0.3 * jnp.ones((16,), jnp.float32), (32, 64))
        _ctx_2048t = jnp.einsum('bsk,bkd->bsd', _ctx_2048c, _ctx_2048P)
        _ctx_2048t = _ctx_2048t * jax.lax.rsqrt(jnp.mean(jnp.square(_ctx_2048t)) + 1e-12) * 0.953939
        ctx_2048 = 0.000173663 + 1.0001 * (_ctx_2048t + 0.3 * jax.random.normal(jax.random.fold_in(_rk, 611), (32, 64, 256), jnp.float32))
        return (x, ctx_2048)
    x, ctx_2048 = _rec_inputs()

    def _L0_attn_setup():
        import math
        import jax, jax.numpy as jnp
        import numpy as np
        HID = 256
        H = 16
        HKV = 8
        D = HID // H
        F = D
        SEQ = 256
        BATCH = 2
        THETA = 10000.0

        def _rotate_half(x):
            x1, x2 = (x[..., :x.shape[-1] // 2], x[..., x.shape[-1] // 2:])
            return jnp.concatenate((-x2, x1), axis=-1)

        def _softmax_kernel(x, R):
            n = jnp.sqrt(jnp.sum(x * x, axis=-1, keepdims=True))
            x = x / jnp.maximum(n, 1e-06)
            p = jnp.einsum('...d,ed->...e', x, R)
            feats = jnp.concatenate([jnp.sin(p), jnp.cos(p)], axis=-1)
            return feats / math.sqrt(F)
        key = jax.random.key(seed)
        ks = jax.random.split(key, 10)
        s = lambda k, shape, scale=0.02: jax.random.normal(k, shape, dtype=jnp.float32) * scale
        return {'hidden_states': jax.random.normal(ks[0], (BATCH, SEQ, HID), dtype=jnp.float32), 'Wq': s(ks[1], (HID, HID)), 'bq': s(ks[2], (HID,)), 'Wk': s(ks[3], (HKV * D, HID)), 'bk': s(ks[4], (HKV * D,)), 'Wv': s(ks[5], (HKV * D, HID)), 'bv': s(ks[6], (HKV * D,)), 'Wo': s(ks[7], (HID, HID)), 'bo': s(ks[8], (HID,)), 'rand_matrix': jax.random.normal(ks[9], (F // 2, D), dtype=jnp.float32)}
    _L0_attn_all = _L0_attn_setup()
    _L0_attn_in = {k: v for k, v in _L0_attn_all.items() if k in ('Wq', 'bq', 'Wk', 'bk', 'Wv', 'bv', 'Wo', 'bo', 'rand_matrix')}
    del _L0_attn_all

    def _L0_xattn_setup():
        import jax, jax.numpy as jnp
        import numpy as np
        B_DIM, T_DIM, C_DIM = (16, 128, 256)

        def _wkv(w, u, k, v):
            Bn, Tn, Cn = k.shape
            NEG_INF = jnp.float32(-1e+38)

            def step(carry, kv_t):
                p, q, o = carry
                kt, vt = kv_t
                no = jnp.maximum(o, u + kt)
                A = jnp.exp(o - no)
                E = jnp.exp(u + kt - no)
                y = (A * p + E * vt) / (A * q + E)
                no2 = jnp.maximum(w + o, kt)
                A2 = jnp.exp(w + o - no2)
                E2 = jnp.exp(kt - no2)
                return ((A2 * p + E2 * vt, A2 * q + E2, no2), y)
            init = (jnp.zeros((Bn, Cn), k.dtype), jnp.zeros((Bn, Cn), k.dtype), jnp.full((Bn, Cn), NEG_INF, k.dtype))
            kT = jnp.moveaxis(k, 1, 0)
            vT = jnp.moveaxis(v, 1, 0)
            _, yT = jax.lax.scan(step, init, (kT, vT))
            return jnp.moveaxis(yT, 0, 1)
        key = jax.random.key(seed)
        k1, k2, k3, k4 = jax.random.split(key, 4)
        w = -jnp.exp(jax.random.normal(k1, (C_DIM,), jnp.float32))
        u = jax.random.normal(k2, (C_DIM,), jnp.float32)
        k = jax.random.normal(k3, (B_DIM, T_DIM, C_DIM), jnp.float32)
        v = jax.random.normal(k4, (B_DIM, T_DIM, C_DIM), jnp.float32)
        return {'B': B_DIM, 'T': T_DIM, 'C': C_DIM, 'w': w, 'u': u, 'k': k, 'v': v}
    _L0_xattn_all = _L0_xattn_setup()
    _L0_xattn_in = {k: v for k, v in _L0_xattn_all.items() if k in ('w', 'u')}
    del _L0_xattn_all

    def _L0_ffn_setup():
        import jax, jax.numpy as jnp
        import numpy as np
        H = 256
        I = 176
        E = 16
        TOP_K = 4
        N_GROUP = 4
        TOPK_GROUP = 2
        SCALE = 16.0
        N_SHARED = 2
        SI = I * N_SHARED
        B, S = (1, 256)

        def _silu_and_mul(gu):
            g, u = jnp.split(gu, 2, axis=-1)
            return jax.nn.silu(g) * u
        key = jax.random.key(seed)
        ks = jax.random.split(key, 6)
        inv_h = 1.0 / np.sqrt(H)
        inv_i = 1.0 / np.sqrt(I)
        inv_si = 1.0 / np.sqrt(SI)
        return {'hidden_states': jax.random.normal(ks[0], (B, S, H), jnp.float32), 'gate_w': jax.random.normal(ks[1], (E, H), jnp.float32) * inv_h, 'w_gate_up': jax.random.normal(ks[2], (E, H, 2 * I), jnp.float32) * inv_h, 'w_down': jax.random.normal(ks[3], (E, I, H), jnp.float32) * inv_i, 'shared_gate_up': jax.random.normal(ks[4], (H, 2 * SI), jnp.float32) * inv_h, 'shared_down': jax.random.normal(ks[5], (SI, H), jnp.float32) * inv_si}
    _L0_ffn_all = _L0_ffn_setup()
    _L0_ffn_in = {k: v for k, v in _L0_ffn_all.items() if k in ('gate_w', 'w_gate_up', 'w_down', 'shared_gate_up', 'shared_down')}
    del _L0_ffn_all

    def _L1_attn_setup():
        import jax, jax.numpy as jnp
        import numpy as np
        B, T, HID = (2, 256, 256)
        NKH, NVH = (16, 32)
        DK, DV = (128, 128)
        R = NVH // NKH
        KDIM, VDIM = (NKH * DK, NVH * DV)
        CONV_K = 4
        EPS = 1e-06

        def _silu(x):
            return x * jax.nn.sigmoid(x)

        def _l2norm(x, eps=1e-06):
            return x * jax.lax.rsqrt(jnp.sum(x * x, axis=-1, keepdims=True) + eps)
        key = jax.random.key(seed)
        ks = jax.random.split(key, 8)
        w = lambda k, shape, sc=0.02: jax.random.normal(k, shape, jnp.float32) * sc
        return {'hidden_states': jax.random.normal(ks[0], (B, T, HID), jnp.float32), 'W_qkvz': w(ks[1], (HID, 2 * KDIM + 2 * VDIM)), 'W_ba': w(ks[2], (HID, 2 * NVH)), 'conv_w': w(ks[3], (2 * KDIM + VDIM, CONV_K), 0.1), 'dt_bias': jnp.ones((NVH,), jnp.float32), 'A_log': jax.random.normal(ks[4], (NVH,), jnp.float32), 'norm_weight': jnp.ones((DV,), jnp.float32), 'W_out': w(ks[5], (VDIM, HID))}
    _L1_attn_all = _L1_attn_setup()
    _L1_attn_in = {k: v for k, v in _L1_attn_all.items() if k in ('W_qkvz', 'W_ba', 'conv_w', 'dt_bias', 'A_log', 'norm_weight', 'W_out')}
    del _L1_attn_all

    def _L1_xattn_setup():
        import jax, jax.numpy as jnp
        import numpy as np
        DIM = 256
        NHEADS = 32
        HEAD_DIM = DIM // NHEADS
        EPS = 1e-06

        def _rmsnorm(t):
            return t * jax.lax.rsqrt(jnp.mean(t * t, axis=-1, keepdims=True) + EPS)
        key = jax.random.key(seed)
        kx, kc, kq, kk, kv = jax.random.split(key, 5)
        x = jax.random.normal(kx, (2, 512, DIM), dtype=jnp.float32)
        context = jax.random.normal(kc, (2, 64, DIM), dtype=jnp.float32)
        std = 0.02
        Wq = jax.random.normal(kq, (DIM, DIM), dtype=jnp.float32) * std
        Wk = jax.random.normal(kk, (DIM, DIM), dtype=jnp.float32) * std
        Wv = jax.random.normal(kv, (DIM, DIM), dtype=jnp.float32) * std
        return {'x': x, 'context': context, 'Wq': Wq, 'Wk': Wk, 'Wv': Wv}
    _L1_xattn_all = _L1_xattn_setup()
    _L1_xattn_in = {k: v for k, v in _L1_xattn_all.items() if k in ('Wq', 'Wk', 'Wv')}
    del _L1_xattn_all

    def _L1_ffn_setup():
        import jax, jax.numpy as jnp
        import numpy as np
        D_MODEL = 256
        D_FF = 1024

        def absmean_quant(w):
            scale = jnp.mean(jnp.abs(w))
            mask = (jnp.abs(w) >= scale * 0.7).astype(w.dtype)
            return jnp.sign(w) * mask
        key = jax.random.key(seed)
        k_x, k_w1, k_w2 = jax.random.split(key, 3)
        x = jax.random.normal(k_x, (4, 512, D_MODEL), dtype=jnp.float32)
        w1 = jax.random.normal(k_w1, (D_FF, D_MODEL), dtype=jnp.float32)
        b1 = jnp.zeros((D_FF,), dtype=jnp.float32)
        w2 = jax.random.normal(k_w2, (D_MODEL, D_FF), dtype=jnp.float32)
        b2 = jnp.zeros((D_MODEL,), dtype=jnp.float32)
        return {'x': x, 'w1': w1, 'b1': b1, 'w2': w2, 'b2': b2}
    _L1_ffn_all = _L1_ffn_setup()
    _L1_ffn_in = {k: v for k, v in _L1_ffn_all.items() if k in ('w1', 'b1', 'w2', 'b2')}
    del _L1_ffn_all

    def _L2_attn_setup():
        import jax, jax.numpy as jnp
        import numpy as np
        B, T, D = (1, 256, 256)
        H, DK, DV, M = (16, 64, 128, 64)
        KEY_DIM, VALUE_DIM = (H * DK, H * DV)
        EPS = 1e-05
        CLAMP_MIN, CLAMP_MAX = (-32.0, 32.0)
        XAVIER_GAIN = 2.0 ** (-2.5)

        def _chunk_abc(q, k, v, s):
            scale = q.shape[-1] ** (-0.5)
            z = jax.lax.cumlogsumexp(s, axis=2)
            g = jnp.exp(jnp.concatenate([z[:, :, :1], z[:, :, :-1]], axis=2) - z)
            p = jnp.exp(s - z)
            tfirst = lambda x: jnp.moveaxis(x, 2, 0)
            qT, kT, vT, pT, gT = map(tfirst, (q * scale, k, v, p, g))
            b, h = (q.shape[0], q.shape[1])
            hk0 = jnp.zeros((b, h, q.shape[-1], s.shape[-1]), q.dtype)

            def step_k(hk, x):
                q_t, k_t, p_t, g_t = x
                hk = hk * g_t[:, :, None, :] + k_t[..., None] * p_t[:, :, None, :]
                return (hk, jnp.einsum('bhk,bhkm->bhm', q_t, hk))
            _, okT = jax.lax.scan(step_k, hk0, (qT, kT, pT, gT))
            pvT = jax.nn.softmax(okT, axis=-1)
            hv0 = jnp.zeros((b, h, s.shape[-1], v.shape[-1]), q.dtype)

            def step_v(hv, x):
                pv_t, v_t, p_t, g_t = x
                hv = hv * g_t[..., None] + p_t[..., None] * v_t[:, :, None, :]
                return (hv, jnp.einsum('bhm,bhmv->bhv', pv_t, hv))
            _, ovT = jax.lax.scan(step_v, hv0, (pvT, vT, pT, gT))
            return jnp.moveaxis(ovT, 0, 2)
        key = jax.random.key(seed)
        ks = jax.random.split(key, 8)

        def w(k, fan_in, fan_out):
            std = XAVIER_GAIN * np.sqrt(2.0 / (fan_in + fan_out))
            return jax.random.normal(k, (fan_in, fan_out), jnp.float32) * std
        return {'hidden_states': jax.random.normal(ks[0], (B, T, D), jnp.float32), 'Wq': w(ks[1], D, KEY_DIM), 'Wk': w(ks[2], D, KEY_DIM), 'Wv': w(ks[3], D, VALUE_DIM), 'Wg': w(ks[4], D, VALUE_DIM), 'Ws': w(ks[5], D, H * M), 'Wo': w(ks[6], VALUE_DIM, D), 'g_norm_weight': jnp.ones((DV,), jnp.float32)}
    _L2_attn_all = _L2_attn_setup()
    _L2_attn_in = {k: v for k, v in _L2_attn_all.items() if k in ('Wq', 'Wk', 'Wv', 'Wg', 'Ws', 'Wo', 'g_norm_weight')}
    del _L2_attn_all

    def _L2_xattn_setup():
        import jax, jax.numpy as jnp
        import numpy as np
        from jax import lax
        LN_EPS = 1e-05
        key = jax.random.key(seed)
        ks = jax.random.split(key, 8)
        B, S, T, D = (4, 128, 256, 256)
        scale = 0.02
        return {'Z': jax.random.normal(ks[0], (B, S, D), dtype=jnp.float32), 'kv': jax.random.normal(ks[1], (B, T, D), dtype=jnp.float32), 'decay': jnp.float32(0.9), 'W_in': jax.random.normal(ks[2], (D, D), dtype=jnp.float32) * scale, 'b_in': jnp.zeros((D,), dtype=jnp.float32), 'W_out': jax.random.normal(ks[3], (D, D), dtype=jnp.float32) * scale, 'b_out': jnp.zeros((D,), dtype=jnp.float32), 'gamma': jnp.ones((D,), dtype=jnp.float32), 'beta': jnp.zeros((D,), dtype=jnp.float32)}
    _L2_xattn_all = _L2_xattn_setup()
    _L2_xattn_in = {k: v for k, v in _L2_xattn_all.items() if k in ('decay', 'W_in', 'b_in', 'W_out', 'b_out', 'gamma', 'beta')}
    del _L2_xattn_all

    def _L2_ffn_setup():
        import jax, jax.numpy as jnp
        import numpy as np
        H = 256
        E = 64
        I = 64
        SI = 64
        TOP_K = 8
        B, T = (2, 64)
        key = jax.random.key(seed)
        ks = jax.random.split(key, 8)
        s = 0.02
        return {'h': jax.random.normal(ks[0], (B, T, H), jnp.float32), 'gate_w': jax.random.normal(ks[1], (E, H), jnp.float32) * s, 'gu_w': jax.random.normal(ks[2], (E, 2 * I, H), jnp.float32) * s, 'dp_w': jax.random.normal(ks[3], (E, H, I), jnp.float32) * s, 'sh_gate_w': jax.random.normal(ks[4], (SI, H), jnp.float32) * s, 'sh_up_w': jax.random.normal(ks[5], (SI, H), jnp.float32) * s, 'sh_down_w': jax.random.normal(ks[6], (H, SI), jnp.float32) * s, 'sh_gate1_w': jax.random.normal(ks[7], (1, H), jnp.float32) * s}
    _L2_ffn_all = _L2_ffn_setup()
    _L2_ffn_in = {k: v for k, v in _L2_ffn_all.items() if k in ('gate_w', 'gu_w', 'dp_w', 'sh_gate_w', 'sh_up_w', 'sh_down_w', 'sh_gate1_w')}
    del _L2_ffn_all

    def _L3_attn_setup():
        import jax, jax.numpy as jnp
        import numpy as np
        B, S, E, H = (4, 256, 256, 16)
        D = E // H
        ROPE_BASE = 10000.0

        def rope(x, base=ROPE_BASE, offset=0):
            d = x.shape[-1]
            s = x.shape[-2]
            inv_freq = base ** (-jnp.arange(0, d, 2, dtype=jnp.float32) / d)
            pos = jnp.arange(offset, s + offset, dtype=jnp.float32)
            ang = pos[:, None] * inv_freq
            sin, cos = (jnp.sin(ang), jnp.cos(ang))
            xe, xo = (x[..., 0::2], x[..., 1::2])
            re = xe * cos - xo * sin
            ro = xe * sin + xo * cos
            return jnp.stack([re, ro], axis=-1).reshape(x.shape)
        key = jax.random.key(seed)
        ks = jax.random.split(key, 9)
        w = lambda k, shp: jax.random.normal(k, shp, dtype=jnp.float32) * 0.02
        return {'x': jax.random.normal(ks[0], (B, S, E), dtype=jnp.float32), 'Wq': w(ks[1], (E, E)), 'bq': w(ks[2], (E,)), 'Wk': w(ks[3], (E, E)), 'bk': w(ks[4], (E,)), 'Wv': w(ks[5], (E, E)), 'bv': w(ks[6], (E,)), 'Wo': w(ks[7], (E, E)), 'bo': w(ks[8], (E,))}
    _L3_attn_all = _L3_attn_setup()
    _L3_attn_in = {k: v for k, v in _L3_attn_all.items() if k in ('Wq', 'bq', 'Wk', 'bk', 'Wv', 'bv', 'Wo', 'bo')}
    del _L3_attn_all

    def _L3_xattn_setup():
        import jax, jax.numpy as jnp
        import numpy as np
        N_HEAD = 8
        key = jax.random.key(seed)
        k1, k2, k3 = jax.random.split(key, 3)
        b, d, m = (4, 128, 256)
        c, n = (128, 256)
        q = jax.random.normal(k1, (b, d, m), dtype=jnp.float32)
        k = jax.random.normal(k2, (d // d * b, d, n), dtype=jnp.float32).reshape(b, d, n)
        v = jax.random.normal(k3, (b, c, n), dtype=jnp.float32)
        return {'q': q, 'k': k, 'v': v}
    _L3_xattn_all = _L3_xattn_setup()
    _L3_xattn_in = {k: v for k, v in _L3_xattn_all.items() if k in ()}
    del _L3_xattn_all

    def _L3_ffn_setup():
        import jax, jax.numpy as jnp
        import numpy as np
        E = 8
        TOP_K = 2
        D = 256
        DE = 176
        DS = 352
        B, S = (2, 256)
        key = jax.random.key(seed)
        ks = jax.random.split(key, 8)
        std = 0.02
        return {'x': jax.random.normal(ks[0], (B, S, D), jnp.float32), 'W_router': jax.random.normal(ks[1], (D, E), jnp.float32) * std, 'We_gate': jax.random.normal(ks[2], (E, D, DE), jnp.float32) * std, 'We_up': jax.random.normal(ks[3], (E, D, DE), jnp.float32) * std, 'We_down': jax.random.normal(ks[4], (E, DE, D), jnp.float32) * std, 'Ws_gate': jax.random.normal(ks[5], (D, DS), jnp.float32) * std, 'Ws_up': jax.random.normal(ks[6], (D, DS), jnp.float32) * std, 'Ws_down': jax.random.normal(ks[7], (DS, D), jnp.float32) * std}
    _L3_ffn_all = _L3_ffn_setup()
    _L3_ffn_in = {k: v for k, v in _L3_ffn_all.items() if k in ('W_router', 'We_gate', 'We_up', 'We_down', 'Ws_gate', 'Ws_up', 'Ws_down')}
    del _L3_ffn_all
    return {'x': x, 'ctx_2048': ctx_2048, 'L0_attn_Wq': _L0_attn_in['Wq'], 'L0_attn_bq': _L0_attn_in['bq'], 'L0_attn_Wk': _L0_attn_in['Wk'], 'L0_attn_bk': _L0_attn_in['bk'], 'L0_attn_Wv': _L0_attn_in['Wv'], 'L0_attn_bv': _L0_attn_in['bv'], 'L0_attn_Wo': _L0_attn_in['Wo'], 'L0_attn_bo': _L0_attn_in['bo'], 'L0_attn_rand_matrix': _L0_attn_in['rand_matrix'], 'L0_xattn_w': _L0_xattn_in['w'], 'L0_xattn_u': _L0_xattn_in['u'], 'L0_ffn_gate_w': _L0_ffn_in['gate_w'], 'L0_ffn_w_gate_up': _L0_ffn_in['w_gate_up'], 'L0_ffn_w_down': _L0_ffn_in['w_down'], 'L0_ffn_shared_gate_up': _L0_ffn_in['shared_gate_up'], 'L0_ffn_shared_down': _L0_ffn_in['shared_down'], 'L1_attn_W_qkvz': _L1_attn_in['W_qkvz'], 'L1_attn_W_ba': _L1_attn_in['W_ba'], 'L1_attn_conv_w': _L1_attn_in['conv_w'], 'L1_attn_dt_bias': _L1_attn_in['dt_bias'], 'L1_attn_A_log': _L1_attn_in['A_log'], 'L1_attn_norm_weight': _L1_attn_in['norm_weight'], 'L1_attn_W_out': _L1_attn_in['W_out'], 'L1_xattn_Wq': _L1_xattn_in['Wq'], 'L1_xattn_Wk': _L1_xattn_in['Wk'], 'L1_xattn_Wv': _L1_xattn_in['Wv'], 'L1_ffn_w1': _L1_ffn_in['w1'], 'L1_ffn_b1': _L1_ffn_in['b1'], 'L1_ffn_w2': _L1_ffn_in['w2'], 'L1_ffn_b2': _L1_ffn_in['b2'], 'L2_attn_Wq': _L2_attn_in['Wq'], 'L2_attn_Wk': _L2_attn_in['Wk'], 'L2_attn_Wv': _L2_attn_in['Wv'], 'L2_attn_Wg': _L2_attn_in['Wg'], 'L2_attn_Ws': _L2_attn_in['Ws'], 'L2_attn_Wo': _L2_attn_in['Wo'], 'L2_attn_g_norm_weight': _L2_attn_in['g_norm_weight'], 'L2_xattn_decay': _L2_xattn_in['decay'], 'L2_xattn_W_in': _L2_xattn_in['W_in'], 'L2_xattn_b_in': _L2_xattn_in['b_in'], 'L2_xattn_W_out': _L2_xattn_in['W_out'], 'L2_xattn_b_out': _L2_xattn_in['b_out'], 'L2_xattn_gamma': _L2_xattn_in['gamma'], 'L2_xattn_beta': _L2_xattn_in['beta'], 'L2_ffn_gate_w': _L2_ffn_in['gate_w'], 'L2_ffn_gu_w': _L2_ffn_in['gu_w'], 'L2_ffn_dp_w': _L2_ffn_in['dp_w'], 'L2_ffn_sh_gate_w': _L2_ffn_in['sh_gate_w'], 'L2_ffn_sh_up_w': _L2_ffn_in['sh_up_w'], 'L2_ffn_sh_down_w': _L2_ffn_in['sh_down_w'], 'L2_ffn_sh_gate1_w': _L2_ffn_in['sh_gate1_w'], 'L3_attn_Wq': _L3_attn_in['Wq'], 'L3_attn_bq': _L3_attn_in['bq'], 'L3_attn_Wk': _L3_attn_in['Wk'], 'L3_attn_bk': _L3_attn_in['bk'], 'L3_attn_Wv': _L3_attn_in['Wv'], 'L3_attn_bv': _L3_attn_in['bv'], 'L3_attn_Wo': _L3_attn_in['Wo'], 'L3_attn_bo': _L3_attn_in['bo'], 'L3_ffn_W_router': _L3_ffn_in['W_router'], 'L3_ffn_We_gate': _L3_ffn_in['We_gate'], 'L3_ffn_We_up': _L3_ffn_in['We_up'], 'L3_ffn_We_down': _L3_ffn_in['We_down'], 'L3_ffn_Ws_gate': _L3_ffn_in['Ws_gate'], 'L3_ffn_Ws_up': _L3_ffn_in['Ws_up'], 'L3_ffn_Ws_down': _L3_ffn_in['Ws_down']}

def reference(x, ctx_2048, L0_attn_Wq, L0_attn_bq, L0_attn_Wk, L0_attn_bk, L0_attn_Wv, L0_attn_bv, L0_attn_Wo, L0_attn_bo, L0_attn_rand_matrix, L0_xattn_w, L0_xattn_u, L0_ffn_gate_w, L0_ffn_w_gate_up, L0_ffn_w_down, L0_ffn_shared_gate_up, L0_ffn_shared_down, L1_attn_W_qkvz, L1_attn_W_ba, L1_attn_conv_w, L1_attn_dt_bias, L1_attn_A_log, L1_attn_norm_weight, L1_attn_W_out, L1_xattn_Wq, L1_xattn_Wk, L1_xattn_Wv, L1_ffn_w1, L1_ffn_b1, L1_ffn_w2, L1_ffn_b2, L2_attn_Wq, L2_attn_Wk, L2_attn_Wv, L2_attn_Wg, L2_attn_Ws, L2_attn_Wo, L2_attn_g_norm_weight, L2_xattn_decay, L2_xattn_W_in, L2_xattn_b_in, L2_xattn_W_out, L2_xattn_b_out, L2_xattn_gamma, L2_xattn_beta, L2_ffn_gate_w, L2_ffn_gu_w, L2_ffn_dp_w, L2_ffn_sh_gate_w, L2_ffn_sh_up_w, L2_ffn_sh_down_w, L2_ffn_sh_gate1_w, L3_attn_Wq, L3_attn_bq, L3_attn_Wk, L3_attn_bk, L3_attn_Wv, L3_attn_bv, L3_attn_Wo, L3_attn_bo, L3_ffn_W_router, L3_ffn_We_gate, L3_ffn_We_up, L3_ffn_We_down, L3_ffn_Ws_gate, L3_ffn_Ws_up, L3_ffn_Ws_down):
    import jax
    import jax.numpy as jnp

    def _L0_attn_ref(hidden_states, Wq, bq, Wk, bk, Wv, bv, Wo, bo, rand_matrix):
        import math
        import jax, jax.numpy as jnp
        import numpy as np
        HID = 256
        H = 16
        HKV = 8
        D = HID // H
        F = D
        SEQ = 256
        BATCH = 2
        THETA = 10000.0

        def _rotate_half(x):
            x1, x2 = (x[..., :x.shape[-1] // 2], x[..., x.shape[-1] // 2:])
            return jnp.concatenate((-x2, x1), axis=-1)

        def _softmax_kernel(x, R):
            n = jnp.sqrt(jnp.sum(x * x, axis=-1, keepdims=True))
            x = x / jnp.maximum(n, 1e-06)
            p = jnp.einsum('...d,ed->...e', x, R)
            feats = jnp.concatenate([jnp.sin(p), jnp.cos(p)], axis=-1)
            return feats / math.sqrt(F)
        b, s, _ = hidden_states.shape
        q = (hidden_states @ Wq.T + bq).reshape(b, s, H, D).transpose(0, 2, 1, 3)
        k = (hidden_states @ Wk.T + bk).reshape(b, s, HKV, D).transpose(0, 2, 1, 3)
        v = (hidden_states @ Wv.T + bv).reshape(b, s, HKV, D).transpose(0, 2, 1, 3)
        inv_freq = 1.0 / THETA ** (jnp.arange(0, D, 2, dtype=jnp.float32) / D)
        freqs = jnp.arange(s, dtype=jnp.float32)[:, None] * inv_freq[None, :]
        emb = jnp.concatenate((freqs, freqs), axis=-1)
        cos = jnp.cos(emb)[None, None, :, :]
        sin = jnp.sin(emb)[None, None, :, :]
        q = q * cos + _rotate_half(q) * sin
        k = k * cos + _rotate_half(k) * sin
        rep = H // HKV
        k = jnp.repeat(k, rep, axis=1)
        v = jnp.repeat(v, rep, axis=1)
        qp = _softmax_kernel(q, rand_matrix)
        kp = _softmax_kernel(k, rand_matrix)
        kv = jnp.einsum('bhsf,bhsd->bsfd', kp, v)
        out = jnp.einsum('bhsf,bsfd->bhsd', qp, kv)
        out = out.reshape(b, s, HID)
        return out @ Wo.T + bo

    def _L0_xattn_ref(B, T, C, w, u, k, v):
        import jax, jax.numpy as jnp
        import numpy as np
        B_DIM, T_DIM, C_DIM = (16, 128, 256)

        def _wkv(w, u, k, v):
            Bn, Tn, Cn = k.shape
            NEG_INF = jnp.float32(-1e+38)

            def step(carry, kv_t):
                p, q, o = carry
                kt, vt = kv_t
                no = jnp.maximum(o, u + kt)
                A = jnp.exp(o - no)
                E = jnp.exp(u + kt - no)
                y = (A * p + E * vt) / (A * q + E)
                no2 = jnp.maximum(w + o, kt)
                A2 = jnp.exp(w + o - no2)
                E2 = jnp.exp(kt - no2)
                return ((A2 * p + E2 * vt, A2 * q + E2, no2), y)
            init = (jnp.zeros((Bn, Cn), k.dtype), jnp.zeros((Bn, Cn), k.dtype), jnp.full((Bn, Cn), NEG_INF, k.dtype))
            kT = jnp.moveaxis(k, 1, 0)
            vT = jnp.moveaxis(v, 1, 0)
            _, yT = jax.lax.scan(step, init, (kT, vT))
            return jnp.moveaxis(yT, 0, 1)
        return _wkv(w, u, k, v)

    def _L0_ffn_ref(hidden_states, gate_w, w_gate_up, w_down, shared_gate_up, shared_down):
        import jax, jax.numpy as jnp
        import numpy as np
        H = 256
        I = 176
        E = 16
        TOP_K = 4
        N_GROUP = 4
        TOPK_GROUP = 2
        SCALE = 16.0
        N_SHARED = 2
        SI = I * N_SHARED
        B, S = (1, 256)

        def _silu_and_mul(gu):
            g, u = jnp.split(gu, 2, axis=-1)
            return jax.nn.silu(g) * u
        b, s, h = hidden_states.shape
        x = hidden_states.reshape(-1, h)
        T = x.shape[0]
        logits = x @ gate_w.T
        grouped = logits.reshape(T, N_GROUP, E // N_GROUP)
        group_scores = grouped.max(axis=-1)
        _, group_idx = jax.lax.top_k(group_scores, TOPK_GROUP)
        rows = jnp.arange(T)[:, None]
        keep = jnp.zeros((T, N_GROUP), bool).at[rows, group_idx].set(True)
        grouped = jnp.where(keep[..., None], grouped, 0.0)
        logits = grouped.reshape(T, E)
        probs = jax.nn.softmax(logits, axis=-1)
        topk_w, topk_ids = jax.lax.top_k(probs, TOP_K)
        topk_w = topk_w * SCALE
        combine = jnp.zeros((T, E), x.dtype).at[rows, topk_ids].add(topk_w)

        def step(acc, ws):
            wgu, wd, c = ws
            y = _silu_and_mul(x @ wgu) @ wd
            return (acc + c[:, None] * y, None)
        out, _ = jax.lax.scan(step, jnp.zeros_like(x), (w_gate_up, w_down, combine.T))
        out = out + _silu_and_mul(x @ shared_gate_up) @ shared_down
        return out.reshape(b, s, h)

    def _L1_attn_ref(hidden_states, W_qkvz, W_ba, conv_w, dt_bias, A_log, norm_weight, W_out):
        import jax, jax.numpy as jnp
        import numpy as np
        B, T, HID = (2, 256, 256)
        NKH, NVH = (16, 32)
        DK, DV = (128, 128)
        R = NVH // NKH
        KDIM, VDIM = (NKH * DK, NVH * DV)
        CONV_K = 4
        EPS = 1e-06

        def _silu(x):
            return x * jax.nn.sigmoid(x)

        def _l2norm(x, eps=1e-06):
            return x * jax.lax.rsqrt(jnp.sum(x * x, axis=-1, keepdims=True) + eps)
        Bv, Tv = hidden_states.shape[:2]
        qkvz = hidden_states @ W_qkvz
        ba = hidden_states @ W_ba
        qkvz = qkvz.reshape(Bv, Tv, NKH, 2 * DK + 2 * R * DV)
        q, k, v, z = jnp.split(qkvz, [DK, 2 * DK, 2 * DK + R * DV], axis=3)
        v = v.reshape(Bv, Tv, NVH, DV)
        z = z.reshape(Bv, Tv, NVH, DV)
        ba = ba.reshape(Bv, Tv, NKH, 2 * R)
        b, a = jnp.split(ba, 2, axis=3)
        b = b.reshape(Bv, Tv, NVH)
        a = a.reshape(Bv, Tv, NVH)
        mixed = jnp.concatenate([q.reshape(Bv, Tv, KDIM), k.reshape(Bv, Tv, KDIM), v.reshape(Bv, Tv, VDIM)], axis=-1)
        xp = jnp.pad(mixed, ((0, 0), (CONV_K - 1, 0), (0, 0)))
        conv = sum((xp[:, j:j + Tv, :] * conv_w[:, j] for j in range(CONV_K)))
        conv = _silu(conv)
        q, k, v = jnp.split(conv, [KDIM, 2 * KDIM], axis=-1)
        q = q.reshape(Bv, Tv, NKH, DK)
        k = k.reshape(Bv, Tv, NKH, DK)
        v = v.reshape(Bv, Tv, NVH, DV)
        beta = jax.nn.sigmoid(b)
        g = -jnp.exp(A_log) * jax.nn.softplus(a + dt_bias)
        alpha = jnp.exp(g)
        q = jnp.repeat(q, R, axis=2)
        k = jnp.repeat(k, R, axis=2)
        q = _l2norm(q) * DK ** (-0.5)
        k = _l2norm(k)

        def step(S, inp):
            q_t, k_t, v_t, a_t, b_t = inp
            S = S * a_t[..., None, None]
            err = jnp.einsum('bhkv,bhk->bhv', S, k_t)
            v_new = (v_t - err) * b_t[..., None]
            S = S + k_t[..., None] * v_new[..., None, :]
            o = jnp.einsum('bhkv,bhk->bhv', S, q_t)
            return (S, o)
        tm = lambda x: jnp.swapaxes(x, 0, 1)
        S0 = jnp.zeros((Bv, NVH, DK, DV), hidden_states.dtype)
        _, o = jax.lax.scan(step, S0, (tm(q), tm(k), tm(v), tm(alpha), tm(beta)))
        o = jnp.swapaxes(o, 0, 1)
        og = o * _silu(z)
        og = og * jax.lax.rsqrt(jnp.mean(og * og, axis=-1, keepdims=True) + EPS) * norm_weight
        return og.reshape(Bv, Tv, VDIM) @ W_out

    def _L1_xattn_ref(x, context, Wq, Wk, Wv):
        import jax, jax.numpy as jnp
        import numpy as np
        DIM = 256
        NHEADS = 32
        HEAD_DIM = DIM // NHEADS
        EPS = 1e-06

        def _rmsnorm(t):
            return t * jax.lax.rsqrt(jnp.mean(t * t, axis=-1, keepdims=True) + EPS)
        b, n, _ = x.shape
        m = context.shape[1]
        q = x @ Wq.T
        k_raw = context @ Wk.T
        v_raw = context @ Wv.T
        q = q.reshape(b, n, NHEADS, HEAD_DIM).transpose(0, 2, 1, 3)
        kv = jnp.concatenate([k_raw, v_raw], axis=-1)
        kv = kv.reshape(b, m, NHEADS, HEAD_DIM, 2)
        k = kv[..., 0].transpose(0, 2, 1, 3)
        v = kv[..., 1].transpose(0, 2, 1, 3)
        q = _rmsnorm(q)
        k = _rmsnorm(k)
        scale = HEAD_DIM ** (-0.5)
        scores = jnp.einsum('bhnd,bhmd->bhnm', q, k) * scale
        attn = jax.nn.softmax(scores, axis=-1)
        out = jnp.einsum('bhnm,bhmd->bhnd', attn, v)
        return out.transpose(0, 2, 1, 3).reshape(b, n, NHEADS * HEAD_DIM)

    def _L1_ffn_ref(x, w1, b1, w2, b2):
        import jax, jax.numpy as jnp
        import numpy as np
        D_MODEL = 256
        D_FF = 1024

        def absmean_quant(w):
            scale = jnp.mean(jnp.abs(w))
            mask = (jnp.abs(w) >= scale * 0.7).astype(w.dtype)
            return jnp.sign(w) * mask
        w1_q = absmean_quant(w1)
        w2_q = absmean_quant(w2)
        h = jnp.einsum('bsd,fd->bsf', x, w1_q) + b1
        h = jax.nn.gelu(h, approximate=False)
        out = jnp.einsum('bsf,df->bsd', h, w2_q) + b2
        return out

    def _L2_attn_ref(hidden_states, Wq, Wk, Wv, Wg, Ws, Wo, g_norm_weight):
        import jax, jax.numpy as jnp
        import numpy as np
        B, T, D = (1, 256, 256)
        H, DK, DV, M = (16, 64, 128, 64)
        KEY_DIM, VALUE_DIM = (H * DK, H * DV)
        EPS = 1e-05
        CLAMP_MIN, CLAMP_MAX = (-32.0, 32.0)
        XAVIER_GAIN = 2.0 ** (-2.5)

        def _chunk_abc(q, k, v, s):
            scale = q.shape[-1] ** (-0.5)
            z = jax.lax.cumlogsumexp(s, axis=2)
            g = jnp.exp(jnp.concatenate([z[:, :, :1], z[:, :, :-1]], axis=2) - z)
            p = jnp.exp(s - z)
            tfirst = lambda x: jnp.moveaxis(x, 2, 0)
            qT, kT, vT, pT, gT = map(tfirst, (q * scale, k, v, p, g))
            b, h = (q.shape[0], q.shape[1])
            hk0 = jnp.zeros((b, h, q.shape[-1], s.shape[-1]), q.dtype)

            def step_k(hk, x):
                q_t, k_t, p_t, g_t = x
                hk = hk * g_t[:, :, None, :] + k_t[..., None] * p_t[:, :, None, :]
                return (hk, jnp.einsum('bhk,bhkm->bhm', q_t, hk))
            _, okT = jax.lax.scan(step_k, hk0, (qT, kT, pT, gT))
            pvT = jax.nn.softmax(okT, axis=-1)
            hv0 = jnp.zeros((b, h, s.shape[-1], v.shape[-1]), q.dtype)

            def step_v(hv, x):
                pv_t, v_t, p_t, g_t = x
                hv = hv * g_t[..., None] + p_t[..., None] * v_t[:, :, None, :]
                return (hv, jnp.einsum('bhm,bhmv->bhv', pv_t, hv))
            _, ovT = jax.lax.scan(step_v, hv0, (pvT, vT, pT, gT))
            return jnp.moveaxis(ovT, 0, 2)
        b, t, _ = hidden_states.shape
        to_heads = lambda x, d: jnp.transpose(x.reshape(b, t, H, d), (0, 2, 1, 3))
        q = to_heads(hidden_states @ Wq, DK)
        k = to_heads(hidden_states @ Wk, DK)
        v = to_heads(hidden_states @ Wv, DV)
        s = jnp.clip(to_heads(hidden_states @ Ws, M), CLAMP_MIN, CLAMP_MAX)
        o = jnp.transpose(_chunk_abc(q, k, v, s), (0, 2, 1, 3))
        g = (hidden_states @ Wg).reshape(b, t, H, DV)
        o = o * jax.lax.rsqrt(jnp.mean(jnp.square(o), axis=-1, keepdims=True) + EPS) * g_norm_weight
        o = o * (g * jax.nn.sigmoid(g))
        return o.reshape(b, t, VALUE_DIM) @ Wo

    def _L2_xattn_ref(Z, kv, decay, W_in, b_in, W_out, b_out, gamma, beta):
        import jax, jax.numpy as jnp
        import numpy as np
        from jax import lax
        LN_EPS = 1e-05
        B, T, D = kv.shape
        K = jax.nn.sigmoid(decay)
        x = jnp.einsum('btd,ed->bte', kv, W_in) + b_in

        def scan_fn(s, xt):
            s = K * s + xt
            return (s, s)
        s0 = jnp.zeros((B, D), dtype=kv.dtype)
        _, states = lax.scan(scan_fn, s0, jnp.swapaxes(x, 0, 1))
        states = jnp.swapaxes(states, 0, 1)
        proj = jnp.einsum('btd,ed->bte', states, W_out) + b_out
        summary = jnp.mean(proj, axis=1, keepdims=True)
        y = Z + summary
        mu = jnp.mean(y, axis=-1, keepdims=True)
        var = jnp.mean((y - mu) ** 2, axis=-1, keepdims=True)
        return (y - mu) / jnp.sqrt(var + LN_EPS) * gamma + beta

    def _L2_ffn_ref(h, gate_w, gu_w, dp_w, sh_gate_w, sh_up_w, sh_down_w, sh_gate1_w):
        import jax, jax.numpy as jnp
        import numpy as np
        H = 256
        E = 64
        I = 64
        SI = 64
        TOP_K = 8
        B, T = (2, 64)
        Bb, Tt, Hh = h.shape
        x = h.reshape(Bb * Tt, Hh)
        N = x.shape[0]
        logits = x @ gate_w.T
        topv, topi = jax.lax.top_k(logits, TOP_K)
        rw = jax.nn.softmax(topv.astype(jnp.float32), axis=-1).astype(x.dtype)
        W = jnp.zeros((N, E), x.dtype).at[jnp.arange(N)[:, None], topi].set(rw)
        gu = jnp.einsum('nh,eih->nei', x, gu_w)
        gate, up = (gu[..., :I], gu[..., I:])
        inter = jax.nn.silu(gate) * up
        inter_w = inter * W[:, :, None]
        out = jnp.einsum('nei,ehi->nh', inter_w, dp_w)
        sh_inter = jax.nn.silu(x @ sh_gate_w.T) * (x @ sh_up_w.T)
        sh_out = sh_inter @ sh_down_w.T
        sh_g = jax.nn.sigmoid(x @ sh_gate1_w.T)
        out = out + sh_g * sh_out
        return out.reshape(Bb, Tt, Hh)

    def _L3_attn_ref(x, Wq, bq, Wk, bk, Wv, bv, Wo, bo):
        import jax, jax.numpy as jnp
        import numpy as np
        B, S, E, H = (4, 256, 256, 16)
        D = E // H
        ROPE_BASE = 10000.0

        def rope(x, base=ROPE_BASE, offset=0):
            d = x.shape[-1]
            s = x.shape[-2]
            inv_freq = base ** (-jnp.arange(0, d, 2, dtype=jnp.float32) / d)
            pos = jnp.arange(offset, s + offset, dtype=jnp.float32)
            ang = pos[:, None] * inv_freq
            sin, cos = (jnp.sin(ang), jnp.cos(ang))
            xe, xo = (x[..., 0::2], x[..., 1::2])
            re = xe * cos - xo * sin
            ro = xe * sin + xo * cos
            return jnp.stack([re, ro], axis=-1).reshape(x.shape)
        b, s, _ = x.shape
        scale = D ** (-0.5)

        def proj(W, bias):
            y = jnp.einsum('bse,fe->bsf', x, W) + bias
            return y.reshape(b, s, H, D).transpose(0, 2, 1, 3)
        q = rope(proj(Wq, bq))
        k = rope(proj(Wk, bk))
        v = proj(Wv, bv)
        attn = jnp.einsum('bhqd,bhkd->bhqk', q, k) * scale
        causal = jnp.triu(jnp.ones((s, s), dtype=bool), k=1)
        attn = jnp.where(causal, -jnp.inf, attn)
        attn_weights = jax.nn.softmax(attn, axis=-1)
        out = jnp.einsum('bhqk,bhkd->bhqd', attn_weights, v)
        out = out.transpose(0, 2, 1, 3).reshape(b, s, E)
        return jnp.einsum('bse,fe->bsf', out, Wo) + bo

    def _L3_xattn_ref(q, k, v):
        import jax, jax.numpy as jnp
        import numpy as np
        N_HEAD = 8
        b, d, m = q.shape
        c = v.shape[1]
        h = N_HEAD
        qh = q.reshape(b * h, d // h, m)
        kh = k.reshape(b * h, d // h, -1)
        vh = v.reshape(b * h, c // h, -1)
        scale = 1.0 / jnp.sqrt(jnp.asarray(d // h, dtype=q.dtype))
        qk = jnp.einsum('bdm,bdn->bmn', qh, kh) * scale
        sm = jax.nn.softmax(qk, axis=-1)
        ret = jnp.einsum('bmn,bcn->bcm', sm, vh)
        return ret.reshape(b, c, m)

    def _L3_ffn_ref(x, W_router, We_gate, We_up, We_down, Ws_gate, Ws_up, Ws_down):
        import jax, jax.numpy as jnp
        import numpy as np
        E = 8
        TOP_K = 2
        D = 256
        DE = 176
        DS = 352
        B, S = (2, 256)
        b, s, d = x.shape
        shared = jax.nn.silu(x @ Ws_gate) * (x @ Ws_up) @ Ws_down
        scores = jax.nn.softmax(x @ W_router, axis=-1)
        topk_vals, topk_idx = jax.lax.top_k(scores, TOP_K)
        onehot = jax.nn.one_hot(topk_idx, E, dtype=x.dtype)
        combine = jnp.einsum('bsk,bske->bse', topk_vals, onehot)
        combine = combine.reshape(b * s, E)
        xf = x.reshape(b * s, d)
        h = jax.nn.silu(jnp.einsum('td,edh->eth', xf, We_gate)) * jnp.einsum('td,edh->eth', xf, We_up)
        y_all = jnp.einsum('eth,ehd->etd', h, We_down)
        routed = jnp.einsum('etd,te->td', y_all, combine)
        return routed.reshape(b, s, d) + shared
    x = _layernorm(x + _L0_attn_ref(x, L0_attn_Wq, L0_attn_bq, L0_attn_Wk, L0_attn_bk, L0_attn_Wv, L0_attn_bv, L0_attn_Wo, L0_attn_bo, L0_attn_rand_matrix), axis=-1)
    x = _layernorm(x + _L0_xattn_ref(32, 64, 256, L0_xattn_w, L0_xattn_u, x, ctx_2048), axis=-1)
    x = _layernorm(x + _L0_ffn_ref(x, L0_ffn_gate_w, L0_ffn_w_gate_up, L0_ffn_w_down, L0_ffn_shared_gate_up, L0_ffn_shared_down), axis=-1)
    x = _layernorm(x + _L1_attn_ref(x, L1_attn_W_qkvz, L1_attn_W_ba, L1_attn_conv_w, L1_attn_dt_bias, L1_attn_A_log, L1_attn_norm_weight, L1_attn_W_out), axis=-1)
    x = _layernorm(x + _L1_xattn_ref(x, ctx_2048, L1_xattn_Wq, L1_xattn_Wk, L1_xattn_Wv), axis=-1)
    x = _layernorm(x + _L1_ffn_ref(x, L1_ffn_w1, L1_ffn_b1, L1_ffn_w2, L1_ffn_b2), axis=-1)
    x = _layernorm(x + _L2_attn_ref(x, L2_attn_Wq, L2_attn_Wk, L2_attn_Wv, L2_attn_Wg, L2_attn_Ws, L2_attn_Wo, L2_attn_g_norm_weight), axis=-1)
    x = _layernorm(x + _L2_xattn_ref(x, ctx_2048, L2_xattn_decay, L2_xattn_W_in, L2_xattn_b_in, L2_xattn_W_out, L2_xattn_b_out, L2_xattn_gamma, L2_xattn_beta), axis=-1)
    x = _layernorm(x + _L2_ffn_ref(x, L2_ffn_gate_w, L2_ffn_gu_w, L2_ffn_dp_w, L2_ffn_sh_gate_w, L2_ffn_sh_up_w, L2_ffn_sh_down_w, L2_ffn_sh_gate1_w), axis=-1)
    x = _layernorm(x + _L3_attn_ref(x, L3_attn_Wq, L3_attn_bq, L3_attn_Wk, L3_attn_bk, L3_attn_Wv, L3_attn_bv, L3_attn_Wo, L3_attn_bo), axis=-1)
    x = _layernorm(x + _L3_xattn_ref(x, ctx_2048, ctx_2048), axis=-1)
    x = _layernorm(x + _L3_ffn_ref(x, L3_ffn_W_router, L3_ffn_We_gate, L3_ffn_We_up, L3_ffn_We_down, L3_ffn_Ws_gate, L3_ffn_Ws_up, L3_ffn_Ws_down), axis=-1)
    return x

_drawn_inputs = setup_inputs


def setup_inputs(seed=0):
    import zlib

    import numpy as np

    out = dict(_drawn_inputs(seed))
    spreads = {'L1_attn_dt_bias': (1.0, 0.6),
     'L1_attn_norm_weight': (1.0, 0.6),
     'L1_ffn_b1': (0.0, 0.8),
     'L1_ffn_b2': (0.0, 0.8),
     'L2_attn_g_norm_weight': (1.0, 0.6),
     'L2_xattn_b_in': (0.0, 0.1),
     'L2_xattn_b_out': (0.0, 0.1),
     'L2_xattn_gamma': (1.0, 0.2),
     'L2_xattn_beta': (0.0, 0.1)}
    factors = {'L1_attn_W_ba': 8.0,
     'L1_attn_A_log': 5.631,
     'L2_attn_Wq': 8.0,
     'L2_attn_Wk': 8.0,
     'L2_attn_Wv': 5.491,
     'L2_attn_Wg': 5.639,
     'L2_attn_Ws': 8.0,
     'L2_attn_Wo': 5.916,
     'L2_ffn_gate_w': 8.0,
     'L2_ffn_gu_w': 8.0,
     'L2_ffn_dp_w': 8.0,
     'L2_ffn_sh_gate_w': 8.0,
     'L2_ffn_sh_up_w': 8.0,
     'L2_ffn_sh_down_w': 8.0,
     'L2_ffn_sh_gate1_w': 8.0,
     'L3_attn_Wq': 8.0,
     'L3_attn_bq': 8.0,
     'L3_attn_Wk': 8.0,
     'L3_attn_bk': 8.0,
     'L3_attn_bv': 7.346,
     'L3_ffn_W_router': 8.0,
     'L3_ffn_We_gate': 8.0,
     'L3_ffn_We_up': 8.0,
     'L3_ffn_We_down': 8.0,
     'L3_ffn_Ws_gate': 2.924,
     'L3_ffn_Ws_up': 2.737,
     'L3_ffn_Ws_down': 2.866}
    for name, (base, spread) in spreads.items():
        noise = np.random.default_rng([zlib.crc32(name.encode()), seed]).standard_normal(out[name].shape)
        drawn = base * np.exp(spread * noise) if base else spread * noise
        out[name] = jnp.asarray(drawn.astype(out[name].dtype))
    for name, factor in factors.items():
        out[name] = (out[name] * factor).astype(out[name].dtype)
    return out
```

```python
from contextlib import ExitStack

import numpy as np
import concourse.bass as bass
from concourse import mybir

P = 128
SEQ = 64
BATCH = 32
D = 256
NTOK = BATCH * SEQ
TILES = NTOK // P
KC = D // P
BLK = 512
NBLK = NTOK // BLK
TPB = BLK // P
LN_EPS = 1e-5

F32 = mybir.dt.float32
ALU = mybir.AluOpType
ACT = mybir.ActivationFunctionType
AX = mybir.AxisListType


EXPERTS = {"f0": 16, "f2": 64, "f3": 8}


class Stage:

    def __init__(self, nc, name):
        self.nc, self.name, self.ctx, self.sems = nc, name, ExitStack(), []

    def __enter__(self):
        self.ctx.__enter__()
        return self

    def __exit__(self, *a):
        if self.sems and a[0] is None:
            with self.nc.Block() as block:
                @block.sync
                def _(sp):
                    for s in self.sems:
                        sp.sem_clear(s)
        return self.ctx.__exit__(*a)

    def sb(self, name, shape):
        return self.ctx.enter_context(self.nc.sbuf_tensor(f"{self.name}_{name}", list(shape), F32))

    def ps(self, name, shape):
        return self.ctx.enter_context(self.nc.psum_tensor(f"{self.name}_{name}", list(shape), F32))

    def sem(self, name):
        self.sems.append(self.ctx.enter_context(self.nc.semaphore(f"{self.name}_{name}")))
        return self.sems[-1]


class Count:

    def __init__(self, eng, sem, per=0, turn=0):
        self.eng, self.sem, self.per, self.turn, self.n = eng, sem, per, turn, 0

    def __call__(self, ins):
        self.n += 1
        ins.then_inc(self.sem, 1)
        self.eng.wait_ge(self.sem, self.turn * self.per + self.n if self.per else self.n)

    def end(self):
        assert not self.per or self.n == self.per, f"{self.sem}: {self.n} steps in a pass, not {self.per}"


def prime(eng, *sems):
    for s in sems:
        eng.sem_inc(s, 1)


def hold(pe, G, sem, value, out):
    pe.wait_ge(sem, value)
    pe.matmul(out, G.zero[:, 0:P], G.zero[:, 0:1], start=True, stop=True)


def rows(ap, n):
    p, m = ap.shape
    return ap.rearrange("p (o m) -> p o m", o=1).to_broadcast([p, n, m])


def cols(ap, m):
    p, n = ap.shape
    return ap.rearrange("p (n o) -> p n o", o=1).to_broadcast([p, n, m])


def dyn(i, n):
    return bass.ds(i * n, n)


def load(nc, pairs, sem):
    with nc.Block() as block:
        @block.sync
        def _(sp):
            for dst, src in pairs:
                sp.dma_start(dst, src).then_inc(sem, 16)
            sp.wait_ge(sem, 16 * len(pairs))


class Norm:

    def __init__(self, st):
        self.s, self.stats = st.sb("s", [P, TPB, D]), st.sb("stats", [P, TPB, 6])
        self.mean, self.gap, self.var = st.sb("mean", [P, TPB]), st.sb("gap", [P, TPB]), st.sb("var", [P, TPB])
        self.std, self.rstd = st.sb("std", [P, TPB]), st.sb("rstd", [P, TPB])
        self.var_ready, self.std_ready = st.sem("var_ready"), st.sem("std_ready")


def normalise(dve, step, N, g, signal):
    for t in range(TPB):
        step(dve.bn_stats(N.stats[:, t, :], N.s[:, t, :]))
    step(dve.tensor_tensor(N.mean[:, :], N.stats[:, :, 1], N.stats[:, :, 4], ALU.add))
    step(dve.tensor_scalar(N.mean[:, :], N.mean[:, :], 0.5, None, ALU.mult))
    step(dve.tensor_tensor(N.gap[:, :], N.stats[:, :, 1], N.stats[:, :, 4], ALU.subtract))
    step(dve.tensor_tensor(N.gap[:, :], N.gap[:, :], N.gap[:, :], ALU.mult))
    step(dve.tensor_tensor(N.var[:, :], N.stats[:, :, 2], N.stats[:, :, 5], ALU.add))
    step(dve.tensor_scalar(N.var[:, :], N.var[:, :], 1.0 / D, LN_EPS, ALU.mult, ALU.add))
    dve.scalar_tensor_tensor(N.var[:, :], N.gap[:, :], 0.25, N.var[:, :], ALU.mult, ALU.add).then_inc(N.var_ready, 1)
    dve.wait_ge(N.std_ready, g + 1)
    step(dve.reciprocal(N.rstd[:, :], N.std[:, :]))
    for t in range(TPB):
        ins = dve.tensor_scalar(N.s[:, t, :], N.s[:, t, :], N.mean[:, t:t + 1], N.rstd[:, t:t + 1],
                                ALU.subtract, ALU.mult)
        if t < TPB - 1:
            step(ins)
        else:
            ins.then_inc(signal, 1)


def norm_root(act, N, g):
    act.wait_ge(N.var_ready, g + 1)
    act.activation(N.std[:, :], N.var[:, :], ACT.Sqrt).then_inc(N.std_ready, 1)


def residual_norm(nc, G, tag):
    with Stage(nc, f"ln{tag}") as st:
        N = Norm(st)
        s = N.s
        pT = st.ps("pT", [P, KC, BLK])
        dve_step = st.sem("step")
        x_ready, stored, turned, xT_stored = st.sem("x_ready"), st.sem("stored"), st.sem("turned"), st.sem("xT")
        with nc.Block() as block:
            @block.vector
            def _(dve):
                with dve.Fori(0, NBLK) as g:
                    step = Count(dve, dve_step, 15, g)
                    dve.wait_ge(stored, g + 1)
                    dve.wait_ge(turned, g + 1)
                    step(dve.tensor_tensor(s[:, :, :], G.x_tok[:, dyn(g, TPB), :], G.y[:, dyn(g, TPB), :], ALU.add))
                    normalise(dve, step, N, g, x_ready)
                    step.end()

            @block.gpsimd
            def _(pool):
                prime(pool, stored)
                with pool.Fori(0, NBLK) as g:
                    pool.wait_ge(x_ready, g + 1)
                    pool.tensor_copy(G.x_tok[:, dyn(g, TPB), :], s[:, :, :]).then_inc(stored, 1)

            @block.tensor
            def _(pe):
                prime(pe, turned)
                with pe.Fori(0, NBLK) as g:
                    pe.wait_ge(x_ready, g + 1)
                    pe.wait_ge(xT_stored, g * 2 + 1)
                    for c in range(KC):
                        for t in range(TPB):
                            last = pe.transpose(pT[:, c, t * P:(t + 1) * P], s[:, t, c * P:(c + 1) * P], G.ident[:, :])
                    last.then_inc(turned, 1)

            @block.scalar
            def _(act):
                prime(act, xT_stored)
                with act.Fori(0, NBLK) as g:
                    norm_root(act, N, g)
                    act.wait_ge(turned, g + 2)
                    for c in range(KC):
                        act.copy(G.xT[:, c, dyn(g, BLK)], pT[:, c, :]).then_inc(xT_stored, 1)


def tile_logits(nc, G, st, gate, width, logits):
    xt = st.sb("xt", [P, KC, P])
    pl = st.ps("pl", [P, width])
    copied, made, taken = st.sem("copied"), st.sem("made"), st.sem("taken")
    with nc.Block() as block:
        @block.scalar
        def _(act):
            with act.Fori(0, TILES) as t:
                act.wait_ge(made, t + 1)
                act.copy(xt[:, :, :], G.xT[:, :, dyn(t, P)]).then_inc(copied, 1)

        @block.tensor
        def _(pe):
            prime(pe, made)
            with pe.Fori(0, TILES) as t:
                pe.wait_ge(copied, t + 1)
                pe.wait_ge(taken, t + 1)
                for k in range(KC):
                    last = pe.matmul(pl[:, :], xt[:, k, :], gate[:, k, :], start=(k == 0), stop=(k == KC - 1))
                last.then_inc(made, 1)

        @block.vector
        def _(dve):
            prime(dve, taken)
            with dve.Fori(0, TILES) as t:
                dve.wait_ge(made, t + 2)
                dve.tensor_copy(logits[:, dyn(t, 1), :], pl[:, :].rearrange("p (o e) -> p o e", o=1)).then_inc(taken, 1)


def top_by_rank(dve, step, chosen, value, n, top, before, cmp, tie, rank):
    full = [P, TILES, n, n]
    mine = value.rearrange("p t (e o) -> p t e o", o=1).to_broadcast(full)
    other = value.rearrange("p t (o f) -> p t o f", o=1).to_broadcast(full)
    c4 = cmp[:, 0:TILES * n * n].rearrange("p (t e f) -> p t e f", t=TILES, e=n)
    t4 = tie[:, 0:TILES * n * n].rearrange("p (t e f) -> p t e f", t=TILES, e=n)
    b4 = before.rearrange("p (t e) f -> p t e f", t=1).to_broadcast(full)
    step(dve.tensor_tensor(c4, other, mine, ALU.is_gt))
    step(dve.tensor_tensor(t4, other, mine, ALU.is_equal))
    step(dve.tensor_tensor(t4, t4, b4, ALU.mult))
    step(dve.tensor_tensor(c4, c4, t4, ALU.add))
    r = rank[:, 0:TILES * n]
    step(dve.tensor_reduce(r, cmp[:, 0:TILES * n * n].rearrange("p (te f) -> p te f", f=n), AX.X, ALU.add))
    step(dve.tensor_scalar(chosen, r.rearrange("p (t e) -> p t e", t=TILES), float(top), None, ALU.is_lt))


def route_l0(nc, G, st, logits, combine, before16, before4):
    E, NG, GS, TOP, KEEP, SCALE = 16, 4, 4, 4, 2, 16.0
    cmp, tie, rank = st.sb("cmp", [P, TILES * E * E]), st.sb("tie", [P, TILES * E * E]), st.sb("rank", [P, TILES * E])
    best, keep = st.sb("best", [P, TILES, NG]), st.sb("keep", [P, TILES, NG])
    prob, mx, total = st.sb("prob", [P, TILES, E]), st.sb("mx", [P, TILES]), st.sb("total", [P, TILES])
    chosen = st.sb("chosen", [P, TILES, E])
    dve_step, shifted, exped = st.sem("rstep"), st.sem("shifted"), st.sem("exped")
    with nc.Block() as block:
        @block.vector
        def _(dve):
            step = Count(dve, dve_step)
            grouped = logits[:, :, :].rearrange("p t (g s) -> p (t g) s", g=NG)
            step(dve.tensor_reduce(best[:, :, :], grouped, AX.X, ALU.max))
            top_by_rank(dve, step, keep[:, :, :], best[:, :, :], NG, KEEP, before4[:, :, :], cmp, tie, rank)
            keep_all = cols(keep[:, :, :].rearrange("p t g -> p (t g)"), GS)
            step(dve.tensor_tensor(grouped, grouped, keep_all, ALU.mult))
            step(dve.tensor_reduce(mx[:, :], logits[:, :, :], AX.X, ALU.max))
            dve.tensor_tensor(prob[:, :, :], logits[:, :, :], cols(mx[:, :], E), ALU.subtract).then_inc(shifted, 1)
            dve.wait_ge(exped, 1)
            step(dve.tensor_reduce(total[:, :], prob[:, :, :], AX.X, ALU.add))
            step(dve.reciprocal(total[:, :], total[:, :]))
            step(dve.tensor_tensor(prob[:, :, :], prob[:, :, :], cols(total[:, :], E), ALU.mult))
            top_by_rank(dve, step, chosen[:, :, :], prob[:, :, :], E, TOP, before16[:, :, :], cmp, tie, rank)
            step(dve.tensor_tensor(prob[:, :, :], prob[:, :, :], chosen[:, :, :], ALU.mult))
            step(dve.tensor_scalar(combine[:, :, 0:E], prob[:, :, :], SCALE, None, ALU.mult))
            step(dve.memset(combine[:, :, E:E + 1], 1.0))

        @block.scalar
        def _(act):
            act.wait_ge(shifted, 1)
            act.activation(prob[:, :, :], prob[:, :, :], ACT.Exp).then_inc(exped, 1)


def route_l3(nc, G, st, logits, combine, before8):
    E, TOP = 8, 2
    cmp, tie, rank = st.sb("cmp", [P, TILES * E * E]), st.sb("tie", [P, TILES * E * E]), st.sb("rank", [P, TILES * E])
    prob, mx, total = st.sb("prob", [P, TILES, E]), st.sb("mx", [P, TILES]), st.sb("total", [P, TILES])
    chosen = st.sb("chosen", [P, TILES, E])
    dve_step, shifted, exped = st.sem("rstep"), st.sem("shifted"), st.sem("exped")
    with nc.Block() as block:
        @block.vector
        def _(dve):
            step = Count(dve, dve_step)
            step(dve.tensor_reduce(mx[:, :], logits[:, :, :], AX.X, ALU.max))
            dve.tensor_tensor(prob[:, :, :], logits[:, :, :], cols(mx[:, :], E), ALU.subtract).then_inc(shifted, 1)
            dve.wait_ge(exped, 1)
            step(dve.tensor_reduce(total[:, :], prob[:, :, :], AX.X, ALU.add))
            step(dve.reciprocal(total[:, :], total[:, :]))
            step(dve.tensor_tensor(prob[:, :, :], prob[:, :, :], cols(total[:, :], E), ALU.mult))
            top_by_rank(dve, step, chosen[:, :, :], prob[:, :, :], E, TOP, before8[:, :, :], cmp, tie, rank)
            step(dve.tensor_tensor(combine[:, :, 0:E], prob[:, :, :], chosen[:, :, :], ALU.mult))
            step(dve.memset(combine[:, :, E:E + 1], 1.0))

        @block.scalar
        def _(act):
            act.wait_ge(shifted, 1)
            act.activation(prob[:, :, :], prob[:, :, :], ACT.Exp).then_inc(exped, 1)


def route_l2(nc, G, st, logits, combine):
    E, TOP = 64, 8
    GONE = -3.0e38
    best, left, mask = st.sb("best", [P, TILES, TOP]), st.sb("left", [P, TILES, E]), st.sb("mask", [P, TILES, E])
    prob, total = st.sb("prob", [P, TILES, E]), st.sb("total", [P, TILES])
    dve_step, shifted, exped = st.sem("rstep"), st.sem("shifted"), st.sem("exped")
    with nc.Block() as block:
        @block.vector
        def _(dve):
            step = Count(dve, dve_step)
            for t in range(TILES):
                step(dve.max(best[:, t, :], logits[:, t, 0:E]))
            for t in range(TILES):
                step(dve.match_replace(left[:, t, :], best[:, t, :], logits[:, t, 0:E], GONE))
            step(dve.tensor_tensor(mask[:, :, :], left[:, :, :], logits[:, :, 0:E], ALU.not_equal))
            dve.tensor_tensor(prob[:, :, :], logits[:, :, 0:E], best[:, :, 0:1].to_broadcast([P, TILES, E]),
                              ALU.subtract).then_inc(shifted, 1)
            dve.wait_ge(exped, 2)
            step(dve.tensor_tensor(prob[:, :, :], prob[:, :, :], mask[:, :, :], ALU.mult))
            step(dve.tensor_reduce(total[:, :], prob[:, :, :], AX.X, ALU.add))
            step(dve.reciprocal(total[:, :], total[:, :]))
            step(dve.tensor_tensor(combine[:, :, 0:E], prob[:, :, :], cols(total[:, :], E), ALU.mult))

        @block.scalar
        def _(act):
            act.wait_ge(shifted, 1)
            act.activation(prob[:, :, :], prob[:, :, :], ACT.Exp).then_inc(exped, 1)
            act.activation(combine[:, :, E:E + 1], logits[:, :, E:E + 1], ACT.Sigmoid).then_inc(exped, 1)


def gated_experts(nc, G, tag, d):
    W, WO = d[f"{tag}_in_w"], d[f"{tag}_out_w"]
    FT = W.shape[0]
    E1 = EXPERTS[tag] + 1
    EW = d[f"{tag}_gate"].shape[2]
    with Stage(nc, tag) as st:
        combT = st.sb("combT", [E1, NTOK])
        sem = st.sem("loaded")
        with Stage(nc, tag + "r") as rt:
            combine = rt.sb("combine", [P, TILES, E1])
            logits = rt.sb("logits", [P, TILES, EW])
            gate = rt.sb("gate", [P, KC, EW])
            todo = [(gate[:, :, :], d[f"{tag}_gate"])]
            if tag == "f0":
                b16, b4 = rt.sb("b16", [P, 16, 16]), rt.sb("b4", [P, 4, 4])
                todo += [(b16[:, :, :], d["before16"]), (b4[:, :, :], d["before4"])]
            if tag == "f3":
                b8 = rt.sb("b8", [P, 8, 8])
                todo += [(b8[:, :, :], d["before8"])]
            load(nc, todo, sem)
            tile_logits(nc, G, rt, gate, EW, logits)
            if tag == "f0":
                route_l0(nc, G, rt, logits, combine, b16, b4)
            elif tag == "f2":
                route_l2(nc, G, rt, logits, combine)
            else:
                route_l3(nc, G, rt, logits, combine, b8)
            pT = rt.ps("pT", [P, NBLK, BLK])
            turned, stored = rt.sem("turned"), rt.sem("stored")
            with nc.Block() as block:
                @block.tensor
                def _(pe):
                    for t in range(TILES):
                        pe.transpose(pT[0:E1, t // TPB, (t % TPB) * P:(t % TPB + 1) * P], combine[:, t, :],
                                     G.ident[:, :]).then_inc(turned, 1)

                @block.vector
                def _(dve):
                    for b in range(NBLK):
                        dve.wait_ge(turned, TPB * (b + 1))
                        dve.tensor_copy(combT[:, b * BLK:(b + 1) * BLK], pT[0:E1, b, :]).then_inc(stored, 1)
        w_in = [st.sb(f"w_in{u}", [P, 5, P]) for u in range(2)]
        w_out = [st.sb(f"w_out{u}", [P, D]) for u in range(2)]
        act_g = [st.sb(f"act_g{u}", [P, BLK]) for u in range(2)]
        hidden = [st.sb(f"hidden{u}", [P, BLK]) for u in range(2)]
        pg = [st.ps(f"pg{u}", [P, BLK]) for u in range(2)]
        pu = [st.ps(f"pu{u}", [P, BLK]) for u in range(2)]
        pc = [st.ps(f"pc{u}", [P, BLK]) for u in range(2)]
        py = st.ps("py", [P, TPB, D])
        win_in = [st.sem(f"w_in_here{u}") for u in range(2)]
        wout_in = [st.sem(f"w_out_here{u}") for u in range(2)]
        up_made = [st.sem(f"up_made{u}") for u in range(2)]
        silu_done = [st.sem(f"silu_done{u}") for u in range(2)]
        gated = [st.sem(f"gated{u}") for u in range(2)]
        hid_done = [st.sem(f"hid_done{u}") for u in range(2)]
        down_made = [st.sem(f"down_made{u}") for u in range(2)]
        y_made, y_taken = st.sem("y_made"), st.sem("y_taken")
        n = [(FT + 1) // 2, FT // 2]
        pairs = (FT - 1) // 2

        with nc.Block() as block:
            @block.sync
            def _(sp):
                def fetch(b, jj, u):
                    sp.wait_ge(up_made[u], b * n[u] + jj + 1)
                    sp.dma_start(w_in[u][:, :, :], W[bass.ds(jj * 2 + u, 1)].rearrange("o p c m -> (o p) c m")
                                 ).then_inc(win_in[u], 16)
                    sp.wait_ge(down_made[u], b * n[u] + jj + 1)
                    sp.dma_start(w_out[u][:, :], WO[bass.ds(jj * 2 + u, 1)].rearrange("o p m -> (o p) m")
                                 ).then_inc(wout_in[u], 16)

                with sp.Fori(0, NBLK) as b:
                    with sp.Fori(0, FT // 2) as jj:
                        for u in range(2):
                            fetch(b, jj, u)
                    if FT % 2:
                        fetch(b, FT // 2, 0)

            @block.tensor
            def _(pe):
                def up(b, jj, u):
                    pe.wait_ge(win_in[u], (b * n[u] + jj + 1) * 16)
                    pe.wait_ge(hid_done[u], b * n[u] + jj + 1)
                    for c, out in ((0, pg[u]), (1, pu[u])):
                        for k in range(KC):
                            pe.matmul(out[:, :], w_in[u][:, 2 * c + k, :], G.xT[:, k, dyn(b, BLK)],
                                      start=(k == 0), stop=(k == KC - 1))
                    pe.matmul(pc[u][:, :], w_in[u][0:E1, 4, :], combT[:, dyn(b, BLK)],
                              start=True, stop=True).then_inc(up_made[u], 1)

                def down(b, jj, u):
                    pe.wait_ge(wout_in[u], (b * n[u] + jj + 1) * 16)
                    pe.wait_ge(hid_done[u], b * n[u] + jj + 2)
                    for t in range(TPB):
                        last = pe.matmul(py[:, t, :], hidden[u][:, t * P:(t + 1) * P], w_out[u][:, :],
                                         start=False, stop=False, skip_group_check=True)
                    last.then_inc(down_made[u], 1)

                prime(pe, *up_made, *down_made)
                with pe.Fori(0, NBLK) as b:
                    up(b, 0, 0)
                    pe.wait_ge(y_taken, b + 1)
                    for h in range(2):
                        pe.matmul(py[:, 2 * h:2 * h + 2, :], G.zero[0:1, 0:P], G.zero[0:1, 0:BLK],
                                  start=True, stop=False, skip_group_check=True)
                    with pe.Fori(0, pairs) as jj:
                        up(b, jj, 1)
                        down(b, jj, 0)
                        up(b, jj + 1, 0)
                        down(b, jj, 1)
                    if FT % 2 == 0:
                        up(b, pairs, 1)
                    down(b, pairs, 0)
                    if FT % 2 == 0:
                        down(b, pairs, 1)
                    for h in range(2):
                        last = pe.matmul(py[:, 2 * h:2 * h + 2, :], G.zero[0:1, 0:P], G.zero[0:1, 0:BLK],
                                         start=False, stop=True, skip_group_check=True)
                    last.then_inc(y_made, 1)

            @block.scalar
            def _(act):
                def silu(b, jj, u):
                    act.wait_ge(up_made[u], b * n[u] + jj + 2)
                    act.wait_ge(hid_done[u], b * n[u] + jj + 1)
                    act.activation(act_g[u][:, :], pg[u][:, :], ACT.Silu).then_inc(silu_done[u], 1)

                prime(act, y_taken)
                with act.Fori(0, NBLK) as b:
                    with act.Fori(0, FT // 2) as jj:
                        for u in range(2):
                            silu(b, jj, u)
                    if FT % 2:
                        silu(b, FT // 2, 0)
                    act.wait_ge(y_made, b + 1)
                    act.copy(G.y[:, dyn(b, TPB), :], py[:, :, :]).then_inc(y_taken, 1)

            @block.vector
            def _(dve):
                def gate_hidden(b, jj, u):
                    dve.wait_ge(silu_done[u], b * n[u] + jj + 1)
                    dve.wait_ge(down_made[u], b * n[u] + jj + 1)
                    dve.tensor_tensor(act_g[u][:, :], act_g[u][:, :], pu[u][:, :], ALU.mult).then_inc(gated[u], 1)
                    dve.wait_ge(gated[u], b * n[u] + jj + 1)
                    dve.tensor_tensor(hidden[u][:, :], act_g[u][:, :], pc[u][:, :], ALU.mult).then_inc(hid_done[u], 1)

                prime(dve, *hid_done)
                with dve.Fori(0, NBLK) as b:
                    with dve.Fori(0, FT // 2) as jj:
                        for u in range(2):
                            gate_hidden(b, jj, u)
                    if FT % 2:
                        gate_hidden(b, FT // 2, 0)


def store_y(act, G, py, y_made, y_taken, b):
    act.wait_ge(y_made, b + 1)
    act.copy(G.y[:, dyn(b, TPB), :], py[:, :, :]).then_inc(y_taken, 1)


def random_feature_attention(nc, G, tag, d):
    TWO_PI_HI = 6.28125
    TWO_PI_LO = 2 * np.pi - TWO_PI_HI
    ROUND = 12582912.0
    PI = 3.1415925
    HQ, HK, HD, NF = 16, 8, 16, 8
    H, QK = HQ + HK, (HQ + HK) * HD
    with Stage(nc, tag) as st:
        w, b_row = st.sb("w", [P, KC, 2 * BLK]), st.sb("b_row", [1, 2 * BLK])
        wo, bo = st.sb("wo", [P, KC, D]), st.sb("bo", [1, D])
        cos_t, sin_t = st.sb("cos", [P, HD]), st.sb("sin", [P, HD])
        rmat, ones = st.sb("rmat", [P, HK * NF]), st.sb("ones", [1, P])
        xt = st.sb("xt", [P, KC, P])
        x, t1, v = st.sb("x", [P, H, HD]), st.sb("t1", [P, H, HD]), st.sb("v", [P, HK, HD])
        norm = st.sb("norm", [P, H])
        xT = st.sb("xT", [P, 3, P])
        heads_first = nc.dram_tensor("heads_first", (BATCH, HQ, SEQ, HD), F32, kind="Internal").ap()
        angle, whole, feat = (st.sb(m, [P, H, 2, NF]) for m in ("angle", "whole", "feat"))
        prod, sim, o, oT = st.sb("prod", [P, HQ, HK * HD]), st.sb("sim", [P, HQ * HK]), st.sb("o", [P, HQ * HD]), st.sb("oT", [P, KC, P])
        pA, pB, pT = st.ps("pA", [P, BLK]), st.ps("pB", [P, BLK]), st.ps("pT", [P, 3, P])
        pF, pOT, pY = st.ps("pF", [P, H, NF]), st.ps("pOT", [P, KC, P]), st.ps("pY", [P, D])
        load(nc, [(w[:, :, :], d["a0_w"]), (b_row[:, :], d["a0_b"]), (wo[:, :, :], d["a0_wo"]), (bo[:, :], d["a0_bo"]),
                  (cos_t[:, :], d["a0_cos"]), (sin_t[:, :], d["a0_sin"]), (ones[:, :], d["ones_row"]),
                  (rmat[:, :], d["zero"][:, 0:64])], st.sem("loaded"))
        load(nc, [(rmat[HD * h:HD * h + HD, NF * h:NF * h + NF], d["a0_r"]) for h in range(8)], st.sem("loaded_r"))
        z = {m: st.sem(m) for m in ("copied", "projected", "v_kept", "squared", "rooted", "unit", "turned", "t_kept",
                                    "random", "reduced", "featured", "o_ready", "o_turned", "ot_kept", "y_made", "done", "dstep",
                                    "o_sent", "o_here")}
        with nc.Block() as block:
            @block.tensor
            def _(pe):
                with pe.Fori(0, TILES) as t:
                    pe.wait_ge(z["copied"], t + 1)
                    for out, at, n in ((pA, 0, BLK), (pB, BLK, QK)):
                        for k in range(KC):
                            pe.matmul(out[:, 0:n], xt[:, k, :], w[:, k, at:at + n], start=(k == 0), stop=False)
                        last = pe.matmul(out[:, 0:n], ones[:, :], b_row[:, at:at + n], start=False, stop=True)
                    last.then_inc(z["projected"], 1)
                    pe.wait_ge(z["unit"], t + 1)
                    for c in range(3):
                        last = pe.transpose(pT[:, c, :], x[:, 8 * c:8 * c + 8, :], G.ident[:, :])
                    last.then_inc(z["turned"], 1)
                    pe.wait_ge(z["t_kept"], t + 1)
                    for c in range(3):
                        last = pe.matmul(pF[:, 8 * c:8 * c + 8, :], xT[:, c, :], rmat[:, :], start=True, stop=True)
                    last.then_inc(z["random"], 1)

            @block.scalar
            def _(act):
                with act.Fori(0, TILES) as t:
                    act.wait_ge(z["o_ready"], t + 1)
                    act.copy(xt[:, :, :], G.xT[:, :, dyn(t, P)]).then_inc(z["copied"], 1)
                    act.wait_ge(z["squared"], t + 1)
                    act.mul(v[:, :, :], pA[:, QK:BLK].rearrange("p (h e) -> p h e", e=HD), 0.125).then_inc(z["v_kept"], 1)
                    act.activation(norm[:, :], norm[:, :], ACT.Sqrt).then_inc(z["rooted"], 1)
                    act.wait_ge(z["turned"], t + 1)
                    act.copy(xT[:, :, :], pT[:, :, :]).then_inc(z["t_kept"], 1)
                    act.wait_ge(z["reduced"], t + 1)
                    act.activation(feat[:, :, :, :], angle[:, :, :, :], ACT.Sin).then_inc(z["featured"], 1)

            @block.vector
            def _(dve):
                prime(dve, z["o_ready"])
                with dve.Fori(0, TILES) as t:
                    step = Count(dve, z["dstep"], 17, t)
                    a = pA[:, 0:QK].rearrange("p (h e) -> p h e", e=HD)
                    b = pB[:, 0:QK].rearrange("p (h e) -> p h e", e=HD)
                    dve.wait_ge(z["projected"], t + 1)
                    step(dve.tensor_tensor(x[:, :, :], a, rows(cos_t[:, :], H), ALU.mult))
                    step(dve.tensor_tensor(t1[:, :, :], b, rows(sin_t[:, :], H), ALU.mult))
                    step(dve.tensor_tensor(x[:, :, :], x[:, :, :], t1[:, :, :], ALU.add))
                    step(dve.tensor_tensor(t1[:, :, :], x[:, :, :], x[:, :, :], ALU.mult))
                    dve.tensor_reduce(norm[:, :], t1[:, :, :], AX.X, ALU.add).then_inc(z["squared"], 1)
                    dve.wait_ge(z["rooted"], t + 1)
                    step(dve.tensor_scalar(norm[:, :], norm[:, :], 1e-6, None, ALU.max))
                    step(dve.reciprocal(norm[:, :], norm[:, :]))
                    dve.tensor_tensor(x[:, :, :], x[:, :, :], cols(norm[:, :], HD), ALU.mult).then_inc(z["unit"], 1)
                    dve.wait_ge(z["random"], t + 1)
                    for j in range(2):
                        step(dve.tensor_scalar(whole[:, :, j, :], pF[:, :, :], 1.0 / (2 * np.pi), 0.25 * j, ALU.mult, ALU.add))
                    step(dve.tensor_scalar(whole[:, :, :, :], whole[:, :, :, :], ROUND, None, ALU.add))
                    step(dve.tensor_scalar(whole[:, :, :, :], whole[:, :, :, :], -ROUND, None, ALU.add))
                    for j in range(2):
                        step(dve.scalar_tensor_tensor(angle[:, :, j, :], whole[:, :, j, :], -TWO_PI_HI, pF[:, :, :],
                                                      ALU.mult, ALU.add))
                    step(dve.scalar_tensor_tensor(angle[:, :, :, :], whole[:, :, :, :], -TWO_PI_LO, angle[:, :, :, :],
                                                  ALU.mult, ALU.add))
                    step(dve.tensor_scalar(angle[:, :, 1, :], angle[:, :, 1, :], float(np.pi / 2), None, ALU.add))
                    dve.tensor_scalar(angle[:, :, :, :], angle[:, :, :, :], PI, -PI, ALU.min, ALU.max).then_inc(z["reduced"], 1)
                    dve.wait_ge(z["featured"], t + 1)
                    full = [P, HQ, HK, HD]
                    f = feat[:, :, :, :].rearrange("p h j e -> p h (j e)")
                    fq = f[:, 0:HQ, :].rearrange("p h (o f) -> p h o f", o=1).to_broadcast(full)
                    fk = f[:, HQ:H, :].rearrange("p (o h) f -> p o h f", o=1).to_broadcast(full)
                    step(dve.tensor_tensor(prod[:, :, :].rearrange("p h (g f) -> p h g f", f=HD), fq, fk, ALU.mult))
                    step(dve.tensor_reduce(sim[:, :], prod[:, :, :].rearrange("p h (g f) -> p (h g) f", f=HD), AX.X, ALU.add))
                    dve.wait_ge(z["v_kept"], t + 1)
                    full = [P, HQ, HD, HK]
                    s4 = sim[:, :].rearrange("p (h o g) -> p h o g", o=1, g=HK).to_broadcast(full)
                    v4 = v[:, :, :].rearrange("p (o g) e -> p o e g", o=1).to_broadcast(full)
                    step(dve.tensor_tensor(prod[:, :, :].rearrange("p h (e g) -> p h e g", g=HK), s4, v4, ALU.mult))
                    dve.wait_ge(z["o_sent"], t * 32 + 1)
                    dve.tensor_reduce(o[:, :], prod[:, :, :].rearrange("p h (e g) -> p (h e) g", g=HK), AX.X,
                                      ALU.add).then_inc(z["o_ready"], 1)
                    step.end()

            @block.sync
            def _(sp):
                sp.sem_inc(z["o_sent"], 1)
                with sp.Fori(0, TILES) as t:
                    sp.wait_ge(z["o_ready"], t + 2)
                    for s in range(2):
                        sp.dma_start(heads_first[dyn(t * 2 + s, 1)].rearrange("o h t e -> (o t) h e"),
                                     o[s * SEQ:(s + 1) * SEQ, :].rearrange("p (h e) -> p h e", e=HD)).then_inc(z["o_sent"], 16)
                sp.wait_ge(z["o_sent"], TILES * 32 + 1)

        load(nc, [(G.y[:, :, :], heads_first.rearrange("(n s) h (j t) e -> (s h j) n (t e)", s=2, j=4))], st.sem("reshaped"))
        with nc.Block() as block:
            @block.scalar
            def _(act):
                with act.Fori(0, TILES) as t:
                    act.wait_ge(z["o_turned"], t + 1)
                    act.copy(o[:, :].rearrange("p (o e) -> p o e", o=1), G.y[:, dyn(t, 1), :]).then_inc(z["o_here"], 1)
                    act.wait_ge(z["o_turned"], t + 2)
                    act.copy(oT[:, :, :], pOT[:, :, :]).then_inc(z["ot_kept"], 1)

            @block.vector
            def _(dve):
                prime(dve, z["done"])
                with dve.Fori(0, TILES) as t:
                    dve.wait_ge(z["y_made"], t + 1)
                    dve.tensor_scalar(G.y[:, dyn(t, 1), :], pY[:, :].rearrange("p (o e) -> p o e", o=1), 1.0, None,
                                      ALU.mult).then_inc(z["done"], 1)

            @block.tensor
            def _(pe):
                prime(pe, z["o_turned"])
                with pe.Fori(0, TILES) as t:
                    pe.wait_ge(z["o_here"], t + 1)
                    for c in range(KC):
                        last = pe.transpose(pOT[:, c, :], o[:, c * P:(c + 1) * P], G.ident[:, :])
                    last.then_inc(z["o_turned"], 1)
                    pe.wait_ge(z["ot_kept"], t + 1)
                    pe.wait_ge(z["done"], t + 1)
                    for c in range(KC):
                        pe.matmul(pY[:, :], oT[:, c, :], wo[:, c, :], start=(c == 0), stop=False)
                    pe.matmul(pY[:, :], ones[:, :], bo[:, :], start=False, stop=True).then_inc(z["y_made"], 1)


def wkv(nc, G, tag, d):
    S1 = SEQ + 1
    NEG = -1e38
    with Stage(nc, tag) as st:
        wu = st.sb("wu", [P, 2, KC])
        vT = st.sb("vT", [P, NTOK])
        names = ["wtab", "k1", "o", "a2", "e2", "e2v", "p", "q"]
        B = {m: st.sb(m, [P, BATCH, S1]) for m in names}
        no, a, e = st.sb("no", [P, BATCH, SEQ]), st.sb("a", [P, BATCH, SEQ]), st.sb("e", [P, BATCH, SEQ])
        yT = st.sb("yT", [P, KC, NTOK])
        py = st.ps("py", [P, TILES, D])
        v_here, dve_step, half1, exp1 = st.sem("v_here"), st.sem("step"), st.sem("half1"), st.sem("exp1")
        half2, exp2, made, turned, v_used = st.sem("half2"), st.sem("exp2"), st.sem("made"), st.sem("turned"), st.sem("v_used")
        load(nc, [(wu[:, :, :], d["x0_wu"])], st.sem("loaded"))
        flat = {m: B[m][:, :, :].rearrange("p b s -> p (b s)") for m in names}
        pad = {m: B[m][:, :, 0:1] for m in names}
        cur = {m: B[m][:, :, 1:S1] for m in names}
        prev = {m: B[m][:, :, 0:SEQ] for m in names}
        with nc.Block() as block:
            @block.sync
            def _(sp):
                for c in range(KC):
                    if c:
                        sp.wait_ge(v_used, c)
                    sp.dma_start(vT[:, :], d["ctxT"][:, c, :]).then_inc(v_here, 16)

            @block.vector
            def _(dve):
                step = Count(dve, dve_step)
                v3 = vT[:, :].rearrange("p (b s) -> p b s", s=SEQ)
                for m in ("a2", "e2", "e2v"):
                    step(dve.memset(pad[m], 0.0))
                step(dve.memset(pad["k1"], NEG))
                for c in range(KC):
                    w, u = wu[:, 0, c:c + 1], wu[:, 1, c:c + 1]
                    k3 = G.xT[:, c, :].rearrange("p (b s) -> p b s", s=SEQ)
                    step(dve.tensor_copy(cur["k1"], k3))
                    step(dve.memset(flat["wtab"], 0.0))
                    step(dve.tensor_scalar(flat["wtab"], flat["wtab"], w, None, ALU.add))
                    step(dve.memset(pad["wtab"], NEG))
                    step(dve.tensor_tensor_scan(flat["o"], flat["wtab"], flat["k1"], NEG, ALU.add, ALU.max))
                    step(dve.scalar_tensor_tensor(cur["a2"], prev["o"], w, cur["o"], ALU.add, ALU.subtract))
                    dve.tensor_tensor(cur["e2"], k3, cur["o"], ALU.subtract).then_inc(half1, 1)
                    step(dve.scalar_tensor_tensor(no[:, :, :], k3, u, prev["o"], ALU.add, ALU.max))
                    step(dve.tensor_tensor(a[:, :, :], prev["o"], no[:, :, :], ALU.subtract))
                    dve.scalar_tensor_tensor(e[:, :, :], k3, u, no[:, :, :], ALU.add, ALU.subtract).then_inc(half2, 1)
                    dve.wait_ge(exp1, c + 1)
                    dve.wait_ge(v_here, 16 * (c + 1))
                    step(dve.tensor_tensor(cur["e2v"], cur["e2"], v3, ALU.mult))
                    step(dve.tensor_tensor_scan(flat["p"], flat["a2"], flat["e2v"], 0.0, ALU.mult, ALU.add))
                    step(dve.tensor_tensor_scan(flat["q"], flat["a2"], flat["e2"], 0.0, ALU.mult, ALU.add))
                    dve.wait_ge(exp2, c + 1)
                    step(dve.tensor_tensor(prev["p"], prev["p"], a[:, :, :], ALU.mult))
                    step(dve.tensor_tensor(prev["q"], prev["q"], a[:, :, :], ALU.mult))
                    step(dve.tensor_tensor(prev["q"], prev["q"], e[:, :, :], ALU.add))
                    dve.tensor_tensor(a[:, :, :], e[:, :, :], v3, ALU.mult).then_inc(v_used, 1)
                    dve.wait_ge(v_used, c + 1)
                    step(dve.tensor_tensor(prev["p"], prev["p"], a[:, :, :], ALU.add))
                    step(dve.reciprocal(prev["q"], prev["q"]))
                    dve.tensor_tensor(yT[:, c, :].rearrange("p (b s) -> p b s", s=SEQ), prev["p"], prev["q"],
                                      ALU.mult).then_inc(made, 1)

            @block.scalar
            def _(act):
                for c in range(KC):
                    act.wait_ge(half1, c + 1)
                    act.activation(cur["a2"], cur["a2"], ACT.Exp)
                    act.activation(cur["e2"], cur["e2"], ACT.Exp).then_inc(exp1, 1)
                    act.wait_ge(half2, c + 1)
                    act.activation(a[:, :, :], a[:, :, :], ACT.Exp)
                    act.activation(e[:, :, :], e[:, :, :], ACT.Exp).then_inc(exp2, 1)
                for g in range(NBLK):
                    act.wait_ge(turned, (KC - 1) * NBLK + g + 1)
                    act.copy(G.y[:, g * TPB:(g + 1) * TPB, :], py[:, g * TPB:(g + 1) * TPB, :])

            @block.tensor
            def _(pe):
                for c in range(KC):
                    pe.wait_ge(made, c + 1)
                    for t in range(TILES):
                        ins = pe.transpose(py[:, t, c * P:(c + 1) * P], yT[:, c, t * P:(t + 1) * P], G.ident[:, :])
                        if t % TPB == TPB - 1:
                            ins.then_inc(turned, 1)


def ternary_ffn(nc, G, tag, d):
    FF = 1024
    FT = FF // P
    with Stage(nc, tag) as st:
        w1, w2 = st.sb("w1", [P, KC * FF]), st.sb("w2", [P, FT * D])
        q1, q2 = st.sb("q1", [P, KC, FF]), st.sb("q2", [P, FT, D])
        b1, b2, ones = st.sb("b1", [P, FT]), st.sb("b2", [1, D]), st.sb("ones", [1, P])
        allp = st.sb("allp", [P, P])
        part, thr = st.sb("part", [P, 2]), st.sb("thr", [P, 2, 2])
        low = st.sb("low", [P, KC * FF])
        hidden = [st.sb(f"hidden{u}", [P, BLK]) for u in range(2)]
        ph = [st.ps(f"ph{u}", [P, BLK]) for u in range(2)]
        py, psum = st.ps("py", [P, TPB, D]), st.ps("psum", [P, 2])
        load(nc, [(w1[:, :], d["f1_w1"].rearrange("p k f -> p (k f)")), (w2[:, :], d["f1_w2"].rearrange("p k f -> p (k f)")),
                  (b1[:, :], d["f1_b1"]), (b2[:, :], d["f1_b2"]),
                  (ones[:, :], d["ones_row"]), (allp[:, :], d["all_ones"])], st.sem("loaded"))
        q_step, parted, summed = st.sem("q_step"), st.sem("parted"), st.sem("summed")
        with nc.Block() as block:
            @block.vector
            def _(dve):
                step = Count(dve, q_step)
                step(dve.tensor_reduce(part[:, 0:1], w1[:, :], AX.X, ALU.add, apply_absolute_value=True))
                dve.tensor_reduce(part[:, 1:2], w2[:, :], AX.X, ALU.add, apply_absolute_value=True).then_inc(parted, 1)
                dve.wait_ge(summed, 1)
                step(dve.tensor_scalar(thr[:, 1, :], psum[:, :], 1.0 / (FF * D), None, ALU.mult))
                step(dve.tensor_scalar(thr[:, 0, :], thr[:, 1, :], 0.7, None, ALU.mult))
                step(dve.tensor_scalar(thr[:, 1, :], thr[:, 0, :], -1.0, None, ALU.mult))
                for m, (w, q) in enumerate(((w1, q1), (w2, q2))):
                    flat = q[:, :, :].rearrange("p k f -> p (k f)")
                    step(dve.tensor_scalar(flat, w[:, :], thr[:, 0, m:m + 1], None, ALU.is_ge))
                    step(dve.tensor_scalar(low[:, :], w[:, :], thr[:, 1, m:m + 1], None, ALU.is_le))
                    step(dve.tensor_tensor(flat, flat, low[:, :], ALU.subtract))

            @block.tensor
            def _(pe):
                pe.wait_ge(parted, 1)
                pe.matmul(psum[:, :], allp[:, :], part[:, :], start=True, stop=True).then_inc(summed, 1)

        made = [st.sem(f"made{u}") for u in range(2)]
        gelued = [st.sem(f"gelued{u}") for u in range(2)]
        downed = [st.sem(f"downed{u}") for u in range(2)]
        y_made, y_taken = st.sem("y_made"), st.sem("y_taken")
        H = FT // 2
        with nc.Block() as block:
            @block.tensor
            def _(pe):
                prime(pe, *downed)
                with pe.Fori(0, NBLK) as b:
                    pe.wait_ge(y_taken, b + 1)
                    for h in range(2):
                        pe.matmul(py[:, 2 * h:2 * h + 2, :], ones[:, :], rows(b2[:, :], 2), start=True, stop=False,
                                  skip_group_check=True)

                    def up(f):
                        u, turn = f % 2, b * H + f // 2
                        pe.wait_ge(gelued[u], turn + 1)
                        for k in range(KC):
                            last = pe.matmul(ph[u][:, :], q1[:, k, f * P:(f + 1) * P], G.xT[:, k, dyn(b, BLK)],
                                             start=(k == 0), stop=(k == KC - 1))
                        last.then_inc(made[u], 1)

                    def down(f):
                        u, turn = f % 2, b * H + f // 2
                        pe.wait_ge(gelued[u], turn + 2)
                        for t in range(TPB):
                            last = pe.matmul(py[:, t, :], hidden[u][:, t * P:(t + 1) * P], q2[:, f, :],
                                             start=False, stop=(f == FT - 1), skip_group_check=True)
                        last.then_inc(downed[u], 1)

                    up(0)
                    for f in range(1, FT):
                        up(f)
                        down(f - 1)
                    down(FT - 1)
                    pe.matmul(psum[:, 0:1], G.zero[:, 0:P], G.zero[:, 0:1], start=True, stop=True).then_inc(y_made, 1)

            @block.scalar
            def _(act):
                prime(act, *gelued, y_taken)
                with act.Fori(0, NBLK) as b:
                    for f in range(FT):
                        u, turn = f % 2, b * H + f // 2
                        act.wait_ge(made[u], turn + 1)
                        act.wait_ge(downed[u], turn + 1)
                        act.activation(hidden[u][:, :], ph[u][:, :], ACT.Gelu, bias=b1[:, f:f + 1]).then_inc(gelued[u], 1)
                    store_y(act, G, py, y_made, y_taken, b)


def ema_summary(nc, G, tag, d):
    with Stage(nc, tag) as st:
        ctx = st.sb("ctx", [P, KC, NTOK])
        w_in, w_out = st.sb("w_in", [P, KC, D]), st.sb("w_out", [P, KC, D])
        b_in, b_out = st.sb("b_in", [P, KC]), st.sb("b_out", [1, D])
        gamma, beta, ones = st.sb("gamma", [P, D]), st.sb("beta", [P, D]), st.sb("ones", [P, SEQ])
        decay, keep = st.sb("decay", [P, 1]), st.sb("keep", [P, 1])
        ktab, wt, wsum = st.sb("ktab", [P, SEQ]), st.sb("wt", [P, SEQ]), st.sb("wsum", [P, 1])
        mean_ctx, bw, xbar = st.sb("mean_ctx", [P, KC, BATCH]), st.sb("bw", [P, KC]), st.sb("xbar", [P, KC, BATCH])
        summary, of_seq = st.sb("summary", [BATCH, D]), st.sb("of_seq", [BATCH, NTOK])
        row1 = st.sb("row1", [1, P])
        loads = [(ctx[:, :, :], d["ctxT_rev"]), (w_in[:, :, :], d["x2_w_in"]), (w_out[:, :, :], d["x2_w_out"]),
                 (b_in[:, :], d["x2_b_in"]), (b_out[:, :], d["x2_b_out"]),
                 (gamma[:, :], d["x2_gamma"].to_broadcast([P, D])), (beta[:, :], d["x2_beta"].to_broadcast([P, D])),
                 (decay[:, :], d["x2_decay"].to_broadcast([P, 1])), (ones[:, :], d["all_ones"][:, 0:SEQ]),
                 (of_seq[:, :], d["of_seq"]), (row1[:, :], d["ones_row"])]
        load(nc, loads, st.sem("loaded"))
        dstep, kept, averaged, barred, b_ready = st.sem("dstep"), st.sem("kept"), st.sem("averaged"), st.sem("barred"), st.sem("b_ready")
        summed, s_ready, spread = st.sem("summed"), st.sem("s_ready"), st.sem("spread")
        with Stage(nc, tag + "p") as pt:
            px, psm = pt.ps("px", [P, KC, BATCH]), pt.ps("psm", [BATCH, D])
            pspread = pt.ps("pspread", [P, TPB, D])
            taken = pt.sem("taken")
            with nc.Block() as block:
                @block.scalar
                def _(act):
                    act.activation(keep[:, :], decay[:, :], ACT.Sigmoid).then_inc(kept, 1)

                @block.vector
                def _(dve):
                    step = Count(dve, dstep)
                    dve.wait_ge(kept, 1)
                    step(dve.tensor_scalar(ktab[:, :], ones[:, :], keep[:, :], None, ALU.mult))
                    step(dve.tensor_tensor_scan(wt[:, :], ktab[:, :], ones[:, :], 0.0, ALU.mult, ALU.add))
                    step(dve.tensor_scalar(wt[:, :], wt[:, :], 1.0 / SEQ, None, ALU.mult))
                    step(dve.tensor_reduce(wsum[:, :], wt[:, :], AX.X, ALU.add))
                    c3 = ctx[:, :, :].rearrange("p k (b s) -> p (k b) s", s=SEQ)
                    step(dve.tensor_tensor(c3, c3, rows(wt[:, :], KC * BATCH), ALU.mult))
                    step(dve.tensor_scalar(bw[:, :], b_in[:, :], wsum[:, :], None, ALU.mult))
                    dve.tensor_reduce(mean_ctx[:, :, :], c3, AX.X, ALU.add).then_inc(averaged, 1)
                    dve.wait_ge(barred, 1)
                    for c in range(KC):
                        dve.tensor_scalar(xbar[:, c, :], px[:, c, :], bw[:, c:c + 1], None, ALU.add).then_inc(b_ready, 1)
                    dve.wait_ge(summed, 1)
                    dve.tensor_copy(summary[:, :], psm[:, :]).then_inc(s_ready, 1)
                    for g in range(NBLK):
                        dve.wait_ge(spread, g + 1)
                        dve.tensor_copy(G.y[:, g * TPB:(g + 1) * TPB, :], pspread[:, :, :]).then_inc(taken, 1)

                @block.tensor
                def _(pe):
                    pe.wait_ge(averaged, 1)
                    for c in range(KC):
                        for k in range(KC):
                            last = pe.matmul(px[:, c, :], w_in[:, k, c * P:(c + 1) * P], mean_ctx[:, k, :],
                                             start=(k == 0), stop=(k == KC - 1))
                    last.then_inc(barred, 1)
                    pe.wait_ge(b_ready, KC)
                    for k in range(KC):
                        pe.matmul(psm[:, :], xbar[:, k, :], w_out[:, k, :], start=(k == 0), stop=False)
                    pe.matmul(psm[:, :], row1[:, 0:BATCH], b_out[:, :], start=False, stop=True).then_inc(summed, 1)
                    pe.wait_ge(s_ready, 1)
                    for g in range(NBLK):
                        if g:
                            pe.wait_ge(taken, g)
                        for t in range(TPB):
                            tile = g * TPB + t
                            last = pe.matmul(pspread[:, t, :], of_seq[:, tile * P:(tile + 1) * P], summary[:, :],
                                             start=True, stop=True)
                        last.then_inc(spread, 1)
        N = Norm(st)
        step_sem, normed = st.sem("nstep"), st.sem("normed")
        with nc.Block() as block:
            @block.vector
            def _(dve):
                with dve.Fori(0, NBLK) as g:
                    step = Count(dve, step_sem, 17, g)
                    step(dve.tensor_tensor(N.s[:, :, :], G.x_tok[:, dyn(g, TPB), :], G.y[:, dyn(g, TPB), :], ALU.add))
                    normalise(dve, step, N, g, normed)
                    dve.wait_ge(normed, g + 1)
                    step(dve.tensor_tensor(N.s[:, :, :], N.s[:, :, :], rows(gamma[:, :], TPB), ALU.mult))
                    step(dve.tensor_tensor(G.y[:, dyn(g, TPB), :], N.s[:, :, :], rows(beta[:, :], TPB), ALU.add))
                    step.end()

            @block.scalar
            def _(act):
                with act.Fori(0, NBLK) as g:
                    norm_root(act, N, g)


MIXERS = {"a0": random_feature_attention, "x0": wkv, "f1": ternary_ffn, "x2": ema_summary}


def column(v):
    return np.ascontiguousarray(v.reshape(-1, P).T)


def block_ones(width, rows_=P, cols_=P, rw=None, value=1.0):
    rw = rw or width
    r, c = np.arange(rows_)[:, None] // rw, np.arange(cols_)[None, :] // width
    return np.where(r == c, value, 0.0).astype(np.float32)


def mixer_layouts(a, i):
    a["ones_row"] = np.ones((1, P), np.float32)
    a["ones_col"] = np.ones((P, 1), np.float32)
    a["all_ones"] = np.ones((P, P), np.float32)
    a["head_sum16"] = block_ones(16)
    HD = 16
    half = lambda m: m.reshape(-1, 2, HD // 2, *m.shape[1:])[:, ::-1].reshape(m.shape)
    W, B = ([i[f"L0_attn_{n}{m}"] for m in "qkv"] for n in ("W", "b"))
    a["a0_w"] = feature_major(np.concatenate([*W, half(W[0]), half(W[1]), W[2]], axis=0))
    a["a0_b"] = np.concatenate([*B, half(B[0]), half(B[1]), B[2]]).reshape(1, -1)
    a["a0_wo"], a["a0_bo"] = feature_major(i["L0_attn_Wo"]), i["L0_attn_bo"].reshape(1, D)
    inv = (1.0 / np.float32(10000.0) ** (np.arange(0, HD, 2, dtype=np.float32) / HD)).astype(np.float32)
    pos = (np.arange(P) % SEQ).astype(np.float32)
    ang = pos[:, None] * np.tile(inv, 2)[None, :]
    sign = np.where(np.arange(HD) < HD // 2, -1.0, 1.0).astype(np.float32)[None, :]
    a["a0_cos"], a["a0_sin"] = np.cos(ang).astype(np.float32), (np.sin(ang) * sign).astype(np.float32)
    a["a0_r"] = np.ascontiguousarray(i["L0_attn_rand_matrix"].T)
    a["x0_wu"] = np.ascontiguousarray(np.stack([column(i["L0_xattn_w"]), column(i["L0_xattn_u"])], axis=1))
    a["f1_w1"], a["f1_w2"] = feature_major(i["L1_ffn_w1"]), in_rows(i["L1_ffn_w2"].T)
    a["f1_b1"], a["f1_b2"] = column(i["L1_ffn_b1"]), i["L1_ffn_b2"].reshape(1, D)
    a["ctxT_rev"] = feature_major(i["ctx_2048"][:, ::-1].reshape(NTOK, D))
    a["x2_w_in"], a["x2_w_out"] = feature_major(i["L2_xattn_W_in"]), feature_major(i["L2_xattn_W_out"])
    a["x2_b_in"], a["x2_b_out"] = column(i["L2_xattn_b_in"]), i["L2_xattn_b_out"].reshape(1, D)
    a["x2_gamma"], a["x2_beta"] = i["L2_xattn_gamma"].reshape(1, D), i["L2_xattn_beta"].reshape(1, D)
    a["x2_decay"] = i["L2_xattn_decay"].reshape(1, 1)
    a["of_seq"] = np.repeat(np.eye(BATCH, dtype=np.float32), SEQ, axis=1)


def rms_heads_attention(nc, G, tag, d):
    H, HD, EPS = 32, 8, 1e-6
    HC = H // KC
    with Stage(nc, tag) as st:
        qn, kn, ctxT = st.sb("qn", [P, KC, NTOK]), st.sb("kn", [P, KC, NTOK]), st.sb("ctxT", [P, KC, NTOK])
        wq, wk, wv = (st.sb(m, [P, KC, D]) for m in ("wq", "wk", "wv"))
        head_sum, of_head = st.sb("head_sum", [P, P]), st.sb("of_head", [P, HC])
        load(nc, [(ctxT[:, :, :], d["ctxT"]), (wq[:, :, :], d["x1_wq"]), (wk[:, :, :], d["x1_wk"]), (wv[:, :, :], d["x1_wv"]),
                  (head_sum[:, :], d["head_sum8"]), (of_head[:, :], d["of_head8"])], st.sem("loaded"))
        with Stage(nc, tag + "n") as pt:
            sq = [pt.sb(f"sq{j}", [P, BLK]) for j in range(2)]
            pp = [pt.ps(f"pp{j}", [P, BLK]) for j in range(2)]
            pn = [pt.ps(f"pn{j}", [P, BLK]) for j in range(2)]
            projected, squared, summed, rooted, normed, nstep = (pt.sem(m) for m in (
                "projected", "squared", "summed", "rooted", "normed", "nstep"))
            with nc.Block() as block:
                @block.tensor
                def _(pe):
                    with pe.Fori(0, NBLK) as b:
                        for c in range(KC):
                            n = b * KC + c
                            pe.wait_ge(normed, n + 1)
                            for j, (w, src) in enumerate(((wq, G.xT), (wk, ctxT))):
                                for k in range(KC):
                                    last = pe.matmul(pp[j][:, :], w[:, k, c * P:(c + 1) * P], src[:, k, dyn(b, BLK)],
                                                     start=(k == 0), stop=(k == KC - 1))
                            last.then_inc(projected, 1)
                            pe.wait_ge(squared, n + 1)
                            for j in range(2):
                                last = pe.matmul(pn[j][:, :], head_sum[:, :], sq[j][:, :], start=True, stop=True)
                            last.then_inc(summed, 1)

                @block.scalar
                def _(act):
                    with act.Fori(0, NBLK) as b:
                        for c in range(KC):
                            n = b * KC + c
                            act.wait_ge(projected, n + 1)
                            act.activation(sq[0][:, :], pp[0][:, :], ACT.Square)
                            act.activation(sq[1][:, :], pp[1][:, :], ACT.Square).then_inc(squared, 1)
                            act.wait_ge(summed, n + 1)
                            act.activation(sq[0][:, :], pn[0][:, :], ACT.Sqrt, bias=EPS, scale=1.0 / HD)
                            act.activation(sq[1][:, :], pn[1][:, :], ACT.Sqrt, bias=EPS, scale=1.0 / HD).then_inc(rooted, 1)

                @block.vector
                def _(dve):
                    prime(dve, normed)
                    with dve.Fori(0, NBLK) as b:
                        step = Count(dve, nstep, 2 * KC, b)
                        for c in range(KC):
                            dve.wait_ge(rooted, b * KC + c + 1)
                            for j in range(2):
                                step(dve.reciprocal(sq[j][:, :], sq[j][:, :]))
                            dve.tensor_tensor(qn[:, c, dyn(b, BLK)], pp[0][:, :], sq[0][:, :], ALU.mult)
                            dve.tensor_tensor(kn[:, c, dyn(b, BLK)], pp[1][:, :], sq[1][:, :], ALU.mult).then_inc(normed, 1)
                        step.end()
        qt, kt, ct = (st.sb(m, [P, KC, P]) for m in ("qt", "kt", "ct"))
        qx = [[st.sb(f"qx{c}{s}", [P, HC, SEQ]) for s in range(2)] for c in range(KC)]
        prob = [st.sb(f"prob{c}", [P, HC, SEQ]) for c in range(KC)]
        vx, rec = st.sb("vx", [P, H, HD + 1]), st.sb("rec", [P, H])
        pS = [st.ps(f"pS{c}", [P, HC, SEQ]) for c in range(KC)]
        pV, pO = st.ps("pV", [P, D]), st.ps("pO", [P, H, HD + 1])
        copied, spread, v_made, scored, v_kept, exped, attended, done, ones_set, dstep = (st.sem(m) for m in (
            "copied", "spread", "v_made", "scored", "v_kept", "exped", "attended", "done", "ones_set", "dstep"))
        with nc.Block() as block:
            @block.scalar
            def _(act):
                with act.Fori(0, TILES) as t:
                    act.wait_ge(attended, t + 1)
                    act.copy(qt[:, :, :], qn[:, :, dyn(t, P)])
                    act.copy(kt[:, :, :], kn[:, :, dyn(t, P)])
                    act.copy(ct[:, :, :], ctxT[:, :, dyn(t, P)]).then_inc(copied, 1)
                    for c in range(KC):
                        act.wait_ge(scored, t * KC + c + 1)
                        act.activation(prob[c][:, :, :], pS[c][:, :, :], ACT.Exp, scale=HD ** -0.5).then_inc(exped, 1)

            def spread_heads(eng, c, t):
                eng.wait_ge(copied, t + 1)
                for s in range(2):
                    q = rows(qt[:, c, s * SEQ:(s + 1) * SEQ], HC)
                    eng.tensor_tensor(qx[c][s][:, :, :], q, cols(of_head[:, :], SEQ), ALU.mult).then_inc(spread, 1)

            @block.gpsimd
            def _(pool):
                with pool.Fori(0, TILES) as t:
                    spread_heads(pool, 1, t)

            @block.vector
            def _(dve):
                prime(dve, done)
                dve.memset(vx[:, :, HD:HD + 1], 1.0).then_inc(ones_set, 1)
                with dve.Fori(0, TILES) as t:
                    step = Count(dve, dstep, 1, t)
                    spread_heads(dve, 0, t)
                    dve.wait_ge(v_made, t + 1)
                    dve.tensor_copy(vx[:, :, 0:HD], pV[:, :].rearrange("p (h e) -> p h e", e=HD)).then_inc(v_kept, 1)
                    dve.wait_ge(attended, t + 2)
                    step(dve.reciprocal(rec[:, :], pO[:, :, HD]))
                    dve.tensor_tensor(G.y[:, dyn(t, 1), :].rearrange("p o (h e) -> p (o h) e", e=HD), pO[:, :, 0:HD],
                                      cols(rec[:, :], HD), ALU.mult).then_inc(done, 1)
                    step.end()

            @block.tensor
            def _(pe):
                prime(pe, attended)
                pe.wait_ge(ones_set, 1)
                with pe.Fori(0, TILES) as t:
                    pe.wait_ge(copied, t + 1)
                    for k in range(KC):
                        last = pe.matmul(pV[:, :], ct[:, k, :], wv[:, k, :], start=(k == 0), stop=(k == KC - 1))
                    last.then_inc(v_made, 1)
                    pe.wait_ge(spread, (t + 1) * 2 * KC)
                    for c in range(KC):
                        for s in range(2):
                            for h in range(0, HC, 8):
                                last = pe.matmul(pS[c][s * SEQ:(s + 1) * SEQ, h:h + 8, :], kt[:, c, s * SEQ:(s + 1) * SEQ],
                                                 qx[c][s][:, h:h + 8, :], start=True, stop=True)
                        last.then_inc(scored, 1)
                    pe.wait_ge(v_kept, t + 1)
                    pe.wait_ge(done, t + 1)
                    for c in range(KC):
                        hold(pe, G, exped, t * KC + c + 1, pO[:, c * HC, 0:1])
                        for h in range(HC):
                            for s in range(2):
                                r = slice(s * SEQ, (s + 1) * SEQ)
                                last = pe.matmul(pO[r, c * HC + h, :], prob[c][r, h, :], vx[r, c * HC + h, :],
                                                 start=True, stop=True)
                    last.then_inc(attended, 1)


def causal_attention(nc, G, tag, d):
    H, HD = 16, 16
    HC = H // KC
    SCALE = HD ** -0.5
    NAMES = ["wq", "wqr", "wk", "wkr"]
    with Stage(nc, tag) as st:
        qk = [st.sb(f"qk{j}", [P, KC, NTOK]) for j in range(2)]
        w = {m: st.sb(m, [P, KC, D]) for m in NAMES + ["wv", "wo"]}
        bias = st.sb("bias", [P, 4, KC])
        bv, bo, ones = st.sb("bv", [1, D]), st.sb("bo", [1, D]), st.sb("ones", [1, P])
        cos_t, sin_t = st.sb("cos", [P, SEQ]), st.sb("sin", [P, SEQ])
        of_head, hide = st.sb("of_head", [P, HC]), st.sb("hide", [P, SEQ])
        load(nc, [(w[m][:, :, :], d[f"a3_{m}"]) for m in w] +
             [(bias[:, :, :], d["a3_bias"]), (bv[:, :], d["a3_bv"]), (bo[:, :], d["a3_bo"]), (ones[:, :], d["ones_row"]),
              (cos_t[:, :], d["a3_cos"]), (sin_t[:, :], d["a3_sin"]), (of_head[:, :], d["of_head16"]),
              (hide[:, :], d["hide_later"])], st.sem("loaded"))
        with Stage(nc, tag + "r") as pt:
            rot = [pt.sb(f"rot{j}", [P, BLK]) for j in range(4)]
            pp = [pt.ps(f"pp{j}", [P, BLK]) for j in range(4)]
            projected, stored, rstep = pt.sem("projected"), pt.sem("stored"), pt.sem("rstep")
            with nc.Block() as block:
                @block.tensor
                def _(pe):
                    with pe.Fori(0, NBLK) as b:
                        for c in range(KC):
                            pe.wait_ge(stored, b * KC + c + 1)
                            for j, m in enumerate(NAMES):
                                for k in range(KC):
                                    last = pe.matmul(pp[j][:, :], w[m][:, k, c * P:(c + 1) * P], G.xT[:, k, dyn(b, BLK)],
                                                     start=(k == 0), stop=(k == KC - 1))
                            last.then_inc(projected, 1)

                @block.vector
                def _(dve):
                    prime(dve, stored)
                    with dve.Fori(0, NBLK) as b:
                        step = Count(dve, rstep, 8, b)
                        for c in range(KC):
                            dve.wait_ge(projected, b * KC + c + 1)
                            for j in range(4):
                                step(dve.scalar_tensor_tensor(
                                    rot[j][:, :].rearrange("p (s t) -> p s t", t=SEQ),
                                    pp[j][:, :].rearrange("p (s t) -> p s t", t=SEQ), bias[:, j, c:c + 1],
                                    rows((sin_t if j % 2 else cos_t)[:, :], BLK // SEQ), ALU.add, ALU.mult))
                            dve.tensor_tensor(qk[0][:, c, dyn(b, BLK)], rot[0][:, :], rot[1][:, :], ALU.add)
                            dve.tensor_tensor(qk[1][:, c, dyn(b, BLK)], rot[2][:, :], rot[3][:, :], ALU.add).then_inc(stored, 1)
                        step.end()
        qt, kt, xt, xs = (st.sb(m, [P, KC, P]) for m in ("qt", "kt", "xt", "xs"))
        kx = [[st.sb(f"kx{c}{s}", [P, HC, SEQ]) for s in range(2)] for c in range(KC)]
        S, E, ET = st.sb("S", [P, H, SEQ]), st.sb("E", [P, H, SEQ]), st.sb("ET", [P, H // 2, P])
        v, o, oT = st.sb("v", [P, 2, D]), st.sb("o", [P, D]), st.sb("oT", [P, KC, P])
        mx, den = st.sb("mx", [P, H]), st.sb("den", [P, H])
        pS, pV, pT = st.ps("pS", [P, H, SEQ]), st.ps("pV", [P, 2, D]), st.ps("pT", [P, H // 2, P])
        pO, last_bank = st.ps("pO", [P, 2 * BLK]), st.ps("pOT_Y", [P, 2, D])
        pO_of = lambda h: pO[:, (h % 2) * BLK + (h // 2) * HD:(h % 2) * BLK + (h // 2 + 1) * HD]
        pOT, pY = last_bank[:, 0, :].rearrange("p (c m) -> p c m", c=KC), last_bank[:, 1, :]
        names = ["copied", "spread", "scored", "v_made", "v_kept", "shifted", "exped", "turned", "et_kept", "attended",
                 "o_ready", "o_turned", "ot_kept", "y_made", "done", "dstep", "s_free"]
        z = {m: st.sem(m) for m in names}
        with nc.Block() as block:
            @block.scalar
            def _(act):
                prime(act, z["done"])
                with act.Fori(0, TILES) as t:
                    act.wait_ge(z["scored"], t + 1)
                    act.copy(qt[:, :, :], qk[0][:, :, dyn(t, P)])
                    act.copy(kt[:, :, :], qk[1][:, :, dyn(t, P)])
                    act.copy(xt[:, :, :], G.xT[:, :, dyn(t, P)])
                    act.copy(xs[:, :, 0:SEQ], G.xT[:, :, dyn(t * 2 + 1, SEQ)])
                    act.copy(xs[:, :, SEQ:P], G.xT[:, :, dyn(t * 2, SEQ)]).then_inc(z["copied"], 1)
                    act.wait_ge(z["v_made"], t + 1)
                    act.copy(v[:, :, :], pV[:, :, :]).then_inc(z["v_kept"], 1)
                    act.wait_ge(z["shifted"], t + 1)
                    act.activation(E[:, :, :], S[:, :, :], ACT.Exp).then_inc(z["exped"], 1)
                    act.wait_ge(z["turned"], t + 1)
                    act.copy(ET[:, :, :], pT[:, :, :]).then_inc(z["et_kept"], 1)
                    act.wait_ge(z["o_turned"], t + 1)
                    act.copy(oT[:, :, :], pOT).then_inc(z["ot_kept"], 1)
                    act.wait_ge(z["y_made"], t + 1)
                    act.copy(G.y[:, dyn(t, 1), :], pY.rearrange("p (o e) -> p o e", o=1)).then_inc(z["done"], 1)

            @block.gpsimd
            def _(pool):
                with pool.Fori(0, TILES) as t:
                    pool.wait_ge(z["copied"], t + 1)
                    for c in range(KC):
                        for s in range(2):
                            pool.tensor_tensor(kx[c][s][:, :, :], rows(kt[:, c, s * SEQ:(s + 1) * SEQ], HC),
                                               cols(of_head[:, :], SEQ), ALU.mult).then_inc(z["spread"], 1)

            @block.vector
            def _(dve):
                prime(dve, z["s_free"])
                with dve.Fori(0, TILES) as t:
                    step = Count(dve, z["dstep"], 4, t)
                    dve.wait_ge(z["scored"], t + 2)
                    step(dve.scalar_tensor_tensor(S[:, :, :], pS[:, :, :], SCALE, rows(hide[:, :], H), ALU.mult, ALU.add))
                    step(dve.tensor_reduce(mx[:, :], S[:, :, :], AX.X, ALU.max))
                    dve.tensor_tensor(S[:, :, :], S[:, :, :], cols(mx[:, :], SEQ), ALU.subtract).then_inc(z["shifted"], 1)
                    dve.wait_ge(z["exped"], t + 1)
                    step(dve.tensor_reduce(den[:, :], E[:, :, :], AX.X, ALU.add))
                    step(dve.reciprocal(den[:, :], den[:, :]))
                    dve.wait_ge(z["attended"], t + 1)
                    for odd in range(2):
                        part = pO[:, odd * BLK:odd * BLK + H // 2 * HD].rearrange("p (h e) -> p h e", e=HD)
                        scale = cols(den[:, :].rearrange("p (h two) -> p h two", two=2)[:, :, odd], HD)
                        last = dve.tensor_tensor(o[:, :].rearrange("p (h two e) -> p h two e", two=2, e=HD)[:, :, odd, :],
                                                 part, scale, ALU.mult)
                    last.then_inc(z["o_ready"], 1)
                    step.end()

            @block.tensor
            def _(pe):
                prime(pe, z["scored"])
                with pe.Fori(0, TILES) as t:
                    pe.wait_ge(z["copied"], t + 1)
                    pe.wait_ge(z["done"], t + 1)
                    for j, src in enumerate((xt, xs)):
                        for k in range(KC):
                            pe.matmul(pV[:, j, :], src[:, k, :], w["wv"][:, k, :], start=(k == 0), stop=False)
                        last = pe.matmul(pV[:, j, :], ones[:, :], bv[:, :], start=False, stop=True)
                    last.then_inc(z["v_made"], 1)
                    pe.wait_ge(z["spread"], (t + 1) * 2 * KC)
                    for c in range(KC):
                        for s in range(2):
                            last = pe.matmul(pS[s * SEQ:(s + 1) * SEQ, c * HC:(c + 1) * HC, :],
                                             qt[:, c, s * SEQ:(s + 1) * SEQ], kx[c][s][:, :, :], start=True, stop=True)
                    last.then_inc(z["scored"], 1)
                    pe.wait_ge(z["exped"], t + 1)
                    for hh in range(H // 2):
                        last = pe.transpose(pT[:, hh, :], E[:, 2 * hh:2 * hh + 2, :], G.ident[:, :])
                    last.then_inc(z["turned"], 1)
                    pe.wait_ge(z["et_kept"], t + 1)
                    hold(pe, G, z["v_kept"], t + 1, pO[:, 0:1])
                    for h in range(H):
                        for s in range(2):
                            r = slice((h % 2) * SEQ, (h % 2 + 1) * SEQ)
                            last = pe.matmul(pO_of(h)[s * SEQ:(s + 1) * SEQ, :], ET[r, h // 2, s * SEQ:(s + 1) * SEQ],
                                             v[r, int(h % 2 != s), h * HD:(h + 1) * HD], start=True, stop=True)
                    last.then_inc(z["attended"], 1)
                    pe.wait_ge(z["o_ready"], t + 1)
                    for c in range(KC):
                        last = pe.transpose(pOT[:, c, :], o[:, c * P:(c + 1) * P], G.ident[:, :])
                    last.then_inc(z["o_turned"], 1)
                    pe.wait_ge(z["ot_kept"], t + 1)
                    for c in range(KC):
                        pe.matmul(pY, oT[:, c, :], w["wo"][:, c, :], start=(c == 0), stop=False)
                    pe.matmul(pY, ones[:, :], bo[:, :], start=False, stop=True).then_inc(z["y_made"], 1)


def feature_attention(nc, G, tag, d):
    HD, H = 8, 8
    SCALE = HD ** -0.5
    AUG = SEQ + H
    WIDE = P + HD
    with Stage(nc, tag) as st:
        ctxT, ctx = st.sb("ctxT", [P, KC, NTOK]), st.sb("ctx", [P, TILES, D])
        of_head, minus_head = st.sb("of_head", [P, H]), st.sb("minus_head", [AUG, H])
        load(nc, [(ctxT[:, :, :], d["ctxT"]), (ctx[:, :, :], d["ctx_tok"]), (of_head[:, :], d["x3_of_head"]),
                  (minus_head[:, :], d["x3_minus_head"])], st.sem("loaded"))
        xt, kmask = st.sb("xt", [P, D]), st.sb("kmask", [P, H, D])
        kaug = [st.sb(f"kaug{s}", [AUG, D]) for s in range(2)]
        qaug = [st.sb(f"qaug{s}", [AUG, H, D]) for s in range(2)]
        vx = [[st.sb(f"vx{s}{c}", [P, H * WIDE]) for c in range(KC)] for s in range(2)]
        mx = st.sb("mx", [P, 2 * KC, P])
        prob = [[st.sb(f"prob{s}{c}", [P, H, D]) for c in range(KC)] for s in range(2)]
        rec = [st.sb(f"rec{s}", [SEQ, D]) for s in range(2)]
        pS = [st.ps(f"pS{u}", [P, 4, D]) for u in range(2)]
        pM, pO = st.ps("pM", [P, 2 * KC, P]), st.ps("pO", [P, 2, D])
        names = ["set_up", "x_here", "k_ready", "v_ready", "q_ready", "scored", "maxed", "m_turned", "aug_ready", "exped",
                 "shifted", "attended", "done", "dstep", "turn_done"]
        z = {m: st.sem(m) for m in names}
        with nc.Block() as block:
            @block.vector
            def _(dve):
                for s in range(2):
                    dve.memset(kaug[s][SEQ:AUG, :], 1.0)
                    for c in range(KC):
                        dve.memset(vx[s][c][:, :], 0.0)
                dve.memset(mx[:, :, :], 0.0).then_inc(z["set_up"], 1)
                dve.wait_ge(z["set_up"], 1)
                for s in range(2):
                    for c in range(KC):
                        v = vx[s][c][:, :].rearrange("p (h q) -> p h q", q=WIDE)
                        dve.memset(v[:, :, SEQ:SEQ + HD], 1.0)

        with nc.Block() as block:
            @block.gpsimd
            def _(pool):
                with pool.Fori(0, TILES) as t:
                    pool.wait_ge(z["attended"], t + 1)
                    for s in range(2):
                        for c in range(KC):
                            v = vx[s][c][:, :].rearrange("p (h q) -> p h q", q=WIDE)[:, :, 0:HD]
                            src = ctxT[:, c, dyn(t * 2 + s, SEQ)].rearrange("p (h e) -> p h e", e=HD)
                            pool.tensor_copy(v, src).then_inc(z["v_ready"], 1)
                    pool.wait_ge(z["v_ready"], t * 4 + 4)
                    pool.wait_ge(z["x_here"], t + 1)
                    for s in range(2):
                        r = slice(s * SEQ, (s + 1) * SEQ)
                        pool.tensor_tensor(qaug[s][0:SEQ, :, :], rows(xt[r, :], H), cols(of_head[r, :], D),
                                           ALU.mult).then_inc(z["q_ready"], 1)
                        pool.wait_ge(z["q_ready"], t * 2 + s + 1)

            @block.scalar
            def _(act):
                with act.Fori(0, TILES) as t:
                    act.wait_ge(z["attended"], t + 1)
                    act.copy(xt[:, :].rearrange("p (o m) -> p o m", o=1), G.x_tok[:, dyn(t, 1), :]).then_inc(z["x_here"], 1)
                    for s in range(2):
                        act.copy(kaug[s][0:SEQ, :].rearrange("p (o m) -> p o m", o=1),
                                 ctx[s * SEQ:(s + 1) * SEQ, dyn(t, 1), :]).then_inc(z["k_ready"], 1)
                    for j in range(8):
                        s, c, half = j // 4, (j // 2) % 2, j % 2
                        act.wait_ge(z["shifted"], t * 8 + j + 1)
                        act.activation(prob[s][c][:, half * 4:half * 4 + 4, :], pS[j % 2][:, :, :], ACT.Exp,
                                       scale=SCALE).then_inc(z["exped"], 1)

            @block.vector
            def _(dve):
                prime(dve, z["done"])
                with dve.Fori(0, TILES) as t:
                    step = Count(dve, z["dstep"], 3, t)
                    dve.wait_ge(z["attended"], t + 1)
                    step(dve.tensor_tensor(kmask[:, :, :], ctx[:, dyn(t, 1), :].to_broadcast([P, H, D]),
                                           cols(of_head[:, :], D), ALU.mult))
                    for j in range(8):
                        g, half = j // 2, j % 2
                        dve.wait_ge(z["scored"], t * 8 + j + 1)
                        dve.tensor_reduce(mx[:, g, SEQ + half * 4:SEQ + half * 4 + 4], pS[j % 2][:, :, :], AX.X,
                                          ALU.max).then_inc(z["maxed"], 1)
                    dve.wait_ge(z["m_turned"], t + 1)
                    for s in range(2):
                        m = pM[SEQ:AUG, s * KC:(s + 1) * KC, :].rearrange("p c m -> p (c m)")
                        dve.tensor_tensor(qaug[s][SEQ:AUG, :, :], rows(m, H), cols(minus_head[SEQ:AUG, :], D),
                                          ALU.mult).then_inc(z["aug_ready"], 1)
                    dve.wait_ge(z["attended"], t + 2)
                    for s in range(2):
                        step(dve.reciprocal(rec[s][:, :], pO[SEQ:P, s, :]))
                    for s in range(2):
                        last = dve.tensor_tensor(G.y[s * SEQ:(s + 1) * SEQ, dyn(t, 1), :],
                                                 pO[0:SEQ, s:s + 1, :], rec[s][:, :].rearrange("p (o m) -> p o m", o=1),
                                                 ALU.mult)
                    last.then_inc(z["done"], 1)
                    step.end()

            @block.tensor
            def _(pe):
                prime(pe, z["attended"])
                with pe.Fori(0, TILES) as t:
                    pe.wait_ge(z["x_here"], t + 1)
                    pe.wait_ge(z["dstep"], t * 3 + 1)
                    for j in range(8):
                        s, c, half = j // 4, (j // 2) % 2, j % 2
                        if j >= 2:
                            pe.wait_ge(z["maxed"], t * 8 + j - 1)
                        r = slice(s * SEQ, (s + 1) * SEQ)
                        for hh in range(2):
                            h = half * 4 + hh * 2
                            last = pe.matmul(pS[j % 2][:, hh * 2:hh * 2 + 2, :], xt[r, c * P:(c + 1) * P],
                                             kmask[r, h:h + 2, :], start=True, stop=True)
                        last.then_inc(z["scored"], 1)
                    pe.wait_ge(z["maxed"], t * 8 + 8)
                    for g in range(2 * KC):
                        last = pe.transpose(pM[:, g, :], mx[:, g, :], G.ident[:, :])
                    last.then_inc(z["m_turned"], 1)
                    pe.wait_ge(z["aug_ready"], t * 2 + 2)
                    pe.wait_ge(z["q_ready"], t * 2 + 2)
                    pe.wait_ge(z["k_ready"], t * 2 + 2)
                    for j in range(8):
                        s, c, half = j // 4, (j // 2) % 2, j % 2
                        if j >= 2:
                            pe.wait_ge(z["exped"], t * 8 + j - 1)
                        for hh in range(2):
                            h = half * 4 + hh * 2
                            last = pe.matmul(pS[j % 2][:, hh * 2:hh * 2 + 2, :], kaug[s][:, c * P:(c + 1) * P],
                                             qaug[s][:, h:h + 2, :], start=True, stop=True)
                        last.then_inc(z["shifted"], 1)
                    pe.wait_ge(z["exped"], t * 8 + 8)
                    pe.wait_ge(z["v_ready"], t * 4 + 4)
                    pe.wait_ge(z["done"], t + 1)
                    for s in range(2):
                        for c in range(KC):
                            for h in range(H):
                                last = pe.matmul(pO[:, s, :], vx[s][c][:, h * P:(h + 1) * P], prob[s][c][:, h, :],
                                                 start=(c == 0 and h == 0), stop=(c == KC - 1 and h == H - 1))
                    last.then_inc(z["attended"], 1)


MIXERS.update({"x1": rms_heads_attention, "a3": causal_attention, "x3": feature_attention})


def more_layouts(a, i):
    a["head_sum8"] = block_ones(8)
    a["of_head8"] = block_ones(1, P, 16, rw=8)
    a["of_head16"] = block_ones(1, P, 8, rw=16)
    both = np.concatenate([i["L1_xattn_Wk"], i["L1_xattn_Wv"]], axis=0)
    a["x1_wq"], a["x1_wk"], a["x1_wv"] = (feature_major(w) for w in (i["L1_xattn_Wq"], both[0::2], both[1::2]))
    pair = np.arange(256).reshape(-1, 2)[:, ::-1].reshape(-1)
    wq, bq, wk, bk = (i[f"L3_attn_{m}"] for m in ("Wq", "bq", "Wk", "bk"))
    for n, w in (("wq", wq), ("wqr", wq[pair]), ("wk", wk), ("wkr", wk[pair]), ("wv", i["L3_attn_Wv"]), ("wo", i["L3_attn_Wo"])):
        a[f"a3_{n}"] = feature_major(w)
    a["a3_bias"] = np.ascontiguousarray(np.stack([column(b) for b in (bq, bq[pair], bk, bk[pair])], axis=1))
    a["a3_bv"], a["a3_bo"] = i["L3_attn_bv"].reshape(1, D), i["L3_attn_bo"].reshape(1, D)
    inv = np.float32(10000.0) ** (-np.arange(0, 16, 2, dtype=np.float32) / 16)
    ang = np.arange(SEQ, dtype=np.float32)[None, :] * inv.astype(np.float32)[(np.arange(P) % 16) // 2][:, None]
    sign = np.where(np.arange(P) % 2 == 0, -1.0, 1.0).astype(np.float32)[:, None]
    a["a3_cos"], a["a3_sin"] = np.cos(ang).astype(np.float32), (np.sin(ang) * sign).astype(np.float32)
    pos = np.arange(P) % SEQ
    a["hide_later"] = np.where(np.arange(SEQ)[None, :] > pos[:, None], -1e30, 0.0).astype(np.float32)
    a["x3_of_head"] = (pos[:, None] // 8 == np.arange(8)[None, :]).astype(np.float32)
    m = np.zeros((SEQ + 8, 8), np.float32)
    m[SEQ:] = -np.eye(8, dtype=np.float32)
    a["x3_minus_head"] = m


def slot_attention(nc, G, tag, d):
    H, DK, DV, M = 16, 64, 128, 64
    HP = H // 2
    PROBS = TPB * 2
    EPS = 1e-5
    CLAMP = 32.0
    with Stage(nc, tag) as st:
        w = st.sb("w", [P, KC, 3 * P + 4 * P])
        wo = st.sb("wo", [P, 2, D])
        tri, qmask, gain = st.sb("tri", [P, P]), st.sb("qmask", [P, P]), st.sb("gain", [P, DV])
        load(nc, [(tri[:, :], d["causal_T"]), (qmask[:, :], d["causal_T_scaled"]),
                  (gain[:, :], d["a2_gain"].to_broadcast([P, DV]))], st.sem("loaded"))
        xt = st.sb("xt", [P, KC, BLK])
        qT, kT, esT = st.sb("qT", [P, BLK]), st.sb("kT", [P, BLK]), st.sb("esT", [P, BLK])
        es = st.sb("es", [P, TPB, P])
        v, gate = st.sb("v", [P, TPB, 2 * DV]), st.sb("gate", [P, TPB, 2 * DV])
        A, B = st.sb("A", [P, PROBS, P]), st.sb("B", [P, PROBS, P])
        rz, ok = st.sb("rz", [P, PROBS, M]), st.sb("ok", [P, PROBS, M])
        pzT, stat = st.sb("pzT", [P, TPB, P]), st.sb("stat", [P, PROBS])
        o, sq, oT = st.sb("o", [P, PROBS, DV]), st.sb("sq", [P, PROBS, DV]), st.sb("oT", [P, PROBS, P])
        b0, b1, b2, b3 = (st.ps(f"b{j}", [P, BLK]) for j in range(4))
        w0, w1 = st.ps("w0", [P, 2 * BLK]), st.ps("w1", [P, 2 * BLK])
        names = ("w_here", "copied", "projected", "qk_kept", "es_ready", "vg_made", "vg_kept", "es_turned", "es_kept", "a_made",
                 "a_ready", "ok_made", "shifted", "exped", "pz_ready", "pz_turned", "pz_kept", "b_made", "b_ready",
                 "o_made", "o_kept", "squared", "var_ready", "rooted", "o_ready", "o_turned", "ot_kept", "y_made", "done", "dstep",
                 "clipped")
        z = {m: st.sem(m) for m in names}
        w8 = lambda ap, n: ap.rearrange("p (j n) -> p j n", n=n)
        with nc.Block() as block:
            @block.sync
            def _(sp):
                with sp.Fori(0, HP) as hp:
                    sp.wait_ge(z["done"], hp * NBLK + 1)
                    sp.dma_start(w[:, :, :], d["a2_w"][dyn(hp, 1)].rearrange("o p k n -> (o p) k n")).then_inc(z["w_here"], 16)
                    sp.dma_start(wo[:, :, :], d["a2_wo"][dyn(hp, 1)].rearrange("o p k n -> (o p) k n")).then_inc(z["w_here"], 16)

            @block.scalar
            def _(act):
                with act.Fori(0, HP) as hp:
                    with act.Fori(0, NBLK) as b:
                        n = hp * NBLK + b
                        act.wait_ge(z["done"], n + 1)
                        act.copy(xt[:, :, :], G.xT[:, :, dyn(b, BLK)]).then_inc(z["copied"], 1)
                        act.wait_ge(z["projected"], n + 1)
                        act.copy(qT[:, :], b0[:, :])
                        act.copy(kT[:, :], b1[:, :]).then_inc(z["qk_kept"], 1)
                        act.wait_ge(z["clipped"], n + 1)
                        act.activation(esT[:, :], esT[:, :], ACT.Exp).then_inc(z["es_ready"], 1)
                        act.wait_ge(z["es_turned"], n + 1)
                        act.copy(es[:, :, :], w8(b2[:, :], P)).then_inc(z["es_kept"], 1)
                        act.wait_ge(z["shifted"], n + 1)
                        act.activation(ok[:, :, :], ok[:, :, :], ACT.Exp).then_inc(z["exped"], 1)
                        act.wait_ge(z["vg_made"], n + 1)
                        act.copy(v[:, :, :], w8(w0[:, :], 2 * DV))
                        act.activation(gate[:, :, :], w8(w1[:, :], 2 * DV), ACT.Silu).then_inc(z["vg_kept"], 1)
                        act.wait_ge(z["pz_turned"], n + 1)
                        act.copy(pzT[:, :, :], w8(b3[:, :], P)).then_inc(z["pz_kept"], 1)
                        act.wait_ge(z["o_made"], n + 1)
                        act.activation(sq[:, :, :], w8(w1[:, :], DV), ACT.Square).then_inc(z["squared"], 1)
                        act.wait_ge(z["var_ready"], n + 1)
                        act.activation(stat[:, :], stat[:, :], ACT.Sqrt).then_inc(z["rooted"], 1)
                        act.wait_ge(z["o_turned"], n + 1)
                        act.copy(oT[:, :, :], w8(w0[:, :], P)).then_inc(z["ot_kept"], 1)

            @block.vector
            def _(dve):
                prime(dve, z["done"])
                dve.memset(G.y[:, :, :], 0.0).then_inc(z["dstep"], 1)
                with dve.Fori(0, HP) as hp:
                    with dve.Fori(0, NBLK) as b:
                        n = hp * NBLK + b
                        step = Count(dve, z["dstep"], 10, n)
                        step.n = 1
                        dve.wait_ge(z["projected"], n + 1)
                        dve.tensor_scalar(esT[:, :], b2[:, :], CLAMP, -CLAMP, ALU.min, ALU.max).then_inc(z["clipped"], 1)
                        dve.wait_ge(z["a_made"], n + 1)
                        dve.tensor_tensor(A[:, :, :], w8(w0[:, :], P), rows(qmask[:, :], PROBS), ALU.mult).then_inc(z["a_ready"], 1)
                        dve.wait_ge(z["ok_made"], n + 1)
                        step(dve.reciprocal(rz[:, :, :], w8(b1[:, :], M)))
                        step(dve.tensor_tensor(ok[:, :, :], w8(b0[:, :], M), rz[:, :, :], ALU.mult))
                        step(dve.tensor_reduce(stat[:, :], ok[:, :, :], AX.X, ALU.max))
                        dve.tensor_tensor(ok[:, :, :], ok[:, :, :], cols(stat[:, :], M), ALU.subtract).then_inc(z["shifted"], 1)
                        dve.wait_ge(z["exped"], n + 1)
                        step(dve.tensor_reduce(stat[:, :], ok[:, :, :], AX.X, ALU.add))
                        step(dve.reciprocal(stat[:, :], stat[:, :]))
                        step(dve.tensor_tensor(ok[:, :, :], ok[:, :, :], rz[:, :, :], ALU.mult))
                        dve.tensor_tensor(ok[:, :, :], ok[:, :, :], cols(stat[:, :], M), ALU.mult).then_inc(z["pz_ready"], 1)
                        dve.wait_ge(z["b_made"], n + 1)
                        dve.tensor_tensor(B[:, :, :], w8(w0[:, :], P), rows(tri[:, :], PROBS), ALU.mult).then_inc(z["b_ready"], 1)
                        dve.wait_ge(z["squared"], n + 1)
                        step(dve.tensor_reduce(stat[:, :], sq[:, :, :], AX.X, ALU.add))
                        dve.tensor_scalar(stat[:, :], stat[:, :], 1.0 / DV, EPS, ALU.mult, ALU.add).then_inc(z["var_ready"], 1)
                        step(dve.tensor_tensor(o[:, :, :], w8(w1[:, :], DV), rows(gain[:, :], PROBS), ALU.mult))
                        o4 = o[:, :, :].rearrange("p (h t) e -> p h t e", h=2)
                        step(dve.tensor_tensor(o4, o4, gate[:, :, :].rearrange("p t (h e) -> p h t e", e=DV), ALU.mult))
                        dve.wait_ge(z["rooted"], n + 1)
                        step(dve.reciprocal(stat[:, :], stat[:, :]))
                        dve.tensor_tensor(o[:, :, :], o[:, :, :], cols(stat[:, :], DV), ALU.mult).then_inc(z["o_ready"], 1)
                        dve.wait_ge(z["y_made"], n + 1)
                        dve.tensor_tensor(G.y[:, dyn(b, TPB), :], G.y[:, dyn(b, TPB), :], w8(w1[:, :], D),
                                          ALU.add).then_inc(z["done"], 1)
                        step.n -= 1
                        step.end()

            @block.tensor
            def _(pe):
                with pe.Fori(0, HP) as hp:
                    with pe.Fori(0, NBLK) as b:
                        n = hp * NBLK + b
                        pe.wait_ge(z["w_here"], hp * 32 + 32)
                        pe.wait_ge(z["copied"], n + 1)
                        for j, out in enumerate((b0, b1, b2)):
                            for k in range(KC):
                                last = pe.matmul(out[:, :], w[:, k, j * P:(j + 1) * P], xt[:, k, :],
                                                 start=(k == 0), stop=(k == KC - 1))
                        last.then_inc(z["projected"], 1)
                        pe.wait_ge(z["qk_kept"], n + 1)
                        for t in range(TPB):
                            c = slice(t * P, (t + 1) * P)
                            for h in range(2):
                                r, j = slice(h * DK, (h + 1) * DK), h * TPB + t
                                last = pe.matmul(w0[:, j * P:(j + 1) * P], kT[r, c], qT[r, c], start=True, stop=True)
                        last.then_inc(z["a_made"], 1)
                        pe.wait_ge(z["es_ready"], n + 1)
                        for t in range(TPB):
                            last = pe.transpose(b2[:, t * P:(t + 1) * P], esT[:, t * P:(t + 1) * P], G.ident[:, :])
                        last.then_inc(z["es_turned"], 1)
                        pe.wait_ge(z["es_kept"], n + 1)
                        pe.wait_ge(z["a_ready"], n + 1)
                        for t in range(TPB):
                            for h in range(2):
                                j = 2 * t + h
                                pe.matmul(b0[:, j * M:(j + 1) * M], A[:, h * TPB + t, :], es[:, t, h * M:(h + 1) * M], start=True, stop=True)
                        pe.matmul(b1[:, :], tri[:, :], es[:, :, :], start=True, stop=True).then_inc(z["ok_made"], 1)
                        for t in range(TPB):
                            c = slice(t * P, (t + 1) * P)
                            for at, out in ((3 * P, w0), (5 * P, w1)):
                                for k in range(KC):
                                    last = pe.matmul(out[:, t * 2 * DV:(t + 1) * 2 * DV], xt[:, k, c], w[:, k, at:at + 2 * DV],
                                                     start=(k == 0), stop=(k == KC - 1))
                        last.then_inc(z["vg_made"], 1)
                        pe.wait_ge(z["pz_ready"], n + 1)
                        for t in range(TPB):
                            last = pe.transpose(b3[:, t * P:(t + 1) * P], ok[:, 2 * t:2 * t + 2, :], G.ident[:, :])
                        last.then_inc(z["pz_turned"], 1)
                        pe.wait_ge(z["pz_kept"], n + 1)
                        pe.wait_ge(z["vg_kept"], n + 1)
                        for t in range(TPB):
                            c = slice(t * P, (t + 1) * P)
                            for h in range(2):
                                r, j = slice(h * M, (h + 1) * M), h * TPB + t
                                last = pe.matmul(w0[:, j * P:(j + 1) * P], esT[r, c], pzT[r, t, :], start=True, stop=True)
                        last.then_inc(z["b_made"], 1)
                        pe.wait_ge(z["b_ready"], n + 1)
                        for j in range(PROBS):
                            last = pe.matmul(w1[:, j * DV:(j + 1) * DV], B[:, j, :], v[:, j % TPB, (j // TPB) * DV:(j // TPB + 1) * DV],
                                             start=True, stop=True)
                        last.then_inc(z["o_made"], 1)
                        pe.wait_ge(z["o_ready"], n + 1)
                        for j in range(PROBS):
                            last = pe.transpose(w0[:, j * P:(j + 1) * P], o[:, j, :], G.ident[:, :])
                        last.then_inc(z["o_turned"], 1)
                        pe.wait_ge(z["ot_kept"], n + 1)
                        for t in range(TPB):
                            for h in range(2):
                                last = pe.matmul(w1[:, t * D:(t + 1) * D], oT[:, h * TPB + t, :], wo[:, h, :],
                                                 start=(h == 0), stop=(h == 1))
                        last.then_inc(z["y_made"], 1)


def slot_layouts(a, i):
    HP, DV = 8, 128
    W = {m: i[f"L2_attn_W{m}"] for m in "qkvgs"}
    cut = lambda m: np.transpose(W[m].reshape(KC, P, HP, -1), (2, 1, 0, 3))
    a["a2_w"] = np.ascontiguousarray(np.concatenate([cut(m) for m in "qksvg"], axis=3))
    a["a2_wo"] = np.ascontiguousarray(np.transpose(i["L2_attn_Wo"].reshape(HP, 2, DV, D), (0, 2, 1, 3)))
    a["a2_gain"] = i["L2_attn_g_norm_weight"].reshape(1, DV)
    j, t = np.arange(P)[:, None], np.arange(P)[None, :]
    a["causal_T"] = ((j <= t) & (j // SEQ == t // SEQ)).astype(np.float32)
    a["causal_T_scaled"] = a["causal_T"] * np.float32(0.125)


MIXERS["a2"] = slot_attention


def delta_gates(nc, G, tag, d, g_all, b_all):
    NV = 32
    with Stage(nc, tag + "g") as st:
        w, ba = st.sb("w", [P, KC, 2 * NV]), st.sb("ba", [P, TILES, 2 * NV])
        dt, a_log = st.sb("dt", [P, NV]), st.sb("a_log", [P, NV])
        x, e, u, ln = (st.sb(m, [P, TILES, NV]) for m in ("x", "e", "u", "ln"))
        load(nc, [(w[:, :, :], d["a1_w_ba"]), (dt[:, :], d["a1_dt"].to_broadcast([P, NV])),
                  (a_log[:, :], d["a1_a_log"].to_broadcast([P, NV]))], st.sem("loaded"))
        tile_logits(nc, G, st, w, 2 * NV, ba)
        dstep, sized, exped, summed, logged, beta = (st.sem(m) for m in ("dstep", "sized", "exped", "summed", "logged", "beta"))
        by_pass = lambda ap: ap[:, :, :].rearrange("p (k b) (t h) -> p (b t) k h", k=16, h=2)
        by_head = lambda ap: ap.rearrange("p t (k h) -> p t k h", h=2)
        with nc.Block() as block:
            @block.vector
            def _(dve):
                step = Count(dve, dstep)
                step(dve.tensor_tensor(x[:, :, :], ba[:, :, NV:2 * NV], rows(dt[:, :], TILES), ALU.add))
                dve.scalar_tensor_tensor(e[:, :, :], x[:, :, :], -1.0, x[:, :, :], ALU.mult, ALU.max).then_inc(sized, 1)
                dve.wait_ge(exped, 1)
                dve.tensor_scalar(u[:, :, :], e[:, :, :], 1.0, None, ALU.add).then_inc(summed, 1)
                dve.wait_ge(summed, 1)
                step(dve.scalar_tensor_tensor(e[:, :, :], u[:, :, :], -1.0, e[:, :, :], ALU.add, ALU.subtract))
                dve.wait_ge(logged, 1)
                step(dve.reciprocal(u[:, :, :], u[:, :, :]))
                step(dve.tensor_tensor(e[:, :, :], e[:, :, :], u[:, :, :], ALU.mult))
                step(dve.tensor_tensor(ln[:, :, :], ln[:, :, :], e[:, :, :], ALU.subtract))
                step(dve.scalar_tensor_tensor(x[:, :, :], x[:, :, :], 0.0, ln[:, :, :], ALU.max, ALU.add))
                step(dve.tensor_scalar(a_log[:, :], a_log[:, :], -1.0, None, ALU.mult))
                step(dve.tensor_tensor(x[:, :, :], x[:, :, :], rows(a_log[:, :], TILES), ALU.mult))
                dve.wait_ge(beta, 1)
                step(dve.tensor_copy(by_pass(g_all), by_head(x[:, :, :])))
                step(dve.tensor_copy(by_pass(b_all), by_head(ba[:, :, 0:NV])))

            @block.scalar
            def _(act):
                act.wait_ge(sized, 1)
                act.activation(e[:, :, :], e[:, :, :], ACT.Exp, scale=-1.0)
                act.activation(a_log[:, :], a_log[:, :], ACT.Exp).then_inc(exped, 1)
                act.wait_ge(summed, 1)
                act.activation(ln[:, :, :], u[:, :, :], ACT.Ln).then_inc(logged, 1)
                act.activation(ba[:, :, 0:NV], ba[:, :, 0:NV], ACT.Sigmoid).then_inc(beta, 1)


def gated_delta(nc, G, tag, d):
    NK, DK, DV, TAPS = 16, 128, 128, 4
    PROBS, SEQS, PAD = 2 * TPB, BLK // SEQ, TAPS - 1
    PASSES = NK * NBLK
    LEVELS = 6
    RL = LEVELS - 1
    EPS = 1e-6
    FRONT_STEPS, BACK_STEPS = 10, 4
    with Stage(nc, tag) as st:
        g_all, b_all = st.sb("g_all", [P, PASSES, PROBS]), st.sb("b_all", [P, PASSES, PROBS])
        delta_gates(nc, G, tag, d, g_all, b_all)
        w, wo, cw = st.sb("w", [P, KC, 6 * P]), st.sb("wo", [P, 2, D]), st.sb("cw", [P, 4, TAPS])
        gain, one = st.sb("gain", [P, DV]), st.sb("one", [P, 1])
        eye, upto, after = st.sb("eye", [P, SEQ]), st.sb("upto", [P, SEQ]), st.sb("after", [P, SEQ])
        strict, incl, level = st.sb("strict", [P, SEQ]), st.sb("incl", [P, SEQ]), st.sb("level", [P, LEVELS, SEQ])
        load(nc, [(gain[:, :], d["a1_gain"].to_broadcast([P, DV])), (one[:, :], d["ones_col"]), (eye[:, :], d["eye64"]),
                  (upto[:, :], d["upto64"]), (after[:, :], d["after64"]), (strict[:, :], d["strict64"]),
                  (incl[:, :], d["incl64_scaled"]), (level[:, :, :], d["level64"])], st.sem("loaded"))
        xt = st.sb("xt", [P, KC, BLK])
        pre, conv = st.sb("pre", [P, 4, SEQS, SEQ + PAD]), st.sb("conv", [P, 4, BLK])
        sq = st.sb("sq", [P, 2, BLK])
        V, U, zs = st.sb("V", [P, PROBS, DV]), st.sb("U", [P, PROBS, DV]), st.sb("zs", [P, PROBS, DV])
        gt, E = st.sb("gt", [P, PROBS, SEQ]), st.sb("E", [P, PROBS, SEQ])
        kk, kq = st.sb("kk", [P, TPB, SEQ]), st.sb("kq", [P, TPB, SEQ])
        N, A = st.sb("N", [P, PROBS, SEQ]), st.sb("A", [P, PROBS, SEQ])
        C = st.sb("C", [P, LEVELS, PROBS, SEQ])
        R, RT, Y = st.sb("R", [P, PROBS, SEQ]), st.sb("RT", [P, PROBS, SEQ]), st.sb("Y", [P, PROBS, SEQ])
        og, sq2, oT = st.sb("og", [P, PROBS, DV]), st.sb("sq2", [P, PROBS, DV]), st.sb("oT", [P, PROBS, P])
        ss, rt = st.sb("ss", [P, 2, PROBS]), st.sb("rt", [P, 2, PROBS])
        stat, bk = st.sb("stat", [P, PROBS]), st.sb("bk", [P, PROBS])
        f = [st.ps(f"f{j}", [P, BLK]) for j in range(2)]
        pn, pY = st.ps("pn", [P, PROBS]), st.ps("pY", [P, BLK])
        w0, w1 = st.ps("w0", [P, 2 * BLK]), st.ps("w1", [P, 2 * BLK])
        pR, pRT = w1[:, 0:BLK], w1[:, BLK:2 * BLK]
        names = ("w_here", "cw_here", "wo_here", "copied", "projected", "pre_kept", "convolved", "silued", "squared_qk",
                 "normed", "inverted", "rooted_qk", "z_made", "z_kept", "v_turned", "v_kept", "gt_ready", "decayed", "exped",
                 "kq_made", "n_ready", "c0_ready", "c_ready", "c_turned", "r_ready", "t_made", "t_kept", "step_made",
                 "w_made", "u_kept", "o_made", "og_made", "squared", "var_ready", "rooted", "og_ready", "o_turned",
                 "ot_kept", "y_made", "done", "front_step", "back_step", "set_up")
        z = {m: st.sem(m) for m in names}
        v3 = lambda ap, n: ap.rearrange("p (j n) -> p j n", n=n)
        half = [slice(0, SEQ), slice(SEQ, P)]
        c64 = lambda j: slice(j * SEQ, (j + 1) * SEQ)

        def passes(eng, front_only, body):
            front_only()
            with eng.Fori(0, PASSES - 1) as n:
                body(n, n + 1)
            body(PASSES - 1, None)

        with nc.Block() as block:
            @block.sync
            def _(sp):
                def fetch(kh):
                    sp.wait_ge(z["z_made"], kh * NBLK + 1)
                    sp.dma_start(w[:, :, :], d["a1_w"][dyn(kh, 1)].rearrange("o p k n -> (o p) k n")).then_inc(z["w_here"], 16)
                    sp.wait_ge(z["convolved"], kh * NBLK + 1)
                    sp.dma_start(cw[:, :, :], d["a1_cw"][dyn(kh, 1)].rearrange("o p k n -> (o p) k n")).then_inc(z["cw_here"], 16)
                    sp.wait_ge(z["y_made"], kh * NBLK + 1)
                    sp.dma_start(wo[:, :, :], d["a1_wo"][dyn(kh, 1)].rearrange("o p k n -> (o p) k n")).then_inc(z["wo_here"], 16)

                with sp.Fori(0, NK) as kh:
                    fetch(kh)

            @block.gpsimd
            def _(pool):
                with pool.Fori(0, PASSES) as n:
                    pool.wait_ge(z["n_ready"], n + 1)
                    for l in range(1, LEVELS):
                        pool.tensor_tensor(C[:, l, :, :], N[:, :, :], rows(level[:, l, :], PROBS),
                                           ALU.mult).then_inc(z["c_ready"], 1)

            @block.scalar
            def _(act):
                def keep_pre(m, j):
                    act.wait_ge(z["projected"], m * 4 + j + 1)
                    act.copy(pre[:, j, :, PAD:], v3(f[j % 2][:, :], SEQ)).then_inc(z["pre_kept"], 1)

                def copy_x(m):
                    act.wait_ge(z["z_made"], m + 1)
                    act.wait_ge(z["convolved"], m + 1)
                    act.copy(xt[:, :, :], G.xT[:, :, dyn(m % NBLK, BLK)]).then_inc(z["copied"], 1)

                def decay(m):
                    act.wait_ge(z["decayed"], m + 1)
                    act.activation(E[:, :, :], v3(f[0][:, :], SEQ), ACT.Exp).then_inc(z["exped"], 1)

                def silu_conv(m):
                    act.wait_ge(z["convolved"], m + 2)
                    act.activation(conv[:, :, :], conv[:, :, :], ACT.Silu).then_inc(z["silued"], 1)
                    act.wait_ge(z["silued"], m + 1)
                    act.activation(sq[:, :, :], conv[:, 0:2, :], ACT.Square).then_inc(z["squared_qk"], 1)

                def silu_z(m):
                    act.wait_ge(z["z_made"], m + 2)
                    act.activation(zs[:, :, :], v3(w1[:, :], DV), ACT.Silu).then_inc(z["z_kept"], 1)

                def root_norms(m):
                    act.wait_ge(z["inverted"], m + 1)
                    act.activation(rt[:, :, :], ss[:, :, :], ACT.Sqrt).then_inc(z["rooted_qk"], 1)

                def keep_v(m):
                    act.wait_ge(z["rooted_qk"], m + 1)
                    act.wait_ge(z["v_turned"], m + 1)
                    for t in range(TPB):
                        last = act.activation(V[:, 2 * t:2 * t + 2, :], v3(w0[:, t * D:(t + 1) * D], DV), ACT.Copy,
                                              scale=rt[:, 0, TPB + t:TPB + t + 1])
                    last.then_inc(z["v_kept"], 1)

                def front_only():
                    copy_x(0)
                    for j in range(4):
                        keep_pre(0, j)
                    decay(0)
                    silu_conv(0)
                    silu_z(0)
                    root_norms(0)
                    keep_v(0)

                def body(n, m):
                    f_ = m is not None
                    if f_:
                        copy_x(m)
                        keep_pre(m, 0)
                        keep_pre(m, 1)
                    for l in range(1, LEVELS):
                        act.wait_ge(z["t_made"], n * RL + l)
                        act.copy(Y[:, :, :], v3(pY[:, :], SEQ)).then_inc(z["t_kept"], 1)
                        if f_ and l == 1:
                            keep_pre(m, 2)
                            keep_pre(m, 3)
                        if f_ and l == 2:
                            decay(m)
                        if f_ and l == 4:
                            silu_conv(m)
                    act.wait_ge(z["w_made"], n + 1)
                    act.copy(U[:, :, :], v3(w0[:, :], DV)).then_inc(z["u_kept"], 1)
                    act.wait_ge(z["og_made"], n + 1)
                    act.activation(sq2[:, :, :], og[:, :, :], ACT.Square).then_inc(z["squared"], 1)
                    if f_:
                        silu_z(m)
                    act.wait_ge(z["var_ready"], n + 1)
                    act.activation(stat[:, :], stat[:, :], ACT.Sqrt).then_inc(z["rooted"], 1)
                    act.wait_ge(z["o_turned"], n + 1)
                    act.copy(oT[:, :, :], v3(w0[:, :], P)).then_inc(z["ot_kept"], 1)
                    if f_:
                        root_norms(m)
                        keep_v(m)

                passes(act, front_only, body)

            @block.vector
            def _(dve):
                prime(dve, z["done"], z["convolved"])
                step0 = Count(dve, z["set_up"])
                step0(dve.memset(pre[:, :, :, 0:PAD], 0.0))
                step0(dve.memset(G.y[:, :, :], 0.0))

                def of_pass(x, m):
                    return x[:, dyn(m, 1), :].rearrange("p o (j e) -> p (o j) e", e=1).to_broadcast([P, PROBS, SEQ])

                def gates(m):
                    if not isinstance(m, int):
                        dve.wait_ge(z["decayed"], m)
                    dve.tensor_tensor(gt[:, :, :], of_pass(g_all, m), rows(upto[:, :], PROBS), ALU.mult).then_inc(z["gt_ready"], 1)

                def convolve(m, step, pair, tap):
                    if pair == 0 and tap == 0:
                        dve.wait_ge(z["cw_here"], (m // NBLK) * 16 + 16)
                    if tap == 0:
                        dve.wait_ge(z["pre_kept"], m * 4 + 2 * pair + 2)
                    for j in (2 * pair, 2 * pair + 1):
                        out = v3(conv[:, j, :], SEQ)
                        src, scale = pre[:, j, :, tap:tap + SEQ], cw[:, j, tap:tap + 1]
                        if tap == 0:
                            last = dve.tensor_scalar(out, src, scale, None, ALU.mult)
                        else:
                            last = dve.scalar_tensor_tensor(out, src, scale, out, ALU.mult, ALU.add)
                    if pair == 1 and tap == TAPS - 1:
                        last.then_inc(z["convolved"], 1)
                    else:
                        step(last)

                def norms(m, step):
                    dve.wait_ge(z["normed"], m + 1)
                    step(dve.tensor_scalar(ss[:, 0, :], pn[:, :], EPS, None, ALU.add))
                    dve.reciprocal(ss[:, 1, :], ss[:, 0, :]).then_inc(z["inverted"], 1)
                    dve.wait_ge(z["inverted"], m + 1)
                    step(dve.tensor_tensor(v3(bk[:, :], 2), b_all[:, dyn(m, 1), :].rearrange("p o (t h) -> p (o t) h", h=2),
                                           cols(ss[:, 1, TPB:PROBS], 2), ALU.mult))
                    dve.wait_ge(z["exped"], m + 1)
                    dve.tensor_tensor(E[:, :, :], E[:, :, :], cols(bk[:, :], SEQ), ALU.mult)
                    dve.wait_ge(z["kq_made"], m + 1)
                    b4 = f[1][:, :].rearrange("p (w t m) -> p w t m", w=2, m=SEQ)
                    dve.tensor_tensor(kq[:, :, :], b4[:, 0], rows(incl[:, :], TPB), ALU.mult)
                    step(dve.tensor_tensor(kk[:, :, :], b4[:, 1], rows(strict[:, :], TPB), ALU.mult))

                def matrices(m):
                    full = [P, TPB, 2, SEQ]
                    four = lambda ap: ap[:, :, :].rearrange("p (t h) m -> p t h m", h=2)
                    both = lambda ap: ap[:, :, :].rearrange("p t (o m) -> p t o m", o=1).to_broadcast(full)
                    dve.tensor_tensor(four(N), four(E), both(kk), ALU.mult).then_inc(z["n_ready"], 1)
                    dve.wait_ge(z["n_ready"], m + 1)
                    dve.tensor_tensor(C[:, 0, :, :], N[:, :, :], rows(level[:, 0, :], PROBS), ALU.mult).then_inc(z["c0_ready"], 1)
                    dve.tensor_tensor(four(A), four(E), both(kq), ALU.mult)
                    dve.wait_ge(z["c0_ready"], m + 1)
                    dve.tensor_tensor(R[:, :, :], rows(eye[:, :], PROBS), C[:, 0, :, :], ALU.subtract)

                def front_only():
                    step = Count(dve, z["front_step"], FRONT_STEPS, 0)
                    gates(0)
                    for pair in range(2):
                        for tap in range(TAPS):
                            convolve(0, step, pair, tap)
                    norms(0, step)
                    matrices(0)

                def body(n, m):
                    f_ = m is not None
                    step = Count(dve, z["front_step"], FRONT_STEPS, m) if f_ else None
                    back = Count(dve, z["back_step"], BACK_STEPS, n)
                    dve.wait_ge(z["c_turned"], n + 1)
                    dve.tensor_tensor(RT[:, :, :], rows(eye[:, :], PROBS), v3(pY[:, :], SEQ), ALU.subtract).then_inc(z["r_ready"], 1)
                    if f_:
                        gates(m)
                    for l in range(1, LEVELS):
                        if f_ and l == 2:
                            convolve(m, step, 0, 0)
                            convolve(m, step, 0, 1)
                        if f_ and l == 3:
                            convolve(m, step, 0, 2)
                            convolve(m, step, 0, 3)
                        if f_ and l == 4:
                            convolve(m, step, 1, 0)
                            convolve(m, step, 1, 1)
                            convolve(m, step, 1, 2)
                            convolve(m, step, 1, 3)
                        dve.wait_ge(z["step_made"], n * RL + l)
                        last = dve.tensor_tensor(R[:, :, :], R[:, :, :], v3(pR, SEQ), ALU.subtract)
                        if l < RL:
                            last = dve.tensor_tensor(RT[:, :, :], RT[:, :, :], v3(pRT, SEQ), ALU.subtract)
                        last.then_inc(z["r_ready"], 1)
                    dve.wait_ge(z["o_made"], n + 1)
                    dve.tensor_tensor(og[:, :, :], v3(w1[:, :], DV), zs[:, :, :], ALU.mult).then_inc(z["og_made"], 1)
                    dve.wait_ge(z["squared"], n + 1)
                    by_tile = v3(stat[:, :], 2)
                    back(dve.tensor_reduce(stat[:, :], sq2[:, :, :], AX.X, ALU.add))
                    back(dve.tensor_tensor(by_tile, by_tile, cols(ss[:, 1, 0:TPB], 2), ALU.mult))
                    dve.tensor_scalar(stat[:, :], stat[:, :], 1.0 / DV, EPS, ALU.mult, ALU.add).then_inc(z["var_ready"], 1)
                    dve.tensor_tensor(og[:, :, :], og[:, :, :], rows(gain[:, :], PROBS), ALU.mult)
                    dve.wait_ge(z["rooted"], n + 1)
                    back(dve.reciprocal(stat[:, :], stat[:, :]))
                    back(dve.tensor_tensor(by_tile, by_tile, cols(rt[:, 1, 0:TPB], 2), ALU.mult))
                    dve.tensor_tensor(og[:, :, :], og[:, :, :], cols(stat[:, :], DV), ALU.mult).then_inc(z["og_ready"], 1)
                    back.end()
                    if f_:
                        norms(m, step)
                        matrices(m)
                        step.end()
                    dve.wait_ge(z["y_made"], n + 2)
                    y = G.y[:, dyn(n % NBLK, TPB), :]
                    dve.tensor_tensor(y, y, v3(w1[:, :], D), ALU.add).then_inc(z["done"], 1)

                passes(dve, front_only, body)

            @block.tensor
            def _(pe):
                def each(out, lhsT, rhs):
                    for j in range(PROBS):
                        for r in half:
                            last = pe.matmul(out(j, r), lhsT(j, r), rhs(j, r), start=True, stop=True)
                    return last

                bank = lambda b: lambda j, r: b[r, c64(j)]
                of = lambda x: lambda j, r: x[r, j, :]

                def project(m, j):
                    if j == 0:
                        pe.wait_ge(z["w_here"], (m // NBLK) * 16 + 16)
                        pe.wait_ge(z["copied"], m + 1)
                    if j >= 2:
                        pe.wait_ge(z["pre_kept"], m * 4 + j - 1)
                    for k in range(KC):
                        last = pe.matmul(f[j % 2][:, :], w[:, k, j * P:(j + 1) * P], xt[:, k, :],
                                         start=(k == 0), stop=(k == KC - 1))
                    last.then_inc(z["projected"], 1)

                def decay_sums(m):
                    pe.wait_ge(z["pre_kept"], m * 4 + 3)
                    hold(pe, G, z["gt_ready"], m + 1, f[0][:, 0:1])
                    for r in half:
                        last = pe.matmul(f[0][r, :], after[r, :], gt[r, :, :], start=True, stop=True)
                    last.then_inc(z["decayed"], 1)

                def norm_sums(m):
                    pe.wait_ge(z["squared_qk"], m + 1)
                    for j in range(2):
                        for t in range(TPB):
                            last = pe.matmul(pn[:, j * TPB + t:j * TPB + t + 1], sq[:, j, t * P:(t + 1) * P], one[:, :],
                                             start=True, stop=True)
                    last.then_inc(z["normed"], 1)

                def key_products(m):
                    pe.wait_ge(z["pre_kept"], m * 4 + 4)
                    b4 = f[1][:, :].rearrange("p (w t m) -> p w t m", w=2, m=SEQ)
                    for t in range(TPB):
                        for s, r in enumerate(half):
                            c = c64(2 * t + s)
                            last = pe.matmul(b4[r, :, t, :], conv[:, 1, c], conv[:, 0:2, c], start=True, stop=True)
                    last.then_inc(z["kq_made"], 1)

                def project_z(m):
                    for t in range(TPB):
                        for k in range(KC):
                            last = pe.matmul(w1[:, t * D:(t + 1) * D], xt[:, k, t * P:(t + 1) * P], w[:, k, 4 * P:6 * P],
                                             start=(k == 0), stop=(k == KC - 1))
                    last.then_inc(z["z_made"], 1)

                def turn_v(m):
                    for t in range(TPB):
                        for h in range(2):
                            j = 2 * t + h
                            last = pe.transpose(w0[:, j * P:(j + 1) * P], conv[:, 2 + h, t * P:(t + 1) * P], G.ident[:, :])
                    last.then_inc(z["v_turned"], 1)

                def front_only():
                    prime(pe, z["z_made"], z["y_made"])
                    for j in range(4):
                        project(0, j)
                    decay_sums(0)
                    norm_sums(0)
                    key_products(0)
                    project_z(0)
                    turn_v(0)

                def body(n, m):
                    f_ = m is not None
                    hold(pe, G, z["c0_ready"], n + 1, pY[:, 0:1])
                    each(bank(pY), lambda j, r: C[r, 0, j, :], lambda j, r: eye[r, :]).then_inc(z["c_turned"], 1)
                    if f_:
                        project(m, 0)
                        project(m, 1)
                    pe.wait_ge(z["z_kept"], n + 1)
                    pe.wait_ge(z["done"], n + 1)
                    for l in range(1, LEVELS):
                        pe.wait_ge(z["c_ready"], n * RL + l)
                        hold(pe, G, z["r_ready"], n * LEVELS + l, pY[:, 0:1])
                        each(bank(pY), lambda j, r: C[r, l, j, :], of(RT)).then_inc(z["t_made"], 1)
                        if f_ and l in (1, 2):
                            project(m, l + 1)
                        if f_ and l == 3:
                            decay_sums(m)
                        hold(pe, G, z["t_kept"], n * RL + l, pR[:, 0:1])
                        last = each(bank(pR), of(Y), of(R))
                        if l < RL:
                            last = each(bank(pRT), of(R), of(Y))
                        last.then_inc(z["step_made"], 1)
                    pe.wait_ge(z["v_kept"], n + 1)
                    hold(pe, G, z["r_ready"], n * LEVELS + LEVELS, w0[:, 0:1])
                    each(lambda j, r: w0[r, j * DV:(j + 1) * DV], of(R), of(V)).then_inc(z["w_made"], 1)
                    if f_:
                        norm_sums(m)
                    hold(pe, G, z["u_kept"], n + 1, w1[:, 0:1])
                    each(lambda j, r: w1[r, j * DV:(j + 1) * DV], of(A), of(U)).then_inc(z["o_made"], 1)
                    if f_:
                        key_products(m)
                        pe.wait_ge(z["og_made"], n + 1)
                        project_z(m)
                    pe.wait_ge(z["og_ready"], n + 1)
                    for j in range(PROBS):
                        last = pe.transpose(w0[:, j * P:(j + 1) * P], og[:, j, :], G.ident[:, :])
                    last.then_inc(z["o_turned"], 1)
                    if f_:
                        pe.wait_ge(z["z_kept"], m + 1)
                    pe.wait_ge(z["wo_here"], (n // NBLK) * 16 + 16)
                    pe.wait_ge(z["ot_kept"], n + 1)
                    for t in range(TPB):
                        for h in range(2):
                            last = pe.matmul(w1[:, t * D:(t + 1) * D], oT[:, 2 * t + h, :], wo[:, h, :],
                                             start=(h == 0), stop=(h == 1))
                    last.then_inc(z["y_made"], 1)
                    if f_:
                        turn_v(m)

                passes(pe, front_only, body)


def delta_layouts(a, i):
    NK = 16
    w = i["L1_attn_W_qkvz"].reshape(KC, P, NK, 6 * P)
    a["a1_w"] = np.ascontiguousarray(np.transpose(w, (2, 1, 0, 3)))
    a["a1_wo"] = np.ascontiguousarray(np.transpose(i["L1_attn_W_out"].reshape(NK, 2, P, D), (0, 2, 1, 3)))
    cw = i["L1_attn_conv_w"]
    qk = cw[:2 * NK * P].reshape(2, NK, P, 4)
    v = cw[2 * NK * P:].reshape(NK, 2, P, 4)
    a["a1_cw"] = np.ascontiguousarray(np.concatenate([np.transpose(qk, (1, 2, 0, 3)), np.transpose(v, (0, 2, 1, 3))], axis=2))
    ba = i["L1_attn_W_ba"].reshape(D, NK, 2, 2)
    a["a1_w_ba"] = in_rows(np.transpose(ba, (0, 2, 1, 3)).reshape(D, 64))
    a["a1_dt"], a["a1_a_log"] = i["L1_attn_dt_bias"].reshape(1, 32), i["L1_attn_A_log"].reshape(1, 32)
    a["a1_gain"] = i["L1_attn_norm_weight"].reshape(1, P)
    r, c = np.arange(P)[:, None] % SEQ, np.arange(SEQ)[None, :]
    f = lambda m: m.astype(np.float32)
    a["eye64"], a["upto64"], a["after64"], a["strict64"] = f(r == c), f(r <= c), f(r > c), f(r < c)
    a["incl64_scaled"] = f(r <= c) * np.float32(P ** -0.5)
    a["level64"] = np.ascontiguousarray(np.stack(
        [f((r >> (l + 1) == c >> (l + 1)) & (r >> l < c >> l)) for l in range(6)], axis=1))


MIXERS["a1"] = gated_delta


class Globals:
    pass


STAGES = ["a0", "x0", "f0", "a1", "x1", "f1", "a2", "x2", "f2", "a3", "x3", "f3"]


def decoder(nc, d, out):
    G = Globals()
    with Stage(nc, "g") as st:
        G.x_tok, G.y = st.sb("x_tok", [P, TILES, D]), st.sb("y", [P, TILES, D])
        G.xT = st.sb("xT", [P, KC, NTOK])
        G.ident, G.zero = st.sb("ident", [P, P]), st.sb("zero", [P, BLK])
        load(nc, [(G.x_tok[:, :, :], d["x_tok"]), (G.xT[:, :, :], d["xT"]), (G.ident[:, :], d["ident"]),
                  (G.zero[:, :], d["zero"])], st.sem("loaded"))
        for tag in STAGES:
            if tag in EXPERTS:
                gated_experts(nc, G, tag, d)
            else:
                MIXERS[tag](nc, G, tag, d)
            residual_norm(nc, G, tag)
        stored = st.sem("stored")
        with nc.Block() as block:
            @block.sync
            def _(sp):
                sp.dma_start(out, G.x_tok[:, :, :]).then_inc(stored, 16)
                sp.wait_ge(stored, 16)


def feature_major(w):
    return np.ascontiguousarray(np.transpose(w.reshape(w.shape[0], -1, P), (2, 1, 0)))


def in_rows(w):
    return np.ascontiguousarray(np.transpose(w.reshape(-1, P, w.shape[1]), (1, 0, 2)))


def pad_cols(w, n):
    return np.concatenate([w, np.zeros((w.shape[0], n - w.shape[1]), w.dtype)], axis=1)


def pack_experts(gate, up, down, owner):
    F = gate.shape[1]
    FT = -(-F // P)
    parts = []
    for w in (gate, up):
        w = pad_cols(w, FT * P).reshape(KC, P, FT, P)
        parts.append(np.transpose(w, (2, 1, 0, 3)))
    sel = np.zeros((P, FT * P), np.float32)
    sel[owner, np.arange(F)] = 1.0
    parts.append(np.transpose(sel.reshape(P, FT, 1, P), (1, 0, 2, 3)))
    down = np.concatenate([down, np.zeros((FT * P - F, D), down.dtype)], axis=0).reshape(FT, P, D)
    return np.ascontiguousarray(np.concatenate(parts, axis=2)), np.ascontiguousarray(down)


def owners(E, width, shared):
    return np.concatenate([np.repeat(np.arange(E), width), np.full(shared, E)])


def layouts(i):
    a = {}
    x = i["x"].reshape(TILES, P, D)
    a["x_tok"] = np.ascontiguousarray(np.transpose(x, (1, 0, 2)))
    a["xT"] = feature_major(i["x"].reshape(NTOK, D))
    a["ctx_tok"] = np.ascontiguousarray(np.transpose(i["ctx_2048"].reshape(TILES, P, D), (1, 0, 2)))
    a["ctxT"] = feature_major(i["ctx_2048"].reshape(NTOK, D))
    a["ident"] = np.eye(P, dtype=np.float32)
    a["zero"] = np.zeros((P, BLK), np.float32)
    for E in (4, 8, 16):
        a[f"before{E}"] = np.ascontiguousarray(np.broadcast_to(np.tri(E, k=-1, dtype=np.float32), (P, E, E)))
    I = 176
    gu = np.transpose(i["L0_ffn_w_gate_up"], (1, 0, 2))
    sh = i["L0_ffn_shared_gate_up"]
    a["f0_in_w"], a["f0_out_w"] = pack_experts(
        np.concatenate([gu[:, :, :I].reshape(D, -1), sh[:, :2 * I]], axis=1),
        np.concatenate([gu[:, :, I:].reshape(D, -1), sh[:, 2 * I:]], axis=1),
        np.concatenate([i["L0_ffn_w_down"].reshape(-1, D), i["L0_ffn_shared_down"]], axis=0), owners(16, I, 2 * I))
    a["f0_gate"] = feature_major(i["L0_ffn_gate_w"])
    gu = np.transpose(i["L2_ffn_gu_w"], (2, 0, 1))
    a["f2_in_w"], a["f2_out_w"] = pack_experts(
        np.concatenate([gu[:, :, :64].reshape(D, -1), i["L2_ffn_sh_gate_w"].T], axis=1),
        np.concatenate([gu[:, :, 64:].reshape(D, -1), i["L2_ffn_sh_up_w"].T], axis=1),
        np.concatenate([np.transpose(i["L2_ffn_dp_w"], (0, 2, 1)).reshape(-1, D), i["L2_ffn_sh_down_w"].T], axis=0),
        owners(64, 64, 64))
    a["f2_gate"] = feature_major(np.concatenate([i["L2_ffn_gate_w"], i["L2_ffn_sh_gate1_w"]], axis=0))
    a["f3_in_w"], a["f3_out_w"] = pack_experts(
        np.concatenate([np.transpose(i["L3_ffn_We_gate"], (1, 0, 2)).reshape(D, -1), i["L3_ffn_Ws_gate"]], axis=1),
        np.concatenate([np.transpose(i["L3_ffn_We_up"], (1, 0, 2)).reshape(D, -1), i["L3_ffn_Ws_up"]], axis=1),
        np.concatenate([i["L3_ffn_We_down"].reshape(-1, D), i["L3_ffn_Ws_down"]], axis=0), owners(8, I, 2 * I))
    a["f3_gate"] = in_rows(i["L3_ffn_W_router"])
    mixer_layouts(a, i)
    more_layouts(a, i)
    slot_layouts(a, i)
    delta_layouts(a, i)
    return a


def kernel(**inputs):
    import concourse.bacc as _bacc
    from concourse.bass_utils import run_bass_kernel_spmd as _run

    arrays = layouts({n: np.asarray(v) for n, v in inputs.items()})
    nc = _bacc.Bacc("TRN2", target_bir_lowering=False, num_devices=1)
    d = {n: nc.dram_tensor(f"in_{n}", arrays[n].shape, F32, kind="ExternalInput").ap() for n in arrays}
    out = nc.dram_tensor("out", (P, TILES, D), F32, kind="ExternalOutput").ap()
    decoder(nc, d, out)
    r = _run(nc, [{f"in_{n}": arrays[n] for n in arrays}], core_ids=[0])
    got = r.results[0]["out"]
    return np.ascontiguousarray(np.transpose(got, (1, 0, 2))).reshape(BATCH, SEQ, D)
```

```python
from contextlib import ExitStack

import numpy as np
import concourse.bass as bass
from concourse import mybir

P = 128
SEQ = 64
BATCH = 32
D = 256
NTOK = BATCH * SEQ
TILES = NTOK // P
KC = D // P
BLK = 512
NBLK = NTOK // BLK
TPB = BLK // P
LN_EPS = 1e-5

F32 = mybir.dt.float32
ALU = mybir.AluOpType
ACT = mybir.ActivationFunctionType
AX = mybir.AxisListType


EXPERTS = {"f0": 16, "f2": 64, "f3": 8}


class Stage:

    def __init__(self, nc, name):
        self.nc, self.name, self.ctx, self.sems = nc, name, ExitStack(), []

    def __enter__(self):
        self.ctx.__enter__()
        return self

    def __exit__(self, *a):
        if self.sems and a[0] is None:
            with self.nc.Block() as block:
                @block.sync
                def _(sp):
                    for s in self.sems:
                        sp.sem_clear(s)
        return self.ctx.__exit__(*a)

    def sb(self, name, shape):
        return self.ctx.enter_context(self.nc.sbuf_tensor(f"{self.name}_{name}", list(shape), F32))

    def ps(self, name, shape):
        return self.ctx.enter_context(self.nc.psum_tensor(f"{self.name}_{name}", list(shape), F32))

    def sem(self, name):
        self.sems.append(self.ctx.enter_context(self.nc.semaphore(f"{self.name}_{name}")))
        return self.sems[-1]


class Count:

    def __init__(self, eng, sem, per=0, turn=0):
        self.eng, self.sem, self.per, self.turn, self.n = eng, sem, per, turn, 0

    def __call__(self, ins):
        self.n += 1
        ins.then_inc(self.sem, 1)
        self.eng.wait_ge(self.sem, self.turn * self.per + self.n if self.per else self.n)

    def end(self):
        assert not self.per or self.n == self.per, f"{self.sem}: {self.n} steps in a pass, not {self.per}"


def prime(eng, *sems):
    for s in sems:
        eng.sem_inc(s, 1)


def hold(pe, G, sem, value, out):
    pe.wait_ge(sem, value)
    pe.matmul(out[0:32, :], G.zero[:, 0:32], G.zero[:, 0:1], start=True, stop=True)


def rows(ap, n):
    p, m = ap.shape
    return ap.rearrange("p (o m) -> p o m", o=1).to_broadcast([p, n, m])


def cols(ap, m):
    p, n = ap.shape
    return ap.rearrange("p (n o) -> p n o", o=1).to_broadcast([p, n, m])


def dyn(i, n):
    return bass.ds(i * n, n)


def load(nc, pairs, sem):
    with nc.Block() as block:
        @block.sync
        def _(sp):
            for dst, src in pairs:
                sp.dma_start(dst, src).then_inc(sem, 16)
            sp.wait_ge(sem, 16 * len(pairs))


class Norm:

    def __init__(self, st, u=""):
        self.s, self.stats = st.sb(f"s{u}", [P, TPB, D]), st.sb(f"stats{u}", [P, TPB, 6])
        self.mean, self.gap, self.var = (st.sb(f"{m}{u}", [P, TPB]) for m in ("mean", "gap", "var"))
        self.std, self.rstd = st.sb(f"std{u}", [P, TPB]), st.sb(f"rstd{u}", [P, TPB])
        self.var_ready, self.std_ready = st.sem(f"var_ready{u}"), st.sem(f"std_ready{u}")


def normalise(dve, step, N, g, signal):
    for t in range(TPB):
        step(dve.bn_stats(N.stats[:, t, :], N.s[:, t, :]))
    step(dve.tensor_tensor(N.mean[:, :], N.stats[:, :, 1], N.stats[:, :, 4], ALU.add))
    step(dve.tensor_scalar(N.mean[:, :], N.mean[:, :], 0.5, None, ALU.mult))
    step(dve.tensor_tensor(N.gap[:, :], N.stats[:, :, 1], N.stats[:, :, 4], ALU.subtract))
    step(dve.tensor_tensor(N.gap[:, :], N.gap[:, :], N.gap[:, :], ALU.mult))
    step(dve.tensor_tensor(N.var[:, :], N.stats[:, :, 2], N.stats[:, :, 5], ALU.add))
    step(dve.tensor_scalar(N.var[:, :], N.var[:, :], 1.0 / D, LN_EPS, ALU.mult, ALU.add))
    dve.scalar_tensor_tensor(N.var[:, :], N.gap[:, :], 0.25, N.var[:, :], ALU.mult, ALU.add).then_inc(N.var_ready, 1)
    dve.wait_ge(N.std_ready, g + 1)
    step(dve.reciprocal(N.rstd[:, :], N.std[:, :]))
    for t in range(TPB):
        ins = dve.tensor_scalar(N.s[:, t, :], N.s[:, t, :], N.mean[:, t:t + 1], N.rstd[:, t:t + 1],
                                ALU.subtract, ALU.mult)
        if t < TPB - 1:
            step(ins)
        else:
            ins.then_inc(signal, 1)


def norm_root(act, N, g):
    act.wait_ge(N.var_ready, g + 1)
    act.activation(N.std[:, :], N.var[:, :], ACT.Sqrt).then_inc(N.std_ready, 1)


def residual_norm(nc, G, tag):
    with Stage(nc, f"ln{tag}") as st:
        N = [Norm(st, u) for u in range(2)]
        pT = [st.ps(f"pT{u}", [P, KC, BLK]) for u in range(2)]
        dve_step = st.sem("step")
        x_ready, stored, turned, xT_stored = st.sem("x_ready"), st.sem("stored"), st.sem("turned"), st.sem("xT")
        with nc.Block() as block:
            @block.vector
            def _(dve):
                with dve.Fori(0, NBLK // 2) as i:
                    step = Count(dve, dve_step, 30, i)
                    for u in range(2):
                        g, s = i * 2 + u, N[u].s
                        dve.wait_ge(stored, g + 1)
                        dve.wait_ge(turned, g + 1)
                        step(dve.tensor_tensor(s[:, :, :], G.x_tok[:, dyn(g, TPB), :], G.y[:, dyn(g, TPB), :], ALU.add))
                        normalise(dve, step, N[u], i, x_ready)
                    step.end()

            @block.gpsimd
            def _(pool):
                prime(pool, stored, stored)
                with pool.Fori(0, NBLK // 2) as i:
                    for u in range(2):
                        g = i * 2 + u
                        pool.wait_ge(x_ready, g + 1)
                        pool.tensor_copy(G.x_tok[:, dyn(g, TPB), :], N[u].s[:, :, :]).then_inc(stored, 1)

            @block.tensor
            def _(pe):
                prime(pe, turned, turned)
                with pe.Fori(0, NBLK // 2) as i:
                    for u in range(2):
                        g = i * 2 + u
                        pe.wait_ge(x_ready, g + 1)
                        pe.wait_ge(xT_stored, g * 2 + 1)
                        for c in range(KC):
                            for t in range(TPB):
                                last = pe.transpose(pT[u][:, c, t * P:(t + 1) * P], N[u].s[:, t, c * P:(c + 1) * P], G.ident[:, :])
                        last.then_inc(turned, 1)

            @block.scalar
            def _(act):
                prime(act, xT_stored, xT_stored, xT_stored)

                def store(i, u):
                    g = i * 2 + u
                    act.wait_ge(turned, g + 3)
                    for c in range(KC):
                        act.copy(G.xT[:, c, dyn(g, BLK)], pT[u][:, c, :]).then_inc(xT_stored, 1)

                with act.Fori(0, NBLK // 2) as i:
                    norm_root(act, N[0], i)
                    norm_root(act, N[1], i)
                    store(i, 0)
                    store(i, 1)


def tile_logits(nc, G, st, gate, width, logits):
    xt = st.sb("xt", [P, KC, P])
    pl = st.ps("pl", [P, width])
    copied, made, taken = st.sem("copied"), st.sem("made"), st.sem("taken")
    with nc.Block() as block:
        @block.scalar
        def _(act):
            with act.Fori(0, TILES) as t:
                act.wait_ge(made, t + 1)
                act.copy(xt[:, :, :], G.xT[:, :, dyn(t, P)]).then_inc(copied, 1)

        @block.tensor
        def _(pe):
            prime(pe, made)
            with pe.Fori(0, TILES) as t:
                pe.wait_ge(copied, t + 1)
                pe.wait_ge(taken, t + 1)
                for k in range(KC):
                    last = pe.matmul(pl[:, :], xt[:, k, :], gate[:, k, :], start=(k == 0), stop=(k == KC - 1))
                last.then_inc(made, 1)

        @block.vector
        def _(dve):
            prime(dve, taken)
            with dve.Fori(0, TILES) as t:
                dve.wait_ge(made, t + 2)
                dve.tensor_copy(logits[:, dyn(t, 1), :], pl[:, :].rearrange("p (o e) -> p o e", o=1)).then_inc(taken, 1)


def top_by_rank(dve, step, chosen, value, n, top, before, cmp, tie, rank):
    full = [P, TILES, n, n]
    mine = value.rearrange("p t (e o) -> p t e o", o=1).to_broadcast(full)
    other = value.rearrange("p t (o f) -> p t o f", o=1).to_broadcast(full)
    c4 = cmp[:, 0:TILES * n * n].rearrange("p (t e f) -> p t e f", t=TILES, e=n)
    t4 = tie[:, 0:TILES * n * n].rearrange("p (t e f) -> p t e f", t=TILES, e=n)
    b4 = before.rearrange("p (t e) f -> p t e f", t=1).to_broadcast(full)
    step(dve.tensor_tensor(c4, other, mine, ALU.is_gt))
    step(dve.tensor_tensor(t4, other, mine, ALU.is_equal))
    step(dve.tensor_tensor(t4, t4, b4, ALU.mult))
    step(dve.tensor_tensor(c4, c4, t4, ALU.add))
    r = rank[:, 0:TILES * n]
    step(dve.tensor_reduce(r, cmp[:, 0:TILES * n * n].rearrange("p (te f) -> p te f", f=n), AX.X, ALU.add))
    step(dve.tensor_scalar(chosen, r.rearrange("p (t e) -> p t e", t=TILES), float(top), None, ALU.is_lt))


def route_l0(nc, G, st, logits, combine, before16, before4):
    E, NG, GS, TOP, KEEP, SCALE = 16, 4, 4, 4, 2, 16.0
    cmp, tie, rank = st.sb("cmp", [P, TILES * E * E]), st.sb("tie", [P, TILES * E * E]), st.sb("rank", [P, TILES * E])
    best, keep = st.sb("best", [P, TILES, NG]), st.sb("keep", [P, TILES, NG])
    prob, mx, total = st.sb("prob", [P, TILES, E]), st.sb("mx", [P, TILES]), st.sb("total", [P, TILES])
    chosen = st.sb("chosen", [P, TILES, E])
    dve_step, shifted, exped = st.sem("rstep"), st.sem("shifted"), st.sem("exped")
    with nc.Block() as block:
        @block.vector
        def _(dve):
            step = Count(dve, dve_step)
            grouped = logits[:, :, :].rearrange("p t (g s) -> p (t g) s", g=NG)
            step(dve.tensor_reduce(best[:, :, :], grouped, AX.X, ALU.max))
            top_by_rank(dve, step, keep[:, :, :], best[:, :, :], NG, KEEP, before4[:, :, :], cmp, tie, rank)
            keep_all = cols(keep[:, :, :].rearrange("p t g -> p (t g)"), GS)
            step(dve.tensor_tensor(grouped, grouped, keep_all, ALU.mult))
            step(dve.tensor_reduce(mx[:, :], logits[:, :, :], AX.X, ALU.max))
            dve.tensor_tensor(prob[:, :, :], logits[:, :, :], cols(mx[:, :], E), ALU.subtract).then_inc(shifted, 1)
            dve.wait_ge(exped, 1)
            step(dve.tensor_reduce(total[:, :], prob[:, :, :], AX.X, ALU.add))
            step(dve.reciprocal(total[:, :], total[:, :]))
            step(dve.tensor_tensor(prob[:, :, :], prob[:, :, :], cols(total[:, :], E), ALU.mult))
            top_by_rank(dve, step, chosen[:, :, :], prob[:, :, :], E, TOP, before16[:, :, :], cmp, tie, rank)
            step(dve.tensor_tensor(prob[:, :, :], prob[:, :, :], chosen[:, :, :], ALU.mult))
            step(dve.tensor_scalar(combine[:, :, 0:E], prob[:, :, :], SCALE, None, ALU.mult))
            step(dve.memset(combine[:, :, E:E + 1], 1.0))

        @block.scalar
        def _(act):
            act.wait_ge(shifted, 1)
            act.activation(prob[:, :, :], prob[:, :, :], ACT.Exp).then_inc(exped, 1)


def route_l3(nc, G, st, logits, combine, before8):
    E, TOP = 8, 2
    cmp, tie, rank = st.sb("cmp", [P, TILES * E * E]), st.sb("tie", [P, TILES * E * E]), st.sb("rank", [P, TILES * E])
    prob, mx, total = st.sb("prob", [P, TILES, E]), st.sb("mx", [P, TILES]), st.sb("total", [P, TILES])
    chosen = st.sb("chosen", [P, TILES, E])
    dve_step, shifted, exped = st.sem("rstep"), st.sem("shifted"), st.sem("exped")
    with nc.Block() as block:
        @block.vector
        def _(dve):
            step = Count(dve, dve_step)
            step(dve.tensor_reduce(mx[:, :], logits[:, :, :], AX.X, ALU.max))
            dve.tensor_tensor(prob[:, :, :], logits[:, :, :], cols(mx[:, :], E), ALU.subtract).then_inc(shifted, 1)
            dve.wait_ge(exped, 1)
            step(dve.tensor_reduce(total[:, :], prob[:, :, :], AX.X, ALU.add))
            step(dve.reciprocal(total[:, :], total[:, :]))
            step(dve.tensor_tensor(prob[:, :, :], prob[:, :, :], cols(total[:, :], E), ALU.mult))
            top_by_rank(dve, step, chosen[:, :, :], prob[:, :, :], E, TOP, before8[:, :, :], cmp, tie, rank)
            step(dve.tensor_tensor(combine[:, :, 0:E], prob[:, :, :], chosen[:, :, :], ALU.mult))
            step(dve.memset(combine[:, :, E:E + 1], 1.0))

        @block.scalar
        def _(act):
            act.wait_ge(shifted, 1)
            act.activation(prob[:, :, :], prob[:, :, :], ACT.Exp).then_inc(exped, 1)


def route_l2(nc, G, st, logits, combine):
    E, TOP = 64, 8
    GONE = -3.0e38
    best, left, mask = st.sb("best", [P, TILES, TOP]), st.sb("left", [P, TILES, E]), st.sb("mask", [P, TILES, E])
    prob, total = st.sb("prob", [P, TILES, E]), st.sb("total", [P, TILES])
    dve_step, shifted, exped = st.sem("rstep"), st.sem("shifted"), st.sem("exped")
    with nc.Block() as block:
        @block.vector
        def _(dve):
            step = Count(dve, dve_step)
            for t in range(TILES):
                step(dve.max(best[:, t, :], logits[:, t, 0:E]))
            for t in range(TILES):
                step(dve.match_replace(left[:, t, :], best[:, t, :], logits[:, t, 0:E], GONE))
            step(dve.tensor_tensor(mask[:, :, :], left[:, :, :], logits[:, :, 0:E], ALU.not_equal))
            dve.tensor_tensor(prob[:, :, :], logits[:, :, 0:E], best[:, :, 0:1].to_broadcast([P, TILES, E]),
                              ALU.subtract).then_inc(shifted, 1)
            dve.wait_ge(exped, 2)
            step(dve.tensor_tensor(prob[:, :, :], prob[:, :, :], mask[:, :, :], ALU.mult))
            step(dve.tensor_reduce(total[:, :], prob[:, :, :], AX.X, ALU.add))
            step(dve.reciprocal(total[:, :], total[:, :]))
            step(dve.tensor_tensor(combine[:, :, 0:E], prob[:, :, :], cols(total[:, :], E), ALU.mult))

        @block.scalar
        def _(act):
            act.wait_ge(shifted, 1)
            act.activation(prob[:, :, :], prob[:, :, :], ACT.Exp).then_inc(exped, 1)
            act.activation(combine[:, :, E:E + 1], logits[:, :, E:E + 1], ACT.Sigmoid).then_inc(exped, 1)


def gated_experts(nc, G, tag, d):
    W, WO = d[f"{tag}_in_w"], d[f"{tag}_out_w"]
    FT = W.shape[0]
    E1 = EXPERTS[tag] + 1
    EW = d[f"{tag}_gate"].shape[2]
    with Stage(nc, tag) as st:
        combT = st.sb("combT", [E1, NTOK])
        sem = st.sem("loaded")
        with Stage(nc, tag + "r") as rt:
            combine = rt.sb("combine", [P, TILES, E1])
            logits = rt.sb("logits", [P, TILES, EW])
            gate = rt.sb("gate", [P, KC, EW])
            todo = [(gate[:, :, :], d[f"{tag}_gate"])]
            if tag == "f0":
                b16, b4 = rt.sb("b16", [P, 16, 16]), rt.sb("b4", [P, 4, 4])
                todo += [(b16[:, :, :], d["before16"]), (b4[:, :, :], d["before4"])]
            if tag == "f3":
                b8 = rt.sb("b8", [P, 8, 8])
                todo += [(b8[:, :, :], d["before8"])]
            load(nc, todo, sem)
            tile_logits(nc, G, rt, gate, EW, logits)
            if tag == "f0":
                route_l0(nc, G, rt, logits, combine, b16, b4)
            elif tag == "f2":
                route_l2(nc, G, rt, logits, combine)
            else:
                route_l3(nc, G, rt, logits, combine, b8)
            pT = rt.ps("pT", [P, NBLK, BLK])
            turned, stored = rt.sem("turned"), rt.sem("stored")
            with nc.Block() as block:
                @block.tensor
                def _(pe):
                    for t in range(TILES):
                        pe.transpose(pT[0:E1, t // TPB, (t % TPB) * P:(t % TPB + 1) * P], combine[:, t, :],
                                     G.ident[:, :]).then_inc(turned, 1)

                @block.vector
                def _(dve):
                    for b in range(NBLK):
                        dve.wait_ge(turned, TPB * (b + 1))
                        dve.tensor_copy(combT[:, b * BLK:(b + 1) * BLK], pT[0:E1, b, :]).then_inc(stored, 1)
        w_in = [st.sb(f"w_in{u}", [P, 5, P]) for u in range(2)]
        w_out = [st.sb(f"w_out{u}", [P, D]) for u in range(2)]
        act_g = [st.sb(f"act_g{u}", [P, BLK]) for u in range(2)]
        hidden = [st.sb(f"hidden{u}", [P, BLK]) for u in range(2)]
        pg = [st.ps(f"pg{u}", [P, BLK]) for u in range(2)]
        pu = [st.ps(f"pu{u}", [P, BLK]) for u in range(2)]
        pc = [st.ps(f"pc{u}", [P, BLK]) for u in range(2)]
        py = st.ps("py", [P, TPB, D])
        win_in = [st.sem(f"w_in_here{u}") for u in range(2)]
        wout_in = [st.sem(f"w_out_here{u}") for u in range(2)]
        up_made = [st.sem(f"up_made{u}") for u in range(2)]
        silu_done = [st.sem(f"silu_done{u}") for u in range(2)]
        gated = [st.sem(f"gated{u}") for u in range(2)]
        hid_done = [st.sem(f"hid_done{u}") for u in range(2)]
        down_made = [st.sem(f"down_made{u}") for u in range(2)]
        y_made, y_taken = st.sem("y_made"), st.sem("y_taken")
        n = [(FT + 1) // 2, FT // 2]
        pairs = (FT - 1) // 2

        with nc.Block() as block:
            @block.sync
            def _(sp):
                def fetch(b, jj, u):
                    sp.wait_ge(up_made[u], b * n[u] + jj + 1)
                    sp.dma_start(w_in[u][:, :, :], W[bass.ds(jj * 2 + u, 1)].rearrange("o p c m -> (o p) c m")
                                 ).then_inc(win_in[u], 16)
                    sp.wait_ge(down_made[u], b * n[u] + jj + 1)
                    sp.dma_start(w_out[u][:, :], WO[bass.ds(jj * 2 + u, 1)].rearrange("o p m -> (o p) m")
                                 ).then_inc(wout_in[u], 16)

                with sp.Fori(0, NBLK) as b:
                    with sp.Fori(0, FT // 2) as jj:
                        for u in range(2):
                            fetch(b, jj, u)
                    if FT % 2:
                        fetch(b, FT // 2, 0)

            @block.tensor
            def _(pe):
                def up(b, jj, u):
                    pe.wait_ge(win_in[u], (b * n[u] + jj + 1) * 16)
                    pe.wait_ge(hid_done[u], b * n[u] + jj + 1)
                    for c, out in ((0, pg[u]), (1, pu[u])):
                        for k in range(KC):
                            pe.matmul(out[:, :], w_in[u][:, 2 * c + k, :], G.xT[:, k, dyn(b, BLK)],
                                      start=(k == 0), stop=(k == KC - 1))
                    pe.matmul(pc[u][:, :], w_in[u][0:E1, 4, :], combT[:, dyn(b, BLK)],
                              start=True, stop=True).then_inc(up_made[u], 1)

                def down(b, jj, u):
                    pe.wait_ge(wout_in[u], (b * n[u] + jj + 1) * 16)
                    pe.wait_ge(hid_done[u], b * n[u] + jj + 2)
                    for t in range(TPB):
                        last = pe.matmul(py[:, t, :], hidden[u][:, t * P:(t + 1) * P], w_out[u][:, :],
                                         start=False, stop=False, skip_group_check=True)
                    last.then_inc(down_made[u], 1)

                prime(pe, *up_made, *down_made)
                with pe.Fori(0, NBLK) as b:
                    up(b, 0, 0)
                    pe.wait_ge(y_taken, b + 1)
                    for h in range(2):
                        pe.matmul(py[:, 2 * h:2 * h + 2, :], G.zero[0:1, 0:P], G.zero[0:1, 0:BLK],
                                  start=True, stop=False, skip_group_check=True)
                    with pe.Fori(0, pairs) as jj:
                        up(b, jj, 1)
                        down(b, jj, 0)
                        up(b, jj + 1, 0)
                        down(b, jj, 1)
                    if FT % 2 == 0:
                        up(b, pairs, 1)
                    down(b, pairs, 0)
                    if FT % 2 == 0:
                        down(b, pairs, 1)
                    for h in range(2):
                        last = pe.matmul(py[:, 2 * h:2 * h + 2, :], G.zero[0:1, 0:P], G.zero[0:1, 0:BLK],
                                         start=False, stop=True, skip_group_check=True)
                    last.then_inc(y_made, 1)

            @block.scalar
            def _(act):
                def silu(b, jj, u):
                    act.wait_ge(up_made[u], b * n[u] + jj + 2)
                    act.wait_ge(hid_done[u], b * n[u] + jj + 1)
                    act.activation(act_g[u][:, :], pg[u][:, :], ACT.Silu).then_inc(silu_done[u], 1)

                prime(act, y_taken)
                with act.Fori(0, NBLK) as b:
                    with act.Fori(0, FT // 2) as jj:
                        for u in range(2):
                            silu(b, jj, u)
                    if FT % 2:
                        silu(b, FT // 2, 0)
                    act.wait_ge(y_made, b + 1)
                    act.copy(G.y[:, dyn(b, TPB), :], py[:, :, :]).then_inc(y_taken, 1)

            @block.vector
            def _(dve):
                def gate_hidden(b, jj, u):
                    dve.wait_ge(silu_done[u], b * n[u] + jj + 1)
                    dve.wait_ge(down_made[u], b * n[u] + jj + 1)
                    dve.tensor_tensor(act_g[u][:, :], act_g[u][:, :], pu[u][:, :], ALU.mult).then_inc(gated[u], 1)
                    dve.wait_ge(gated[u], b * n[u] + jj + 1)
                    dve.tensor_tensor(hidden[u][:, :], act_g[u][:, :], pc[u][:, :], ALU.mult).then_inc(hid_done[u], 1)

                prime(dve, *hid_done)
                with dve.Fori(0, NBLK) as b:
                    with dve.Fori(0, FT // 2) as jj:
                        for u in range(2):
                            gate_hidden(b, jj, u)
                    if FT % 2:
                        gate_hidden(b, FT // 2, 0)


def store_y(act, G, py, y_made, y_taken, b):
    act.wait_ge(y_made, b + 1)
    act.copy(G.y[:, dyn(b, TPB), :], py[:, :, :]).then_inc(y_taken, 1)


def random_feature_attention(nc, G, tag, d):
    TWO_PI_HI = 6.28125
    TWO_PI_LO = 2 * np.pi - TWO_PI_HI
    ROUND = 12582912.0
    PI = 3.1415925
    HQ, HK, HD, NF = 16, 8, 16, 8
    H, QK = HQ + HK, (HQ + HK) * HD
    with Stage(nc, tag) as st:
        w, b_row = st.sb("w", [P, KC, 2 * BLK]), st.sb("b_row", [1, 2 * BLK])
        wo, bo = st.sb("wo", [P, KC, D]), st.sb("bo", [1, D])
        cos_t, sin_t = st.sb("cos", [P, HD]), st.sb("sin", [P, HD])
        rmat, ones = st.sb("rmat", [P, HK * NF]), st.sb("ones", [1, P])
        xt = st.sb("xt", [P, KC, P])
        x, t1, v = st.sb("x", [P, H, HD]), st.sb("t1", [P, H, HD]), st.sb("v", [P, HK, HD])
        norm = st.sb("norm", [P, H])
        xT = st.sb("xT", [P, 3, P])
        heads_first = nc.dram_tensor("heads_first", (BATCH, HQ, SEQ, HD), F32, kind="Internal").ap()
        angle, whole, feat = (st.sb(m, [P, H, 2, NF]) for m in ("angle", "whole", "feat"))
        prod, sim, o, oT = st.sb("prod", [P, HQ, HK * HD]), st.sb("sim", [P, HQ * HK]), st.sb("o", [P, HQ * HD]), st.sb("oT", [P, KC, P])
        pA, pB, pT = st.ps("pA", [P, BLK]), st.ps("pB", [P, BLK]), st.ps("pT", [P, 3, P])
        pF, pOT, pY = st.ps("pF", [P, H, NF]), st.ps("pOT", [P, KC, P]), st.ps("pY", [P, D])
        load(nc, [(w[:, :, :], d["a0_w"]), (b_row[:, :], d["a0_b"]), (wo[:, :, :], d["a0_wo"]), (bo[:, :], d["a0_bo"]),
                  (cos_t[:, :], d["a0_cos"]), (sin_t[:, :], d["a0_sin"]), (ones[:, :], d["ones_row"]),
                  (rmat[:, :], d["zero"][:, 0:64])], st.sem("loaded"))
        load(nc, [(rmat[HD * h:HD * h + HD, NF * h:NF * h + NF], d["a0_r"]) for h in range(8)], st.sem("loaded_r"))
        z = {m: st.sem(m) for m in ("copied", "projected", "v_kept", "squared", "rooted", "unit", "turned", "t_kept",
                                    "random", "reduced", "featured", "o_ready", "o_turned", "ot_kept", "y_made", "done", "dstep",
                                    "o_sent", "o_here")}
        with nc.Block() as block:
            @block.tensor
            def _(pe):
                def project(t):
                    pe.wait_ge(z["copied"], t + 1)
                    for out, at, n in ((pA, 0, BLK), (pB, BLK, QK)):
                        for k in range(KC):
                            pe.matmul(out[:, 0:n], xt[:, k, :], w[:, k, at:at + n], start=(k == 0), stop=False)
                        last = pe.matmul(out[:, 0:n], ones[:, :], b_row[:, at:at + n], start=False, stop=True)
                    last.then_inc(z["projected"], 1)

                def features(t):
                    pe.wait_ge(z["unit"], t + 1)
                    for c in range(3):
                        last = pe.transpose(pT[:, c, :], x[:, 8 * c:8 * c + 8, :], G.ident[:, :])
                    last.then_inc(z["turned"], 1)
                    pe.wait_ge(z["t_kept"], t + 1)
                    for c in range(3):
                        last = pe.matmul(pF[:, 8 * c:8 * c + 8, :], xT[:, c, :], rmat[:, :], start=True, stop=True)
                    last.then_inc(z["random"], 1)

                project(0)
                with pe.Fori(0, TILES - 1) as t:
                    features(t)
                    pe.wait_ge(z["squared"], t + 1)
                    pe.wait_ge(z["v_kept"], t + 1)
                    project(t + 1)
                features(TILES - 1)

            @block.scalar
            def _(act):
                def take_tile(t):
                    act.copy(xt[:, :, :], G.xT[:, :, dyn(t, P)]).then_inc(z["copied"], 1)

                def body(t, following):
                    act.wait_ge(z["squared"], t + 1)
                    act.wait_ge(z["o_ready"], t + 1)
                    act.mul(v[:, :, :], pA[:, QK:BLK].rearrange("p (h e) -> p h e", e=HD), 0.125).then_inc(z["v_kept"], 1)
                    act.activation(norm[:, :], norm[:, :], ACT.Sqrt).then_inc(z["rooted"], 1)
                    act.wait_ge(z["turned"], t + 1)
                    act.copy(xT[:, :, :], pT[:, :, :]).then_inc(z["t_kept"], 1)
                    if following is not None:
                        take_tile(following)
                    act.wait_ge(z["reduced"], t + 1)
                    act.activation(feat[:, :, :, :], angle[:, :, :, :], ACT.Sin).then_inc(z["featured"], 1)

                take_tile(0)
                with act.Fori(0, TILES - 1) as t:
                    body(t, t + 1)
                body(TILES - 1, None)

            @block.vector
            def _(dve):
                prime(dve, z["o_ready"])
                with dve.Fori(0, TILES) as t:
                    step = Count(dve, z["dstep"], 17, t)
                    a = pA[:, 0:QK].rearrange("p (h e) -> p h e", e=HD)
                    b = pB[:, 0:QK].rearrange("p (h e) -> p h e", e=HD)
                    dve.wait_ge(z["projected"], t + 1)
                    step(dve.tensor_tensor(x[:, :, :], a, rows(cos_t[:, :], H), ALU.mult))
                    step(dve.tensor_tensor(t1[:, :, :], b, rows(sin_t[:, :], H), ALU.mult))
                    step(dve.tensor_tensor(x[:, :, :], x[:, :, :], t1[:, :, :], ALU.add))
                    step(dve.tensor_tensor(t1[:, :, :], x[:, :, :], x[:, :, :], ALU.mult))
                    dve.tensor_reduce(norm[:, :], t1[:, :, :], AX.X, ALU.add).then_inc(z["squared"], 1)
                    dve.wait_ge(z["rooted"], t + 1)
                    step(dve.tensor_scalar(norm[:, :], norm[:, :], 1e-6, None, ALU.max))
                    step(dve.reciprocal(norm[:, :], norm[:, :]))
                    dve.tensor_tensor(x[:, :, :], x[:, :, :], cols(norm[:, :], HD), ALU.mult).then_inc(z["unit"], 1)
                    dve.wait_ge(z["random"], t + 1)
                    for j in range(2):
                        step(dve.tensor_scalar(whole[:, :, j, :], pF[:, :, :], 1.0 / (2 * np.pi), 0.25 * j, ALU.mult, ALU.add))
                    step(dve.tensor_scalar(whole[:, :, :, :], whole[:, :, :, :], ROUND, None, ALU.add))
                    step(dve.tensor_scalar(whole[:, :, :, :], whole[:, :, :, :], -ROUND, None, ALU.add))
                    for j in range(2):
                        step(dve.scalar_tensor_tensor(angle[:, :, j, :], whole[:, :, j, :], -TWO_PI_HI, pF[:, :, :],
                                                      ALU.mult, ALU.add))
                    step(dve.scalar_tensor_tensor(angle[:, :, :, :], whole[:, :, :, :], -TWO_PI_LO, angle[:, :, :, :],
                                                  ALU.mult, ALU.add))
                    step(dve.tensor_scalar(angle[:, :, 1, :], angle[:, :, 1, :], float(np.pi / 2), None, ALU.add))
                    dve.tensor_scalar(angle[:, :, :, :], angle[:, :, :, :], PI, -PI, ALU.min, ALU.max).then_inc(z["reduced"], 1)
                    dve.wait_ge(z["featured"], t + 1)
                    full = [P, HQ, HK, HD]
                    f = feat[:, :, :, :].rearrange("p h j e -> p h (j e)")
                    fq = f[:, 0:HQ, :].rearrange("p h (o f) -> p h o f", o=1).to_broadcast(full)
                    fk = f[:, HQ:H, :].rearrange("p (o h) f -> p o h f", o=1).to_broadcast(full)
                    step(dve.tensor_tensor(prod[:, :, :].rearrange("p h (g f) -> p h g f", f=HD), fq, fk, ALU.mult))
                    step(dve.tensor_reduce(sim[:, :], prod[:, :, :].rearrange("p h (g f) -> p (h g) f", f=HD), AX.X, ALU.add))
                    dve.wait_ge(z["v_kept"], t + 1)
                    full = [P, HQ, HD, HK]
                    s4 = sim[:, :].rearrange("p (h o g) -> p h o g", o=1, g=HK).to_broadcast(full)
                    v4 = v[:, :, :].rearrange("p (o g) e -> p o e g", o=1).to_broadcast(full)
                    step(dve.tensor_tensor(prod[:, :, :].rearrange("p h (e g) -> p h e g", g=HK), s4, v4, ALU.mult))
                    dve.wait_ge(z["o_sent"], t * 32 + 1)
                    dve.tensor_reduce(o[:, :], prod[:, :, :].rearrange("p h (e g) -> p (h e) g", g=HK), AX.X,
                                      ALU.add).then_inc(z["o_ready"], 1)
                    step.end()

            @block.sync
            def _(sp):
                sp.sem_inc(z["o_sent"], 1)
                with sp.Fori(0, TILES) as t:
                    sp.wait_ge(z["o_ready"], t + 2)
                    for s in range(2):
                        sp.dma_start(heads_first[dyn(t * 2 + s, 1)].rearrange("o h t e -> (o t) h e"),
                                     o[s * SEQ:(s + 1) * SEQ, :].rearrange("p (h e) -> p h e", e=HD)).then_inc(z["o_sent"], 16)
                sp.wait_ge(z["o_sent"], TILES * 32 + 1)

        load(nc, [(G.y[:, :, :], heads_first.rearrange("(n s) h (j t) e -> (s h j) n (t e)", s=2, j=4))], st.sem("reshaped"))
        with nc.Block() as block:
            @block.scalar
            def _(act):
                with act.Fori(0, TILES) as t:
                    act.wait_ge(z["o_turned"], t + 1)
                    act.copy(o[:, :].rearrange("p (o e) -> p o e", o=1), G.y[:, dyn(t, 1), :]).then_inc(z["o_here"], 1)
                    act.wait_ge(z["o_turned"], t + 2)
                    act.copy(oT[:, :, :], pOT[:, :, :]).then_inc(z["ot_kept"], 1)

            @block.vector
            def _(dve):
                prime(dve, z["done"])
                with dve.Fori(0, TILES) as t:
                    dve.wait_ge(z["y_made"], t + 1)
                    dve.tensor_scalar(G.y[:, dyn(t, 1), :], pY[:, :].rearrange("p (o e) -> p o e", o=1), 1.0, None,
                                      ALU.mult).then_inc(z["done"], 1)

            @block.tensor
            def _(pe):
                prime(pe, z["o_turned"])
                with pe.Fori(0, TILES) as t:
                    pe.wait_ge(z["o_here"], t + 1)
                    for c in range(KC):
                        last = pe.transpose(pOT[:, c, :], o[:, c * P:(c + 1) * P], G.ident[:, :])
                    last.then_inc(z["o_turned"], 1)
                    pe.wait_ge(z["ot_kept"], t + 1)
                    pe.wait_ge(z["done"], t + 1)
                    for c in range(KC):
                        pe.matmul(pY[:, :], oT[:, c, :], wo[:, c, :], start=(c == 0), stop=False)
                    pe.matmul(pY[:, :], ones[:, :], bo[:, :], start=False, stop=True).then_inc(z["y_made"], 1)


def wkv(nc, G, tag, d):
    S1 = SEQ + 1
    NEG = -1e38
    with Stage(nc, tag) as st:
        wu = st.sb("wu", [P, 2, KC])
        vT = st.sb("vT", [P, NTOK])
        names = ["wtab", "k1", "o", "a2", "e2", "e2v", "p", "q"]
        B = {m: st.sb(m, [P, BATCH, S1]) for m in names}
        no, a, e = st.sb("no", [P, BATCH, SEQ]), st.sb("a", [P, BATCH, SEQ]), st.sb("e", [P, BATCH, SEQ])
        yT = st.sb("yT", [P, KC, NTOK])
        py = st.ps("py", [P, TILES, D])
        v_here, dve_step, half1, exp1 = st.sem("v_here"), st.sem("step"), st.sem("half1"), st.sem("exp1")
        half2, exp2, made, turned, v_used = st.sem("half2"), st.sem("exp2"), st.sem("made"), st.sem("turned"), st.sem("v_used")
        load(nc, [(wu[:, :, :], d["x0_wu"])], st.sem("loaded"))
        flat = {m: B[m][:, :, :].rearrange("p b s -> p (b s)") for m in names}
        pad = {m: B[m][:, :, 0:1] for m in names}
        cur = {m: B[m][:, :, 1:S1] for m in names}
        prev = {m: B[m][:, :, 0:SEQ] for m in names}
        with nc.Block() as block:
            @block.sync
            def _(sp):
                for c in range(KC):
                    if c:
                        sp.wait_ge(v_used, c)
                    sp.dma_start(vT[:, :], d["ctxT"][:, c, :]).then_inc(v_here, 16)

            @block.vector
            def _(dve):
                step = Count(dve, dve_step)
                v3 = vT[:, :].rearrange("p (b s) -> p b s", s=SEQ)
                for m in ("a2", "e2", "e2v"):
                    step(dve.memset(pad[m], 0.0))
                step(dve.memset(pad["k1"], NEG))
                for c in range(KC):
                    w, u = wu[:, 0, c:c + 1], wu[:, 1, c:c + 1]
                    k3 = G.xT[:, c, :].rearrange("p (b s) -> p b s", s=SEQ)
                    step(dve.tensor_copy(cur["k1"], k3))
                    step(dve.memset(flat["wtab"], 0.0))
                    step(dve.tensor_scalar(flat["wtab"], flat["wtab"], w, None, ALU.add))
                    step(dve.memset(pad["wtab"], NEG))
                    step(dve.tensor_tensor_scan(flat["o"], flat["wtab"], flat["k1"], NEG, ALU.add, ALU.max))
                    step(dve.scalar_tensor_tensor(cur["a2"], prev["o"], w, cur["o"], ALU.add, ALU.subtract))
                    dve.tensor_tensor(cur["e2"], k3, cur["o"], ALU.subtract).then_inc(half1, 1)
                    step(dve.scalar_tensor_tensor(no[:, :, :], k3, u, prev["o"], ALU.add, ALU.max))
                    step(dve.tensor_tensor(a[:, :, :], prev["o"], no[:, :, :], ALU.subtract))
                    dve.scalar_tensor_tensor(e[:, :, :], k3, u, no[:, :, :], ALU.add, ALU.subtract).then_inc(half2, 1)
                    dve.wait_ge(exp1, c + 1)
                    dve.wait_ge(v_here, 16 * (c + 1))
                    step(dve.tensor_tensor(cur["e2v"], cur["e2"], v3, ALU.mult))
                    step(dve.tensor_tensor_scan(flat["p"], flat["a2"], flat["e2v"], 0.0, ALU.mult, ALU.add))
                    step(dve.tensor_tensor_scan(flat["q"], flat["a2"], flat["e2"], 0.0, ALU.mult, ALU.add))
                    dve.wait_ge(exp2, c + 1)
                    step(dve.tensor_tensor(prev["p"], prev["p"], a[:, :, :], ALU.mult))
                    step(dve.tensor_tensor(prev["q"], prev["q"], a[:, :, :], ALU.mult))
                    step(dve.tensor_tensor(prev["q"], prev["q"], e[:, :, :], ALU.add))
                    dve.tensor_tensor(a[:, :, :], e[:, :, :], v3, ALU.mult).then_inc(v_used, 1)
                    dve.wait_ge(v_used, c + 1)
                    step(dve.tensor_tensor(prev["p"], prev["p"], a[:, :, :], ALU.add))
                    step(dve.reciprocal(prev["q"], prev["q"]))
                    dve.tensor_tensor(yT[:, c, :].rearrange("p (b s) -> p b s", s=SEQ), prev["p"], prev["q"],
                                      ALU.mult).then_inc(made, 1)

            @block.scalar
            def _(act):
                for c in range(KC):
                    act.wait_ge(half1, c + 1)
                    act.activation(cur["a2"], cur["a2"], ACT.Exp)
                    act.activation(cur["e2"], cur["e2"], ACT.Exp).then_inc(exp1, 1)
                    act.wait_ge(half2, c + 1)
                    act.activation(a[:, :, :], a[:, :, :], ACT.Exp)
                    act.activation(e[:, :, :], e[:, :, :], ACT.Exp).then_inc(exp2, 1)
                for g in range(NBLK):
                    act.wait_ge(turned, (KC - 1) * NBLK + g + 1)
                    act.copy(G.y[:, g * TPB:(g + 1) * TPB, :], py[:, g * TPB:(g + 1) * TPB, :])

            @block.tensor
            def _(pe):
                for c in range(KC):
                    pe.wait_ge(made, c + 1)
                    for t in range(TILES):
                        ins = pe.transpose(py[:, t, c * P:(c + 1) * P], yT[:, c, t * P:(t + 1) * P], G.ident[:, :])
                        if t % TPB == TPB - 1:
                            ins.then_inc(turned, 1)


def ternary_ffn(nc, G, tag, d):
    FF = 1024
    FT = FF // P
    with Stage(nc, tag) as st:
        w1, w2 = st.sb("w1", [P, KC * FF]), st.sb("w2", [P, FT * D])
        q1, q2 = st.sb("q1", [P, KC, FF]), st.sb("q2", [P, FT, D])
        b1, b2, ones = st.sb("b1", [P, FT]), st.sb("b2", [1, D]), st.sb("ones", [1, P])
        allp = st.sb("allp", [P, P])
        part, thr = st.sb("part", [P, 2]), st.sb("thr", [P, 2, 2])
        low = st.sb("low", [P, KC * FF])
        hidden = [st.sb(f"hidden{u}", [P, BLK]) for u in range(2)]
        ph = [st.ps(f"ph{u}", [P, BLK]) for u in range(2)]
        py, psum = st.ps("py", [P, TPB, D]), st.ps("psum", [P, 2])
        load(nc, [(w1[:, :], d["f1_w1"].rearrange("p k f -> p (k f)")), (w2[:, :], d["f1_w2"].rearrange("p k f -> p (k f)")),
                  (b1[:, :], d["f1_b1"]), (b2[:, :], d["f1_b2"]),
                  (ones[:, :], d["ones_row"]), (allp[:, :], d["all_ones"])], st.sem("loaded"))
        q_step, parted, summed = st.sem("q_step"), st.sem("parted"), st.sem("summed")
        with nc.Block() as block:
            @block.vector
            def _(dve):
                step = Count(dve, q_step)
                step(dve.tensor_reduce(part[:, 0:1], w1[:, :], AX.X, ALU.add, apply_absolute_value=True))
                dve.tensor_reduce(part[:, 1:2], w2[:, :], AX.X, ALU.add, apply_absolute_value=True).then_inc(parted, 1)
                dve.wait_ge(summed, 1)
                step(dve.tensor_scalar(thr[:, 1, :], psum[:, :], 1.0 / (FF * D), None, ALU.mult))
                step(dve.tensor_scalar(thr[:, 0, :], thr[:, 1, :], 0.7, None, ALU.mult))
                step(dve.tensor_scalar(thr[:, 1, :], thr[:, 0, :], -1.0, None, ALU.mult))
                for m, (w, q) in enumerate(((w1, q1), (w2, q2))):
                    flat = q[:, :, :].rearrange("p k f -> p (k f)")
                    step(dve.tensor_scalar(flat, w[:, :], thr[:, 0, m:m + 1], None, ALU.is_ge))
                    step(dve.tensor_scalar(low[:, :], w[:, :], thr[:, 1, m:m + 1], None, ALU.is_le))
                    step(dve.tensor_tensor(flat, flat, low[:, :], ALU.subtract))

            @block.tensor
            def _(pe):
                pe.wait_ge(parted, 1)
                pe.matmul(psum[:, :], allp[:, :], part[:, :], start=True, stop=True).then_inc(summed, 1)

        made = [st.sem(f"made{u}") for u in range(2)]
        gelued = [st.sem(f"gelued{u}") for u in range(2)]
        downed = [st.sem(f"downed{u}") for u in range(2)]
        y_made, y_taken = st.sem("y_made"), st.sem("y_taken")
        H = FT // 2
        with nc.Block() as block:
            @block.tensor
            def _(pe):
                prime(pe, *downed)
                with pe.Fori(0, NBLK) as b:
                    pe.wait_ge(y_taken, b + 1)
                    for h in range(2):
                        pe.matmul(py[:, 2 * h:2 * h + 2, :], ones[:, :], rows(b2[:, :], 2), start=True, stop=False,
                                  skip_group_check=True)

                    def up(f):
                        u, turn = f % 2, b * H + f // 2
                        pe.wait_ge(gelued[u], turn + 1)
                        for k in range(KC):
                            last = pe.matmul(ph[u][:, :], q1[:, k, f * P:(f + 1) * P], G.xT[:, k, dyn(b, BLK)],
                                             start=(k == 0), stop=(k == KC - 1))
                        last.then_inc(made[u], 1)

                    def down(f):
                        u, turn = f % 2, b * H + f // 2
                        pe.wait_ge(gelued[u], turn + 2)
                        for t in range(TPB):
                            last = pe.matmul(py[:, t, :], hidden[u][:, t * P:(t + 1) * P], q2[:, f, :],
                                             start=False, stop=(f == FT - 1), skip_group_check=True)
                        last.then_inc(downed[u], 1)

                    up(0)
                    for f in range(1, FT):
                        up(f)
                        down(f - 1)
                    down(FT - 1)
                    pe.matmul(psum[:, 0:1], G.zero[:, 0:P], G.zero[:, 0:1], start=True, stop=True).then_inc(y_made, 1)

            @block.scalar
            def _(act):
                prime(act, *gelued, y_taken)
                with act.Fori(0, NBLK) as b:
                    for f in range(FT):
                        u, turn = f % 2, b * H + f // 2
                        act.wait_ge(made[u], turn + 1)
                        act.wait_ge(downed[u], turn + 1)
                        act.activation(hidden[u][:, :], ph[u][:, :], ACT.Gelu, bias=b1[:, f:f + 1]).then_inc(gelued[u], 1)
                    store_y(act, G, py, y_made, y_taken, b)


def ema_summary(nc, G, tag, d):
    with Stage(nc, tag) as st:
        ctx = st.sb("ctx", [P, KC, NTOK])
        w_in, w_out = st.sb("w_in", [P, KC, D]), st.sb("w_out", [P, KC, D])
        b_in, b_out = st.sb("b_in", [P, KC]), st.sb("b_out", [1, D])
        gamma, beta, ones = st.sb("gamma", [P, D]), st.sb("beta", [P, D]), st.sb("ones", [P, SEQ])
        decay, keep = st.sb("decay", [P, 1]), st.sb("keep", [P, 1])
        ktab, wt, wsum = st.sb("ktab", [P, SEQ]), st.sb("wt", [P, SEQ]), st.sb("wsum", [P, 1])
        mean_ctx, bw, xbar = st.sb("mean_ctx", [P, KC, BATCH]), st.sb("bw", [P, KC]), st.sb("xbar", [P, KC, BATCH])
        summary, of_seq = st.sb("summary", [BATCH, D]), st.sb("of_seq", [BATCH, NTOK])
        row1 = st.sb("row1", [1, P])
        loads = [(ctx[:, :, :], d["ctxT_rev"]), (w_in[:, :, :], d["x2_w_in"]), (w_out[:, :, :], d["x2_w_out"]),
                 (b_in[:, :], d["x2_b_in"]), (b_out[:, :], d["x2_b_out"]),
                 (gamma[:, :], d["x2_gamma"].to_broadcast([P, D])), (beta[:, :], d["x2_beta"].to_broadcast([P, D])),
                 (decay[:, :], d["x2_decay"].to_broadcast([P, 1])), (ones[:, :], d["all_ones"][:, 0:SEQ]),
                 (of_seq[:, :], d["of_seq"]), (row1[:, :], d["ones_row"])]
        load(nc, loads, st.sem("loaded"))
        dstep, kept, averaged, barred, b_ready = st.sem("dstep"), st.sem("kept"), st.sem("averaged"), st.sem("barred"), st.sem("b_ready")
        summed, s_ready, spread = st.sem("summed"), st.sem("s_ready"), st.sem("spread")
        with Stage(nc, tag + "p") as pt:
            px, psm = pt.ps("px", [P, KC, BATCH]), pt.ps("psm", [BATCH, D])
            pspread = pt.ps("pspread", [P, TPB, D])
            taken = pt.sem("taken")
            with nc.Block() as block:
                @block.scalar
                def _(act):
                    act.activation(keep[:, :], decay[:, :], ACT.Sigmoid).then_inc(kept, 1)

                @block.vector
                def _(dve):
                    step = Count(dve, dstep)
                    dve.wait_ge(kept, 1)
                    step(dve.tensor_scalar(ktab[:, :], ones[:, :], keep[:, :], None, ALU.mult))
                    step(dve.tensor_tensor_scan(wt[:, :], ktab[:, :], ones[:, :], 0.0, ALU.mult, ALU.add))
                    step(dve.tensor_scalar(wt[:, :], wt[:, :], 1.0 / SEQ, None, ALU.mult))
                    step(dve.tensor_reduce(wsum[:, :], wt[:, :], AX.X, ALU.add))
                    c3 = ctx[:, :, :].rearrange("p k (b s) -> p (k b) s", s=SEQ)
                    step(dve.tensor_tensor(c3, c3, rows(wt[:, :], KC * BATCH), ALU.mult))
                    step(dve.tensor_scalar(bw[:, :], b_in[:, :], wsum[:, :], None, ALU.mult))
                    dve.tensor_reduce(mean_ctx[:, :, :], c3, AX.X, ALU.add).then_inc(averaged, 1)
                    dve.wait_ge(barred, 1)
                    for c in range(KC):
                        dve.tensor_scalar(xbar[:, c, :], px[:, c, :], bw[:, c:c + 1], None, ALU.add).then_inc(b_ready, 1)
                    dve.wait_ge(summed, 1)
                    dve.tensor_copy(summary[:, :], psm[:, :]).then_inc(s_ready, 1)
                    for g in range(NBLK):
                        dve.wait_ge(spread, g + 1)
                        dve.tensor_copy(G.y[:, g * TPB:(g + 1) * TPB, :], pspread[:, :, :]).then_inc(taken, 1)

                @block.tensor
                def _(pe):
                    pe.wait_ge(averaged, 1)
                    for c in range(KC):
                        for k in range(KC):
                            last = pe.matmul(px[:, c, :], w_in[:, k, c * P:(c + 1) * P], mean_ctx[:, k, :],
                                             start=(k == 0), stop=(k == KC - 1))
                    last.then_inc(barred, 1)
                    pe.wait_ge(b_ready, KC)
                    for k in range(KC):
                        pe.matmul(psm[:, :], xbar[:, k, :], w_out[:, k, :], start=(k == 0), stop=False)
                    pe.matmul(psm[:, :], row1[:, 0:BATCH], b_out[:, :], start=False, stop=True).then_inc(summed, 1)
                    pe.wait_ge(s_ready, 1)
                    for g in range(NBLK):
                        if g:
                            pe.wait_ge(taken, g)
                        for t in range(TPB):
                            tile = g * TPB + t
                            last = pe.matmul(pspread[:, t, :], of_seq[:, tile * P:(tile + 1) * P], summary[:, :],
                                             start=True, stop=True)
                        last.then_inc(spread, 1)
        N = Norm(st)
        step_sem, normed = st.sem("nstep"), st.sem("normed")
        with nc.Block() as block:
            @block.vector
            def _(dve):
                with dve.Fori(0, NBLK) as g:
                    step = Count(dve, step_sem, 17, g)
                    step(dve.tensor_tensor(N.s[:, :, :], G.x_tok[:, dyn(g, TPB), :], G.y[:, dyn(g, TPB), :], ALU.add))
                    normalise(dve, step, N, g, normed)
                    dve.wait_ge(normed, g + 1)
                    step(dve.tensor_tensor(N.s[:, :, :], N.s[:, :, :], rows(gamma[:, :], TPB), ALU.mult))
                    step(dve.tensor_tensor(G.y[:, dyn(g, TPB), :], N.s[:, :, :], rows(beta[:, :], TPB), ALU.add))
                    step.end()

            @block.scalar
            def _(act):
                with act.Fori(0, NBLK) as g:
                    norm_root(act, N, g)


MIXERS = {"a0": random_feature_attention, "x0": wkv, "f1": ternary_ffn, "x2": ema_summary}


def column(v):
    return np.ascontiguousarray(v.reshape(-1, P).T)


def block_ones(width, rows_=P, cols_=P, rw=None, value=1.0):
    rw = rw or width
    r, c = np.arange(rows_)[:, None] // rw, np.arange(cols_)[None, :] // width
    return np.where(r == c, value, 0.0).astype(np.float32)


def mixer_layouts(a, i):
    a["ones_row"] = np.ones((1, P), np.float32)
    a["ones_col"] = np.ones((P, 1), np.float32)
    a["all_ones"] = np.ones((P, P), np.float32)
    a["head_sum16"] = block_ones(16)
    HD = 16
    half = lambda m: m.reshape(-1, 2, HD // 2, *m.shape[1:])[:, ::-1].reshape(m.shape)
    W, B = ([i[f"L0_attn_{n}{m}"] for m in "qkv"] for n in ("W", "b"))
    a["a0_w"] = feature_major(np.concatenate([*W, half(W[0]), half(W[1]), W[2]], axis=0))
    a["a0_b"] = np.concatenate([*B, half(B[0]), half(B[1]), B[2]]).reshape(1, -1)
    a["a0_wo"], a["a0_bo"] = feature_major(i["L0_attn_Wo"]), i["L0_attn_bo"].reshape(1, D)
    inv = (1.0 / np.float32(10000.0) ** (np.arange(0, HD, 2, dtype=np.float32) / HD)).astype(np.float32)
    pos = (np.arange(P) % SEQ).astype(np.float32)
    ang = pos[:, None] * np.tile(inv, 2)[None, :]
    sign = np.where(np.arange(HD) < HD // 2, -1.0, 1.0).astype(np.float32)[None, :]
    a["a0_cos"], a["a0_sin"] = np.cos(ang).astype(np.float32), (np.sin(ang) * sign).astype(np.float32)
    a["a0_r"] = np.ascontiguousarray(i["L0_attn_rand_matrix"].T)
    a["x0_wu"] = np.ascontiguousarray(np.stack([column(i["L0_xattn_w"]), column(i["L0_xattn_u"])], axis=1))
    a["f1_w1"], a["f1_w2"] = feature_major(i["L1_ffn_w1"]), in_rows(i["L1_ffn_w2"].T)
    a["f1_b1"], a["f1_b2"] = column(i["L1_ffn_b1"]), i["L1_ffn_b2"].reshape(1, D)
    a["ctxT_rev"] = feature_major(i["ctx_2048"][:, ::-1].reshape(NTOK, D))
    a["x2_w_in"], a["x2_w_out"] = feature_major(i["L2_xattn_W_in"]), feature_major(i["L2_xattn_W_out"])
    a["x2_b_in"], a["x2_b_out"] = column(i["L2_xattn_b_in"]), i["L2_xattn_b_out"].reshape(1, D)
    a["x2_gamma"], a["x2_beta"] = i["L2_xattn_gamma"].reshape(1, D), i["L2_xattn_beta"].reshape(1, D)
    a["x2_decay"] = i["L2_xattn_decay"].reshape(1, 1)
    a["of_seq"] = np.repeat(np.eye(BATCH, dtype=np.float32), SEQ, axis=1)


def rms_heads_attention(nc, G, tag, d):
    H, HD, EPS = 32, 8, 1e-6
    HC = H // KC
    with Stage(nc, tag) as st:
        qn, kn, ctxT = st.sb("qn", [P, KC, NTOK]), st.sb("kn", [P, KC, NTOK]), st.sb("ctxT", [P, KC, NTOK])
        wq, wk, wv = (st.sb(m, [P, KC, D]) for m in ("wq", "wk", "wv"))
        head_sum, of_head = st.sb("head_sum", [P, P]), st.sb("of_head", [P, HC])
        load(nc, [(ctxT[:, :, :], d["ctxT"]), (wq[:, :, :], d["x1_wq"]), (wk[:, :, :], d["x1_wk"]), (wv[:, :, :], d["x1_wv"]),
                  (head_sum[:, :], d["head_sum8"]), (of_head[:, :], d["of_head8"])], st.sem("loaded"))
        with Stage(nc, tag + "n") as pt:
            sq = [pt.sb(f"sq{j}", [P, BLK]) for j in range(2)]
            pp = [pt.ps(f"pp{j}", [P, BLK]) for j in range(2)]
            pn = [pt.ps(f"pn{j}", [P, BLK]) for j in range(2)]
            projected, squared, summed, rooted, normed, nstep = (pt.sem(m) for m in (
                "projected", "squared", "summed", "rooted", "normed", "nstep"))
            with nc.Block() as block:
                @block.tensor
                def _(pe):
                    with pe.Fori(0, NBLK) as b:
                        for c in range(KC):
                            n = b * KC + c
                            pe.wait_ge(normed, n + 1)
                            for j, (w, src) in enumerate(((wq, G.xT), (wk, ctxT))):
                                for k in range(KC):
                                    last = pe.matmul(pp[j][:, :], w[:, k, c * P:(c + 1) * P], src[:, k, dyn(b, BLK)],
                                                     start=(k == 0), stop=(k == KC - 1))
                            last.then_inc(projected, 1)
                            pe.wait_ge(squared, n + 1)
                            for j in range(2):
                                last = pe.matmul(pn[j][:, :], head_sum[:, :], sq[j][:, :], start=True, stop=True)
                            last.then_inc(summed, 1)

                @block.scalar
                def _(act):
                    with act.Fori(0, NBLK) as b:
                        for c in range(KC):
                            n = b * KC + c
                            act.wait_ge(projected, n + 1)
                            act.activation(sq[0][:, :], pp[0][:, :], ACT.Square)
                            act.activation(sq[1][:, :], pp[1][:, :], ACT.Square).then_inc(squared, 1)
                            act.wait_ge(summed, n + 1)
                            act.activation(sq[0][:, :], pn[0][:, :], ACT.Sqrt, bias=EPS, scale=1.0 / HD)
                            act.activation(sq[1][:, :], pn[1][:, :], ACT.Sqrt, bias=EPS, scale=1.0 / HD).then_inc(rooted, 1)

                @block.vector
                def _(dve):
                    prime(dve, normed)
                    with dve.Fori(0, NBLK) as b:
                        step = Count(dve, nstep, 2 * KC, b)
                        for c in range(KC):
                            dve.wait_ge(rooted, b * KC + c + 1)
                            for j in range(2):
                                step(dve.reciprocal(sq[j][:, :], sq[j][:, :]))
                            dve.tensor_tensor(qn[:, c, dyn(b, BLK)], pp[0][:, :], sq[0][:, :], ALU.mult)
                            dve.tensor_tensor(kn[:, c, dyn(b, BLK)], pp[1][:, :], sq[1][:, :], ALU.mult).then_inc(normed, 1)
                        step.end()
        qt, kt, ct = (st.sb(m, [P, KC, P]) for m in ("qt", "kt", "ct"))
        qx = [[st.sb(f"qx{c}{s}", [P, HC, SEQ]) for s in range(2)] for c in range(KC)]
        prob = [st.sb(f"prob{c}", [P, HC, SEQ]) for c in range(KC)]
        vx, rec = st.sb("vx", [P, H, HD + 1]), st.sb("rec", [P, H])
        pS = [st.ps(f"pS{c}", [P, HC, SEQ]) for c in range(KC)]
        pV, pO = st.ps("pV", [P, D]), st.ps("pO", [P, H, HD + 1])
        copied, spread, v_made, scored, v_kept, exped, attended, done, ones_set, dstep = (st.sem(m) for m in (
            "copied", "spread", "v_made", "scored", "v_kept", "exped", "attended", "done", "ones_set", "dstep"))
        def tiles(eng, front, body):
            front(0)
            with eng.Fori(0, TILES - 1) as t:
                body(t, t + 1)
            body(TILES - 1, None)

        with nc.Block() as block:
            @block.scalar
            def _(act):
                def take_tile(m):
                    act.copy(qt[:, :, :], qn[:, :, dyn(m, P)])
                    act.copy(kt[:, :, :], kn[:, :, dyn(m, P)])
                    act.copy(ct[:, :, :], ctxT[:, :, dyn(m, P)]).then_inc(copied, 1)

                def body(t, m):
                    act.wait_ge(attended, t + 1)
                    for c in range(KC):
                        act.wait_ge(scored, t * KC + c + 1)
                        act.activation(prob[c][:, :, :], pS[c][:, :, :], ACT.Exp, scale=HD ** -0.5).then_inc(exped, 1)
                    if m is not None:
                        take_tile(m)

                tiles(act, take_tile, body)

            def spread_heads(eng, c, m):
                eng.wait_ge(copied, m + 1)
                for s in range(2):
                    q = rows(qt[:, c, s * SEQ:(s + 1) * SEQ], HC)
                    eng.tensor_tensor(qx[c][s][:, :, :], q, cols(of_head[:, :], SEQ), ALU.mult).then_inc(spread, 1)

            @block.gpsimd
            def _(pool):
                with pool.Fori(0, TILES) as t:
                    spread_heads(pool, 1, t)

            @block.vector
            def _(dve):
                def keep_v(m):
                    dve.wait_ge(v_made, m + 1)
                    dve.tensor_copy(vx[:, :, 0:HD], pV[:, :].rearrange("p (h e) -> p h e", e=HD)).then_inc(v_kept, 1)

                def front(m):
                    spread_heads(dve, 0, m)
                    keep_v(m)

                def body(t, m):
                    if m is not None:
                        spread_heads(dve, 0, m)
                    step = Count(dve, dstep, 1, t)
                    dve.wait_ge(attended, t + 2)
                    step(dve.reciprocal(rec[:, :], pO[:, :, HD]))
                    dve.tensor_tensor(G.y[:, dyn(t, 1), :].rearrange("p o (h e) -> p (o h) e", e=HD), pO[:, :, 0:HD],
                                      cols(rec[:, :], HD), ALU.mult).then_inc(done, 1)
                    step.end()
                    if m is not None:
                        keep_v(m)

                prime(dve, done)
                dve.memset(vx[:, :, HD:HD + 1], 1.0).then_inc(ones_set, 1)
                tiles(dve, front, body)

            @block.tensor
            def _(pe):
                def values(m):
                    pe.wait_ge(copied, m + 1)
                    for k in range(KC):
                        last = pe.matmul(pV[:, :], ct[:, k, :], wv[:, k, :], start=(k == 0), stop=(k == KC - 1))
                    last.then_inc(v_made, 1)

                def scores(m):
                    pe.wait_ge(spread, (m + 1) * 2 * KC)
                    for c in range(KC):
                        for s in range(2):
                            for h in range(0, HC, 8):
                                last = pe.matmul(pS[c][s * SEQ:(s + 1) * SEQ, h:h + 8, :], kt[:, c, s * SEQ:(s + 1) * SEQ],
                                                 qx[c][s][:, h:h + 8, :], start=True, stop=True)
                        last.then_inc(scored, 1)

                def front(m):
                    values(m)
                    scores(m)

                def body(t, m):
                    pe.wait_ge(v_kept, t + 1)
                    pe.wait_ge(done, t + 1)
                    for c in range(KC):
                        hold(pe, G, exped, t * KC + c + 1, pO[:, c * HC, 0:1])
                        for h in range(HC):
                            for s in range(2):
                                r = slice(s * SEQ, (s + 1) * SEQ)
                                last = pe.matmul(pO[r, c * HC + h, :], prob[c][r, h, :], vx[r, c * HC + h, :],
                                                 start=True, stop=True)
                    last.then_inc(attended, 1)
                    if m is not None:
                        values(m)
                        scores(m)

                prime(pe, attended)
                pe.wait_ge(ones_set, 1)
                tiles(pe, front, body)


def causal_attention(nc, G, tag, d):
    H, HD = 16, 16
    HC = H // KC
    SCALE = HD ** -0.5
    NAMES = ["wq", "wqr", "wk", "wkr"]
    with Stage(nc, tag) as st:
        qk = [st.sb(f"qk{j}", [P, KC, NTOK]) for j in range(2)]
        w = {m: st.sb(m, [P, KC, D]) for m in NAMES + ["wv", "wo"]}
        bias = st.sb("bias", [P, 4, KC])
        bv, bo, ones = st.sb("bv", [1, D]), st.sb("bo", [1, D]), st.sb("ones", [1, P])
        cos_t, sin_t = st.sb("cos", [P, SEQ]), st.sb("sin", [P, SEQ])
        of_head, hide = st.sb("of_head", [P, HC]), st.sb("hide", [P, SEQ])
        load(nc, [(w[m][:, :, :], d[f"a3_{m}"]) for m in w] +
             [(bias[:, :, :], d["a3_bias"]), (bv[:, :], d["a3_bv"]), (bo[:, :], d["a3_bo"]), (ones[:, :], d["ones_row"]),
              (cos_t[:, :], d["a3_cos"]), (sin_t[:, :], d["a3_sin"]), (of_head[:, :], d["of_head16"]),
              (hide[:, :], d["hide_later"])], st.sem("loaded"))
        with Stage(nc, tag + "r") as pt:
            rot = [pt.sb(f"rot{j}", [P, BLK]) for j in range(4)]
            pp = [pt.ps(f"pp{j}", [P, BLK]) for j in range(4)]
            projected, stored, rstep = pt.sem("projected"), pt.sem("stored"), pt.sem("rstep")
            with nc.Block() as block:
                @block.tensor
                def _(pe):
                    with pe.Fori(0, NBLK) as b:
                        for c in range(KC):
                            pe.wait_ge(stored, b * KC + c + 1)
                            for j, m in enumerate(NAMES):
                                for k in range(KC):
                                    last = pe.matmul(pp[j][:, :], w[m][:, k, c * P:(c + 1) * P], G.xT[:, k, dyn(b, BLK)],
                                                     start=(k == 0), stop=(k == KC - 1))
                            last.then_inc(projected, 1)

                @block.vector
                def _(dve):
                    prime(dve, stored)
                    with dve.Fori(0, NBLK) as b:
                        step = Count(dve, rstep, 8, b)
                        for c in range(KC):
                            dve.wait_ge(projected, b * KC + c + 1)
                            for j in range(4):
                                step(dve.scalar_tensor_tensor(
                                    rot[j][:, :].rearrange("p (s t) -> p s t", t=SEQ),
                                    pp[j][:, :].rearrange("p (s t) -> p s t", t=SEQ), bias[:, j, c:c + 1],
                                    rows((sin_t if j % 2 else cos_t)[:, :], BLK // SEQ), ALU.add, ALU.mult))
                            dve.tensor_tensor(qk[0][:, c, dyn(b, BLK)], rot[0][:, :], rot[1][:, :], ALU.add)
                            dve.tensor_tensor(qk[1][:, c, dyn(b, BLK)], rot[2][:, :], rot[3][:, :], ALU.add).then_inc(stored, 1)
                        step.end()
        qt, kt, xt, xs = (st.sb(m, [P, KC, P]) for m in ("qt", "kt", "xt", "xs"))
        kx = [[st.sb(f"kx{c}{s}", [P, HC, SEQ]) for s in range(2)] for c in range(KC)]
        S, E, ET = st.sb("S", [P, H, SEQ]), st.sb("E", [P, H, SEQ]), st.sb("ET", [P, H // 2, P])
        v, o, oT = st.sb("v", [P, 2, D]), st.sb("o", [P, D]), st.sb("oT", [P, KC, P])
        mx, den = st.sb("mx", [P, H]), st.sb("den", [P, H])
        pS, pV, pT = st.ps("pS", [P, H, SEQ]), st.ps("pV", [P, 2, D]), st.ps("pT", [P, H // 2, P])
        pO, last_bank = st.ps("pO", [P, 2 * BLK]), st.ps("pOT_Y", [P, 2, D])
        pO_of = lambda h: pO[:, (h % 2) * BLK + (h // 2) * HD:(h % 2) * BLK + (h // 2 + 1) * HD]
        pOT, pY = last_bank[:, 0, :].rearrange("p (c m) -> p c m", c=KC), last_bank[:, 1, :]
        names = ["copied", "spread", "scored", "v_made", "v_kept", "shifted", "exped", "turned", "et_kept", "attended",
                 "o_ready", "o_turned", "ot_kept", "y_made", "done", "dstep"]
        z = {m: st.sem(m) for m in names}

        def tiles(eng, front, body):
            front(0)
            with eng.Fori(0, TILES - 1) as t:
                body(t, t + 1)
            body(TILES - 1, None)

        with nc.Block() as block:
            @block.scalar
            def _(act):
                def take_tile(m):
                    act.copy(qt[:, :, :], qk[0][:, :, dyn(m, P)])
                    act.copy(kt[:, :, :], qk[1][:, :, dyn(m, P)])
                    act.copy(xt[:, :, :], G.xT[:, :, dyn(m, P)])
                    act.copy(xs[:, :, 0:SEQ], G.xT[:, :, dyn(m * 2 + 1, SEQ)])
                    act.copy(xs[:, :, SEQ:P], G.xT[:, :, dyn(m * 2, SEQ)]).then_inc(z["copied"], 1)

                def keep_v(m):
                    act.wait_ge(z["v_made"], m + 1)
                    act.copy(v[:, :, :], pV[:, :, :]).then_inc(z["v_kept"], 1)

                def exp(m):
                    act.wait_ge(z["shifted"], m + 1)
                    act.activation(E[:, :, :], S[:, :, :], ACT.Exp).then_inc(z["exped"], 1)

                def front(m):
                    take_tile(m)
                    keep_v(m)
                    exp(m)

                def body(t, m):
                    act.wait_ge(z["turned"], t + 1)
                    act.copy(ET[:, :, :], pT[:, :, :]).then_inc(z["et_kept"], 1)
                    if m is not None:
                        take_tile(m)
                        act.wait_ge(z["attended"], t + 1)
                        keep_v(m)
                    act.wait_ge(z["o_turned"], t + 1)
                    act.copy(oT[:, :, :], pOT).then_inc(z["ot_kept"], 1)
                    act.wait_ge(z["y_made"], t + 1)
                    act.copy(G.y[:, dyn(t, 1), :], pY.rearrange("p (o e) -> p o e", o=1)).then_inc(z["done"], 1)
                    if m is not None:
                        exp(m)

                prime(act, z["done"])
                tiles(act, front, body)

            @block.gpsimd
            def _(pool):
                with pool.Fori(0, TILES) as t:
                    pool.wait_ge(z["copied"], t + 1)
                    pool.wait_ge(z["scored"], t + 1)
                    for c in range(KC):
                        for s in range(2):
                            pool.tensor_tensor(kx[c][s][:, :, :], rows(kt[:, c, s * SEQ:(s + 1) * SEQ], HC),
                                               cols(of_head[:, :], SEQ), ALU.mult).then_inc(z["spread"], 1)

            @block.vector
            def _(dve):
                def shift(m):
                    step = Count(dve, z["dstep"], 4, m)
                    dve.wait_ge(z["scored"], m + 2)
                    step(dve.scalar_tensor_tensor(S[:, :, :], pS[:, :, :], SCALE, rows(hide[:, :], H), ALU.mult, ALU.add))
                    step(dve.tensor_reduce(mx[:, :], S[:, :, :], AX.X, ALU.max))
                    dve.tensor_tensor(S[:, :, :], S[:, :, :], cols(mx[:, :], SEQ), ALU.subtract).then_inc(z["shifted"], 1)

                def body(t, m):
                    step = Count(dve, z["dstep"], 4, t)
                    step.n = 2
                    dve.wait_ge(z["exped"], t + 1)
                    step(dve.tensor_reduce(den[:, :], E[:, :, :], AX.X, ALU.add))
                    step(dve.reciprocal(den[:, :], den[:, :]))
                    step.end()
                    dve.wait_ge(z["attended"], t + 1)
                    for odd in range(2):
                        part = pO[:, odd * BLK:odd * BLK + H // 2 * HD].rearrange("p (h e) -> p h e", e=HD)
                        scale = cols(den[:, :].rearrange("p (h two) -> p h two", two=2)[:, :, odd], HD)
                        last = dve.tensor_tensor(o[:, :].rearrange("p (h two e) -> p h two e", two=2, e=HD)[:, :, odd, :],
                                                 part, scale, ALU.mult)
                    last.then_inc(z["o_ready"], 1)
                    if m is not None:
                        shift(m)

                tiles(dve, shift, body)

            @block.tensor
            def _(pe):
                def values(m):
                    pe.wait_ge(z["copied"], m + 1)
                    for j, src in enumerate((xt, xs)):
                        for k in range(KC):
                            pe.matmul(pV[:, j, :], src[:, k, :], w["wv"][:, k, :], start=(k == 0), stop=False)
                        last = pe.matmul(pV[:, j, :], ones[:, :], bv[:, :], start=False, stop=True)
                    last.then_inc(z["v_made"], 1)

                def scores(m):
                    pe.wait_ge(z["spread"], (m + 1) * 2 * KC)
                    for c in range(KC):
                        for s in range(2):
                            last = pe.matmul(pS[s * SEQ:(s + 1) * SEQ, c * HC:(c + 1) * HC, :],
                                             qt[:, c, s * SEQ:(s + 1) * SEQ], kx[c][s][:, :, :], start=True, stop=True)
                    last.then_inc(z["scored"], 1)

                def front(m):
                    values(m)
                    scores(m)

                def body(t, m):
                    pe.wait_ge(z["exped"], t + 1)
                    for hh in range(H // 2):
                        last = pe.transpose(pT[:, hh, :], E[:, 2 * hh:2 * hh + 2, :], G.ident[:, :])
                    last.then_inc(z["turned"], 1)
                    pe.wait_ge(z["v_kept"], t + 1)
                    pe.wait_ge(z["done"], t + 1)
                    if m is not None:
                        values(m)
                    hold(pe, G, z["et_kept"], t + 1, pO[:, 0:1])
                    for h in range(H):
                        for s in range(2):
                            r = slice((h % 2) * SEQ, (h % 2 + 1) * SEQ)
                            last = pe.matmul(pO_of(h)[s * SEQ:(s + 1) * SEQ, :], ET[r, h // 2, s * SEQ:(s + 1) * SEQ],
                                             v[r, int(h % 2 != s), h * HD:(h + 1) * HD], start=True, stop=True)
                    last.then_inc(z["attended"], 1)
                    if m is not None:
                        scores(m)
                    pe.wait_ge(z["o_ready"], t + 1)
                    for c in range(KC):
                        last = pe.transpose(pOT[:, c, :], o[:, c * P:(c + 1) * P], G.ident[:, :])
                    last.then_inc(z["o_turned"], 1)
                    pe.wait_ge(z["ot_kept"], t + 1)
                    for c in range(KC):
                        pe.matmul(pY, oT[:, c, :], w["wo"][:, c, :], start=(c == 0), stop=False)
                    pe.matmul(pY, ones[:, :], bo[:, :], start=False, stop=True).then_inc(z["y_made"], 1)

                prime(pe, z["scored"])
                tiles(pe, front, body)


def feature_attention(nc, G, tag, d):
    HD, H = 8, 8
    SCALE = HD ** -0.5
    AUG = SEQ + H
    WIDE = P + HD
    with Stage(nc, tag) as st:
        ctxT, ctx = st.sb("ctxT", [P, KC, NTOK]), st.sb("ctx", [P, TILES, D])
        of_head, minus_head = st.sb("of_head", [P, H]), st.sb("minus_head", [AUG, H])
        load(nc, [(ctxT[:, :, :], d["ctxT"]), (ctx[:, :, :], d["ctx_tok"]), (of_head[:, :], d["x3_of_head"]),
                  (minus_head[:, :], d["x3_minus_head"])], st.sem("loaded"))
        xt, kmask = st.sb("xt", [P, D]), st.sb("kmask", [P, H, D])
        kaug = [st.sb(f"kaug{s}", [AUG, D]) for s in range(2)]
        qaug = [st.sb(f"qaug{s}", [AUG, H, D]) for s in range(2)]
        vx = [[st.sb(f"vx{s}{c}", [P, H * WIDE]) for c in range(KC)] for s in range(2)]
        mx = st.sb("mx", [P, 2 * KC, P])
        prob = [[st.sb(f"prob{s}{c}", [P, H, D]) for c in range(KC)] for s in range(2)]
        rec = [st.sb(f"rec{s}", [SEQ, D]) for s in range(2)]
        pX, pS = st.ps("pX", [P, 4, D]), [st.ps(f"pS{u}", [P, 4, D]) for u in range(2)]
        pM, pO = st.ps("pM", [P, 2 * KC, P]), st.ps("pO", [P, 2, D])
        names = ["set_up", "x_here", "k_ready", "v_ready", "q_ready", "scored", "maxed", "m_turned", "aug_ready", "exped",
                 "shifted", "attended", "done", "dstep", "k_masked"]
        z = {m: st.sem(m) for m in names}
        with nc.Block() as block:
            @block.vector
            def _(dve):
                for s in range(2):
                    dve.memset(kaug[s][SEQ:AUG, :], 1.0)
                    for c in range(KC):
                        dve.memset(vx[s][c][:, :], 0.0)
                dve.memset(mx[:, :, :], 0.0).then_inc(z["set_up"], 1)
                dve.wait_ge(z["set_up"], 1)
                for s in range(2):
                    for c in range(KC):
                        v = vx[s][c][:, :].rearrange("p (h q) -> p h q", q=WIDE)
                        dve.memset(v[:, :, SEQ:SEQ + HD], 1.0)

        parts = [(j // 4, (j // 2) % 2, j % 2) for j in range(8)]

        def tiles(eng, front, body):
            front(0)
            with eng.Fori(0, TILES - 1) as t:
                body(t, t + 1)
            body(TILES - 1, None)

        with nc.Block() as block:
            @block.gpsimd
            def _(pool):
                def values(m):
                    for s in range(2):
                        for c in range(KC):
                            v = vx[s][c][:, :].rearrange("p (h q) -> p h q", q=WIDE)[:, :, 0:HD]
                            src = ctxT[:, c, dyn(m * 2 + s, SEQ)].rearrange("p (h e) -> p h e", e=HD)
                            pool.tensor_copy(v, src).then_inc(z["v_ready"], 1)
                    pool.wait_ge(z["v_ready"], m * 4 + 4)

                def queries(m):
                    pool.wait_ge(z["x_here"], m + 1)
                    for s in range(2):
                        r = slice(s * SEQ, (s + 1) * SEQ)
                        pool.tensor_tensor(qaug[s][0:SEQ, :, :], rows(xt[r, :], H), cols(of_head[r, :], D),
                                           ALU.mult).then_inc(z["q_ready"], 1)
                        pool.wait_ge(z["q_ready"], m * 2 + s + 1)

                def front(m):
                    values(m)
                    queries(m)

                def body(t, m):
                    if m is None:
                        return
                    pool.wait_ge(z["shifted"], t * 8 + 8)
                    queries(m)
                    pool.wait_ge(z["attended"], t + 1)
                    values(m)

                tiles(pool, front, body)

            @block.scalar
            def _(act):
                def take_x(m):
                    act.copy(xt[:, :].rearrange("p (o m) -> p o m", o=1), G.x_tok[:, dyn(m, 1), :]).then_inc(z["x_here"], 1)

                def take_keys(m):
                    for s in range(2):
                        act.copy(kaug[s][0:SEQ, :].rearrange("p (o m) -> p o m", o=1),
                                 ctx[s * SEQ:(s + 1) * SEQ, dyn(m, 1), :]).then_inc(z["k_ready"], 1)

                def front(m):
                    take_x(m)
                    take_keys(m)

                def body(t, m):
                    if m is not None:
                        act.wait_ge(z["q_ready"], t * 2 + 2)
                        act.wait_ge(z["scored"], t * 8 + 8)
                        take_x(m)
                    for j, (s, c, half) in enumerate(parts):
                        act.wait_ge(z["shifted"], t * 8 + j + 1)
                        act.activation(prob[s][c][:, half * 4:half * 4 + 4, :], pS[j % 2][:, :, :], ACT.Exp,
                                       scale=SCALE).then_inc(z["exped"], 1)
                    if m is not None:
                        take_keys(m)

                tiles(act, front, body)

            @block.vector
            def _(dve):
                prime(dve, z["done"])

                def key_masks(m):
                    dve.tensor_tensor(kmask[:, :, :], ctx[:, dyn(m, 1), :].to_broadcast([P, H, D]),
                                      cols(of_head[:, :], D), ALU.mult).then_inc(z["k_masked"], 1)

                def maxima(m):
                    for j, (s, c, half) in enumerate(parts):
                        dve.wait_ge(z["scored"], m * 8 + j + 1)
                        dve.tensor_reduce(mx[:, j // 2, SEQ + half * 4:SEQ + half * 4 + 4], pX[:, :, :], AX.X,
                                          ALU.max).then_inc(z["maxed"], 1)
                    dve.wait_ge(z["m_turned"], m + 1)
                    for s in range(2):
                        turned = pM[SEQ:AUG, s * KC:(s + 1) * KC, :].rearrange("p c m -> p (c m)")
                        dve.tensor_tensor(qaug[s][SEQ:AUG, :, :], rows(turned, H), cols(minus_head[SEQ:AUG, :], D),
                                          ALU.mult).then_inc(z["aug_ready"], 1)

                def body(t, m, following):
                    if m is not None:
                        maxima(m)
                    if following is not None:
                        key_masks(following)
                    step = Count(dve, z["dstep"], 2, t)
                    dve.wait_ge(z["attended"], t + 1)
                    for s in range(2):
                        step(dve.reciprocal(rec[s][:, :], pO[SEQ:P, s, :]))
                    for s in range(2):
                        last = dve.tensor_tensor(G.y[s * SEQ:(s + 1) * SEQ, dyn(t, 1), :],
                                                 pO[0:SEQ, s:s + 1, :], rec[s][:, :].rearrange("p (o m) -> p o m", o=1),
                                                 ALU.mult)
                    last.then_inc(z["done"], 1)
                    step.end()

                key_masks(0)
                maxima(0)
                key_masks(1)
                with dve.Fori(0, TILES - 2) as t:
                    body(t, t + 1, t + 2)
                body(TILES - 2, TILES - 1, None)
                body(TILES - 1, None, None)

            @block.tensor
            def _(pe):
                def scores(m, j):
                    s, c, half = parts[j]
                    if j == 0:
                        pe.wait_ge(z["x_here"], m + 1)
                        pe.wait_ge(z["k_masked"], m + 1)
                    else:
                        pe.wait_ge(z["maxed"], m * 8 + j)
                    r = slice(s * SEQ, (s + 1) * SEQ)
                    for hh in range(2):
                        h = half * 4 + hh * 2
                        last = pe.matmul(pX[:, hh * 2:hh * 2 + 2, :], xt[r, c * P:(c + 1) * P],
                                         kmask[r, h:h + 2, :], start=True, stop=True)
                    last.then_inc(z["scored"], 1)

                def turn_maxima(m):
                    pe.wait_ge(z["maxed"], m * 8 + 8)
                    for g in range(2 * KC):
                        last = pe.transpose(pM[:, g, :], mx[:, g, :], G.ident[:, :])
                    last.then_inc(z["m_turned"], 1)

                def shifted_scores(t, j):
                    s, c, half = parts[j]
                    if j == 0:
                        pe.wait_ge(z["aug_ready"], t * 2 + 2)
                        pe.wait_ge(z["q_ready"], t * 2 + 2)
                        pe.wait_ge(z["k_ready"], t * 2 + 2)
                    if j >= 2:
                        pe.wait_ge(z["exped"], t * 8 + j - 1)
                    for hh in range(2):
                        h = half * 4 + hh * 2
                        last = pe.matmul(pS[j % 2][:, hh * 2:hh * 2 + 2, :], kaug[s][:, c * P:(c + 1) * P],
                                         qaug[s][:, h:h + 2, :], start=True, stop=True)
                    last.then_inc(z["shifted"], 1)

                def front(m):
                    for j in range(8):
                        scores(m, j)
                    turn_maxima(m)

                def body(t, m):
                    for j in range(8):
                        shifted_scores(t, j)
                        if m is not None and j >= 1:
                            scores(m, j - 1)
                    if m is not None:
                        scores(m, 7)
                        turn_maxima(m)
                    pe.wait_ge(z["exped"], t * 8 + 8)
                    pe.wait_ge(z["v_ready"], t * 4 + 4)
                    pe.wait_ge(z["done"], t + 1)
                    for s in range(2):
                        for c in range(KC):
                            for h in range(H):
                                last = pe.matmul(pO[:, s, :], vx[s][c][:, h * P:(h + 1) * P], prob[s][c][:, h, :],
                                                 start=(c == 0 and h == 0), stop=(c == KC - 1 and h == H - 1))
                    last.then_inc(z["attended"], 1)

                tiles(pe, front, body)


MIXERS.update({"x1": rms_heads_attention, "a3": causal_attention, "x3": feature_attention})


def more_layouts(a, i):
    a["head_sum8"] = block_ones(8)
    a["of_head8"] = block_ones(1, P, 16, rw=8)
    a["of_head16"] = block_ones(1, P, 8, rw=16)
    both = np.concatenate([i["L1_xattn_Wk"], i["L1_xattn_Wv"]], axis=0)
    a["x1_wq"], a["x1_wk"], a["x1_wv"] = (feature_major(w) for w in (i["L1_xattn_Wq"], both[0::2], both[1::2]))
    pair = np.arange(256).reshape(-1, 2)[:, ::-1].reshape(-1)
    wq, bq, wk, bk = (i[f"L3_attn_{m}"] for m in ("Wq", "bq", "Wk", "bk"))
    for n, w in (("wq", wq), ("wqr", wq[pair]), ("wk", wk), ("wkr", wk[pair]), ("wv", i["L3_attn_Wv"]), ("wo", i["L3_attn_Wo"])):
        a[f"a3_{n}"] = feature_major(w)
    a["a3_bias"] = np.ascontiguousarray(np.stack([column(b) for b in (bq, bq[pair], bk, bk[pair])], axis=1))
    a["a3_bv"], a["a3_bo"] = i["L3_attn_bv"].reshape(1, D), i["L3_attn_bo"].reshape(1, D)
    inv = np.float32(10000.0) ** (-np.arange(0, 16, 2, dtype=np.float32) / 16)
    ang = np.arange(SEQ, dtype=np.float32)[None, :] * inv.astype(np.float32)[(np.arange(P) % 16) // 2][:, None]
    sign = np.where(np.arange(P) % 2 == 0, -1.0, 1.0).astype(np.float32)[:, None]
    a["a3_cos"], a["a3_sin"] = np.cos(ang).astype(np.float32), (np.sin(ang) * sign).astype(np.float32)
    pos = np.arange(P) % SEQ
    a["hide_later"] = np.where(np.arange(SEQ)[None, :] > pos[:, None], -1e30, 0.0).astype(np.float32)
    a["x3_of_head"] = (pos[:, None] // 8 == np.arange(8)[None, :]).astype(np.float32)
    m = np.zeros((SEQ + 8, 8), np.float32)
    m[SEQ:] = -np.eye(8, dtype=np.float32)
    a["x3_minus_head"] = m


def slot_attention(nc, G, tag, d):
    H, DK, DV, M = 16, 64, 128, 64
    HP = H // 2
    PROBS = TPB * 2
    PASSES = HP * NBLK
    FRONT_STEPS, BACK_STEPS = 6, 2
    EPS = 1e-5
    CLAMP = 32.0
    with Stage(nc, tag) as st:
        w = st.sb("w", [P, KC, 3 * P + 4 * P])
        wo = st.sb("wo", [P, 2, D])
        tri, qmask, gain = st.sb("tri", [P, P]), st.sb("qmask", [P, P]), st.sb("gain", [P, DV])
        load(nc, [(tri[:, :], d["causal_T"]), (qmask[:, :], d["causal_T_scaled"]),
                  (gain[:, :], d["a2_gain"].to_broadcast([P, DV]))], st.sem("loaded"))
        xt = st.sb("xt", [P, KC, BLK])
        qT, kT, esT = st.sb("qT", [P, BLK]), st.sb("kT", [P, BLK]), st.sb("esT", [P, BLK])
        es = st.sb("es", [P, TPB, P])
        v, gate = st.sb("v", [P, TPB, 2 * DV]), st.sb("gate", [P, TPB, 2 * DV])
        A, B = st.sb("A", [P, PROBS, P]), st.sb("B", [P, PROBS, P])
        rz, ok = st.sb("rz", [P, PROBS, M]), st.sb("ok", [P, PROBS, M])
        pzT, top, stat = st.sb("pzT", [P, TPB, P]), st.sb("top", [P, PROBS]), st.sb("stat", [P, PROBS])
        o, sq, oT = st.sb("o", [P, PROBS, DV]), st.sb("sq", [P, PROBS, DV]), st.sb("oT", [P, PROBS, P])
        b0, b1, b2, b3 = (st.ps(f"b{j}", [P, BLK]) for j in range(4))
        w0, w1 = st.ps("w0", [P, 2 * BLK]), st.ps("w1", [P, 2 * BLK])
        names = ("w_here", "wo_here", "copied", "projected", "qk_kept", "clipped", "es_ready", "es_turned", "es_kept", "a_made",
                 "a_ready", "ok_made", "shifted", "exped", "pz_ready", "pz_turned", "pz_kept", "v_made", "v_kept", "g_made",
                 "gate_kept", "b_made", "b_ready", "o_made", "o_taken", "gated", "squared", "var_ready", "rooted", "o_ready",
                 "o_turned", "ot_kept", "y_made", "done", "y_zero", "front_step", "back_step")
        z = {m: st.sem(m) for m in names}
        w8 = lambda ap, n: ap.rearrange("p (j n) -> p j n", n=n)

        def passes(eng, front_only, body):
            front_only()
            with eng.Fori(0, PASSES - 1) as n:
                body(n, n + 1)
            body(PASSES - 1, None)

        with nc.Block() as block:
            @block.sync
            def _(sp):
                with sp.Fori(0, HP) as hp:
                    sp.wait_ge(z["g_made"], hp * NBLK + 1)
                    sp.dma_start(w[:, :, :], d["a2_w"][dyn(hp, 1)].rearrange("o p k n -> (o p) k n")).then_inc(z["w_here"], 16)
                    sp.wait_ge(z["y_made"], hp * NBLK + 1)
                    sp.dma_start(wo[:, :, :], d["a2_wo"][dyn(hp, 1)].rearrange("o p k n -> (o p) k n")).then_inc(z["wo_here"], 16)

            @block.scalar
            def _(act):
                prime(act, z["ot_kept"])

                def copy_x(m):
                    act.wait_ge(z["g_made"], m + 1)
                    act.copy(xt[:, :, :], G.xT[:, :, dyn(m % NBLK, BLK)]).then_inc(z["copied"], 1)

                def keep_projected(m):
                    act.wait_ge(z["projected"], m + 1)
                    act.copy(qT[:, :], b0[:, :])
                    act.copy(kT[:, :], b1[:, :]).then_inc(z["qk_kept"], 1)
                    act.wait_ge(z["clipped"], m + 1)
                    act.activation(esT[:, :], esT[:, :], ACT.Exp).then_inc(z["es_ready"], 1)
                    act.wait_ge(z["es_turned"], m + 1)
                    act.copy(es[:, :, :], w8(b3[:, :], P)).then_inc(z["es_kept"], 1)

                def exp_ok(m):
                    act.wait_ge(z["shifted"], m + 1)
                    act.activation(ok[:, :, :], ok[:, :, :], ACT.Exp).then_inc(z["exped"], 1)

                def keep_v(m):
                    act.wait_ge(z["v_made"], m + 1)
                    act.copy(v[:, :, :], w8(w0[:, :], 2 * DV)).then_inc(z["v_kept"], 1)

                def keep_gate(m):
                    act.wait_ge(z["g_made"], m + 2)
                    act.activation(gate[:, :, :], w8(w1[:, :], 2 * DV), ACT.Silu).then_inc(z["gate_kept"], 1)

                def front_only():
                    copy_x(0)
                    keep_projected(0)
                    exp_ok(0)
                    keep_v(0)
                    keep_gate(0)

                def body(n, m):
                    f = m is not None
                    if f:
                        copy_x(m)
                    act.wait_ge(z["pz_turned"], n + 1)
                    act.copy(pzT[:, :, :], w8(b3[:, :], P)).then_inc(z["pz_kept"], 1)
                    if f:
                        keep_projected(m)
                    act.wait_ge(z["o_made"], n + 1)
                    act.activation(sq[:, :, :], w8(w1[:, :], DV), ACT.Square).then_inc(z["squared"], 1)
                    act.wait_ge(z["var_ready"], n + 1)
                    act.activation(stat[:, :], stat[:, :], ACT.Sqrt).then_inc(z["rooted"], 1)
                    if f:
                        keep_v(m)
                        act.wait_ge(z["gated"], n + 1)
                        keep_gate(m)
                    act.wait_ge(z["o_turned"], n + 1)
                    act.copy(oT[:, :, :], w8(w0[:, :], P)).then_inc(z["ot_kept"], 1)
                    if f:
                        exp_ok(m)

                passes(act, front_only, body)

            @block.vector
            def _(dve):
                prime(dve, z["done"])
                dve.memset(G.y[:, :, :], 0.0).then_inc(z["y_zero"], 1)
                dve.wait_ge(z["y_zero"], 1)

                def clip(m):
                    dve.tensor_scalar(esT[:, :], b2[:, :], CLAMP, -CLAMP, ALU.min, ALU.max).then_inc(z["clipped"], 1)

                def mask_A(m):
                    dve.wait_ge(z["a_made"], m + 1)
                    dve.tensor_tensor(A[:, :, :], w8(w0[:, :], P), rows(qmask[:, :], PROBS), ALU.mult).then_inc(z["a_ready"], 1)

                def invert_z(m, step):
                    dve.wait_ge(z["ok_made"], m + 1)
                    step(dve.reciprocal(rz[:, :, :], w8(b1[:, :], M)))

                def shift_ok(m, step):
                    step(dve.tensor_tensor(ok[:, :, :], w8(b0[:, :], M), rz[:, :, :], ALU.mult))
                    step(dve.tensor_reduce(top[:, :], ok[:, :, :], AX.X, ALU.max))
                    dve.tensor_tensor(ok[:, :, :], ok[:, :, :], cols(top[:, :], M), ALU.subtract).then_inc(z["shifted"], 1)

                def softmax_ok(m, step):
                    dve.wait_ge(z["exped"], m + 1)
                    step(dve.tensor_reduce(top[:, :], ok[:, :, :], AX.X, ALU.add))
                    step(dve.reciprocal(top[:, :], top[:, :]))
                    step(dve.tensor_tensor(ok[:, :, :], ok[:, :, :], rz[:, :, :], ALU.mult))
                    dve.tensor_tensor(ok[:, :, :], ok[:, :, :], cols(top[:, :], M), ALU.mult).then_inc(z["pz_ready"], 1)

                def front_only():
                    step = Count(dve, z["front_step"], FRONT_STEPS, 0)
                    dve.wait_ge(z["projected"], 1)
                    clip(0)
                    mask_A(0)
                    invert_z(0, step)
                    shift_ok(0, step)
                    softmax_ok(0, step)
                    step.end()

                def body(n, m):
                    f = m is not None
                    step = Count(dve, z["front_step"], FRONT_STEPS, m) if f else None
                    back = Count(dve, z["back_step"], BACK_STEPS, n)
                    dve.wait_ge(z["b_made"], n + 1)
                    if f:
                        clip(m)
                    dve.tensor_tensor(B[:, :, :], w8(w0[:, :], P), rows(tri[:, :], PROBS), ALU.mult).then_inc(z["b_ready"], 1)
                    if f:
                        mask_A(m)
                    dve.wait_ge(z["squared"], n + 1)
                    dve.tensor_tensor(o[:, :, :], w8(w1[:, :], DV), rows(gain[:, :], PROBS), ALU.mult).then_inc(z["o_taken"], 1)
                    dve.wait_ge(z["o_taken"], n + 1)
                    o4 = o[:, :, :].rearrange("p (h t) e -> p h t e", h=2)
                    dve.tensor_tensor(o4, o4, gate[:, :, :].rearrange("p t (h e) -> p h t e", e=DV), ALU.mult).then_inc(z["gated"], 1)
                    back(dve.tensor_reduce(stat[:, :], sq[:, :, :], AX.X, ALU.add))
                    dve.tensor_scalar(stat[:, :], stat[:, :], 1.0 / DV, EPS, ALU.mult, ALU.add).then_inc(z["var_ready"], 1)
                    if f:
                        invert_z(m, step)
                    dve.wait_ge(z["rooted"], n + 1)
                    back(dve.reciprocal(stat[:, :], stat[:, :]))
                    dve.wait_ge(z["gated"], n + 1)
                    dve.tensor_tensor(o[:, :, :], o[:, :, :], cols(stat[:, :], DV), ALU.mult).then_inc(z["o_ready"], 1)
                    back.end()
                    if f:
                        shift_ok(m, step)
                        softmax_ok(m, step)
                        step.end()
                    dve.wait_ge(z["y_made"], n + 2)
                    y = G.y[:, dyn(n % NBLK, TPB), :]
                    dve.tensor_tensor(y, y, w8(w1[:, :], D), ALU.add).then_inc(z["done"], 1)

                passes(dve, front_only, body)

            @block.tensor
            def _(pe):
                prime(pe, z["g_made"], z["y_made"])

                def project(m):
                    pe.wait_ge(z["w_here"], (m // NBLK) * 16 + 16)
                    pe.wait_ge(z["copied"], m + 1)
                    for j, out in enumerate((b0, b1, b2)):
                        for k in range(KC):
                            last = pe.matmul(out[:, :], w[:, k, j * P:(j + 1) * P], xt[:, k, :],
                                             start=(k == 0), stop=(k == KC - 1))
                    last.then_inc(z["projected"], 1)

                def turn_es(m):
                    pe.wait_ge(z["es_ready"], m + 1)
                    for t in range(TPB):
                        last = pe.transpose(b3[:, t * P:(t + 1) * P], esT[:, t * P:(t + 1) * P], G.ident[:, :])
                    last.then_inc(z["es_turned"], 1)

                def make_A(m):
                    pe.wait_ge(z["qk_kept"], m + 1)
                    for t in range(TPB):
                        c = slice(t * P, (t + 1) * P)
                        for h in range(2):
                            r, j = slice(h * DK, (h + 1) * DK), h * TPB + t
                            last = pe.matmul(w0[:, j * P:(j + 1) * P], kT[r, c], qT[r, c], start=True, stop=True)
                    last.then_inc(z["a_made"], 1)

                def make_ok(m):
                    pe.wait_ge(z["es_kept"], m + 1)
                    pe.wait_ge(z["a_ready"], m + 1)
                    for t in range(TPB):
                        for h in range(2):
                            j = 2 * t + h
                            pe.matmul(b0[:, j * M:(j + 1) * M], A[:, h * TPB + t, :], es[:, t, h * M:(h + 1) * M], start=True, stop=True)
                    pe.matmul(b1[:, :], tri[:, :], es[:, :, :], start=True, stop=True).then_inc(z["ok_made"], 1)

                def token_major(at, out, signal):
                    for t in range(TPB):
                        for k in range(KC):
                            last = pe.matmul(out[:, t * 2 * DV:(t + 1) * 2 * DV], xt[:, k, t * P:(t + 1) * P],
                                             w[:, k, at:at + 2 * DV], start=(k == 0), stop=(k == KC - 1))
                    last.then_inc(signal, 1)

                def front_only():
                    project(0)
                    turn_es(0)
                    make_A(0)
                    make_ok(0)
                    token_major(3 * P, w0, z["v_made"])
                    token_major(5 * P, w1, z["g_made"])

                def body(n, m):
                    f = m is not None
                    pe.wait_ge(z["pz_ready"], n + 1)
                    for t in range(TPB):
                        last = pe.transpose(b3[:, t * P:(t + 1) * P], ok[:, 2 * t:2 * t + 2, :], G.ident[:, :])
                    last.then_inc(z["pz_turned"], 1)
                    if f:
                        project(m)
                    pe.wait_ge(z["pz_kept"], n + 1)
                    pe.wait_ge(z["v_kept"], n + 1)
                    pe.wait_ge(z["ot_kept"], n + 1)
                    for t in range(TPB):
                        c = slice(t * P, (t + 1) * P)
                        for h in range(2):
                            r, j = slice(h * M, (h + 1) * M), h * TPB + t
                            last = pe.matmul(w0[:, j * P:(j + 1) * P], esT[r, c], pzT[r, t, :], start=True, stop=True)
                    last.then_inc(z["b_made"], 1)
                    if f:
                        turn_es(m)
                    pe.wait_ge(z["b_ready"], n + 1)
                    if f:
                        make_A(m)
                    pe.wait_ge(z["gate_kept"], n + 1)
                    pe.wait_ge(z["done"], n + 1)
                    for j in range(PROBS):
                        last = pe.matmul(w1[:, j * DV:(j + 1) * DV], B[:, j, :], v[:, j % TPB, (j // TPB) * DV:(j // TPB + 1) * DV],
                                         start=True, stop=True)
                    last.then_inc(z["o_made"], 1)
                    if f:
                        make_ok(m)
                        token_major(3 * P, w0, z["v_made"])
                        pe.wait_ge(z["o_taken"], n + 1)
                        token_major(5 * P, w1, z["g_made"])
                        pe.wait_ge(z["v_kept"], m + 1)
                    pe.wait_ge(z["o_ready"], n + 1)
                    for j in range(PROBS):
                        last = pe.transpose(w0[:, j * P:(j + 1) * P], o[:, j, :], G.ident[:, :])
                    last.then_inc(z["o_turned"], 1)
                    if f:
                        pe.wait_ge(z["gate_kept"], m + 1)
                    pe.wait_ge(z["wo_here"], (n // NBLK) * 16 + 16)
                    pe.wait_ge(z["ot_kept"], n + 2)
                    for t in range(TPB):
                        for h in range(2):
                            last = pe.matmul(w1[:, t * D:(t + 1) * D], oT[:, h * TPB + t, :], wo[:, h, :],
                                             start=(h == 0), stop=(h == 1))
                    last.then_inc(z["y_made"], 1)

                passes(pe, front_only, body)


def slot_layouts(a, i):
    HP, DV = 8, 128
    W = {m: i[f"L2_attn_W{m}"] for m in "qkvgs"}
    cut = lambda m: np.transpose(W[m].reshape(KC, P, HP, -1), (2, 1, 0, 3))
    a["a2_w"] = np.ascontiguousarray(np.concatenate([cut(m) for m in "qksvg"], axis=3))
    a["a2_wo"] = np.ascontiguousarray(np.transpose(i["L2_attn_Wo"].reshape(HP, 2, DV, D), (0, 2, 1, 3)))
    a["a2_gain"] = i["L2_attn_g_norm_weight"].reshape(1, DV)
    j, t = np.arange(P)[:, None], np.arange(P)[None, :]
    a["causal_T"] = ((j <= t) & (j // SEQ == t // SEQ)).astype(np.float32)
    a["causal_T_scaled"] = a["causal_T"] * np.float32(0.125)


MIXERS["a2"] = slot_attention


def delta_gates(nc, G, tag, d, g_all, b_all):
    NV = 32
    with Stage(nc, tag + "g") as st:
        w, ba = st.sb("w", [P, KC, 2 * NV]), st.sb("ba", [P, TILES, 2 * NV])
        dt, a_log = st.sb("dt", [P, NV]), st.sb("a_log", [P, NV])
        x, e, u, ln = (st.sb(m, [P, TILES, NV]) for m in ("x", "e", "u", "ln"))
        load(nc, [(w[:, :, :], d["a1_w_ba"]), (dt[:, :], d["a1_dt"].to_broadcast([P, NV])),
                  (a_log[:, :], d["a1_a_log"].to_broadcast([P, NV]))], st.sem("loaded"))
        tile_logits(nc, G, st, w, 2 * NV, ba)
        dstep, sized, exped, summed, logged, beta = (st.sem(m) for m in ("dstep", "sized", "exped", "summed", "logged", "beta"))
        by_pass = lambda ap: ap[:, :, :].rearrange("p (k b) (t h) -> p (b t) k h", k=16, h=2)
        by_head = lambda ap: ap.rearrange("p t (k h) -> p t k h", h=2)
        with nc.Block() as block:
            @block.vector
            def _(dve):
                step = Count(dve, dstep)
                step(dve.tensor_tensor(x[:, :, :], ba[:, :, NV:2 * NV], rows(dt[:, :], TILES), ALU.add))
                dve.scalar_tensor_tensor(e[:, :, :], x[:, :, :], -1.0, x[:, :, :], ALU.mult, ALU.max).then_inc(sized, 1)
                dve.wait_ge(exped, 1)
                dve.tensor_scalar(u[:, :, :], e[:, :, :], 1.0, None, ALU.add).then_inc(summed, 1)
                dve.wait_ge(summed, 1)
                step(dve.scalar_tensor_tensor(e[:, :, :], u[:, :, :], -1.0, e[:, :, :], ALU.add, ALU.subtract))
                dve.wait_ge(logged, 1)
                step(dve.reciprocal(u[:, :, :], u[:, :, :]))
                step(dve.tensor_tensor(e[:, :, :], e[:, :, :], u[:, :, :], ALU.mult))
                step(dve.tensor_tensor(ln[:, :, :], ln[:, :, :], e[:, :, :], ALU.subtract))
                step(dve.scalar_tensor_tensor(x[:, :, :], x[:, :, :], 0.0, ln[:, :, :], ALU.max, ALU.add))
                step(dve.tensor_scalar(a_log[:, :], a_log[:, :], -1.0, None, ALU.mult))
                step(dve.tensor_tensor(x[:, :, :], x[:, :, :], rows(a_log[:, :], TILES), ALU.mult))
                dve.wait_ge(beta, 1)
                step(dve.tensor_copy(by_pass(g_all), by_head(x[:, :, :])))
                step(dve.tensor_copy(by_pass(b_all), by_head(ba[:, :, 0:NV])))

            @block.scalar
            def _(act):
                act.wait_ge(sized, 1)
                act.activation(e[:, :, :], e[:, :, :], ACT.Exp, scale=-1.0)
                act.activation(a_log[:, :], a_log[:, :], ACT.Exp).then_inc(exped, 1)
                act.wait_ge(summed, 1)
                act.activation(ln[:, :, :], u[:, :, :], ACT.Ln).then_inc(logged, 1)
                act.activation(ba[:, :, 0:NV], ba[:, :, 0:NV], ACT.Sigmoid).then_inc(beta, 1)


def gated_delta(nc, G, tag, d):
    NK, DK, DV, TAPS = 16, 128, 128, 4
    PROBS, SEQS, PAD = 2 * TPB, BLK // SEQ, TAPS - 1
    PASSES = NK * NBLK
    LEVELS = 6
    RL = LEVELS - 1
    EPS = 1e-6
    GROUPS, GP = 2, PROBS // 2
    FRONT_STEPS, BACK_STEPS = 10, 5
    with Stage(nc, tag) as st:
        g_all, b_all = st.sb("g_all", [P, PASSES, PROBS]), st.sb("b_all", [P, PASSES, PROBS])
        delta_gates(nc, G, tag, d, g_all, b_all)
        w, wo, cw = st.sb("w", [P, KC, 6 * P]), st.sb("wo", [P, 2, D]), st.sb("cw", [P, 4, TAPS])
        gain, one = st.sb("gain", [P, DV]), st.sb("one", [P, 1])
        eye, upto, after = st.sb("eye", [P, SEQ]), st.sb("upto", [P, SEQ]), st.sb("after", [P, SEQ])
        strict, incl, level = st.sb("strict", [P, SEQ]), st.sb("incl", [P, SEQ]), st.sb("level", [P, LEVELS, SEQ])
        load(nc, [(gain[:, :], d["a1_gain"].to_broadcast([P, DV])), (one[:, :], d["ones_col"]), (eye[:, :], d["eye64"]),
                  (upto[:, :], d["upto64"]), (after[:, :], d["after64"]), (strict[:, :], d["strict64"]),
                  (incl[:, :], d["incl64_scaled"]), (level[:, :, :], d["level64"])], st.sem("loaded"))
        xt = st.sb("xt", [P, KC, BLK])
        pre, conv = st.sb("pre", [P, 4, SEQS, SEQ + PAD]), st.sb("conv", [P, 4, BLK])
        sq = st.sb("sq", [P, 2, BLK])
        V, U, zs = st.sb("V", [P, PROBS, DV]), st.sb("U", [P, PROBS, DV]), st.sb("zs", [P, PROBS, DV])
        gt, E = st.sb("gt", [P, PROBS, SEQ]), st.sb("E", [P, PROBS, SEQ])
        kk, kq = st.sb("kk", [P, TPB, SEQ]), st.sb("kq", [P, TPB, SEQ])
        N, A = st.sb("N", [P, PROBS, SEQ]), st.sb("A", [P, PROBS, SEQ])
        C = st.sb("C", [P, LEVELS, PROBS, SEQ])
        RR, Y = st.sb("RR", [P, GROUPS, 2, GP, SEQ]), st.sb("Y", [P, PROBS, SEQ])
        og, sq2, oT = st.sb("og", [P, PROBS, DV]), st.sb("sq2", [P, PROBS, DV]), st.sb("oT", [P, PROBS, P])
        ss, rt = st.sb("ss", [P, 2, PROBS]), st.sb("rt", [P, 2, PROBS])
        stat, bk = st.sb("stat", [P, PROBS]), st.sb("bk", [P, PROBS])
        qs = st.sb("qs", [P, 2, TPB])
        f = [st.ps(f"f{j}", [P, BLK]) for j in range(2)]
        pT = [st.ps(f"pT{g}", [P, BLK]) for g in range(GROUPS)]
        pn = pT[1][:, 0:PROBS]
        w0, w1 = st.ps("w0", [P, 2 * BLK]), st.ps("w1", [P, 2 * BLK])
        pRR = [w1[:, g * BLK:(g + 1) * BLK] for g in range(GROUPS)]
        names = ("w_here", "cw_here", "wo_here", "copied", "projected", "pre_kept", "convolved", "silued", "squared_qk",
                 "normed", "inverted", "rooted_qk", "z_made", "z_kept", "v_turned", "v_kept", "gt_ready", "decayed", "exped",
                 "kq_made", "n_ready", "c0_ready", "c_ready", "c_turned", "r_ready0", "r_ready1", "t_made0", "t_made1",
                 "t_kept0", "t_kept1", "step_made0", "step_made1",
                 "w_made", "u_kept", "o_made", "og_made", "squared", "var_ready", "rooted", "og_ready", "o_turned",
                 "ot_kept", "y_made", "done", "front_step", "back_step", "set_up")
        z = {m: st.sem(m) for m in names}
        v3 = lambda ap, n: ap.rearrange("p (j n) -> p j n", n=n)
        half = [slice(0, SEQ), slice(SEQ, P)]
        c64 = lambda j: slice(j * SEQ, (j + 1) * SEQ)

        def passes(eng, front_only, body):
            front_only()
            with eng.Fori(0, PASSES - 1) as n:
                body(n, n + 1)
            body(PASSES - 1, None)

        with nc.Block() as block:
            @block.sync
            def _(sp):
                def fetch(kh):
                    sp.wait_ge(z["z_made"], kh * NBLK + 1)
                    sp.dma_start(w[:, :, :], d["a1_w"][dyn(kh, 1)].rearrange("o p k n -> (o p) k n")).then_inc(z["w_here"], 16)
                    sp.wait_ge(z["convolved"], kh * NBLK + 1)
                    sp.dma_start(cw[:, :, :], d["a1_cw"][dyn(kh, 1)].rearrange("o p k n -> (o p) k n")).then_inc(z["cw_here"], 16)
                    sp.wait_ge(z["y_made"], kh * NBLK + 1)
                    sp.dma_start(wo[:, :, :], d["a1_wo"][dyn(kh, 1)].rearrange("o p k n -> (o p) k n")).then_inc(z["wo_here"], 16)

                with sp.Fori(0, NK) as kh:
                    fetch(kh)

            @block.gpsimd
            def _(pool):
                with pool.Fori(0, PASSES) as n:
                    pool.wait_ge(z["n_ready"], n + 1)
                    for l in range(1, LEVELS):
                        pool.tensor_tensor(C[:, l, :, :], N[:, :, :], rows(level[:, l, :], PROBS),
                                           ALU.mult).then_inc(z["c_ready"], 1)

            @block.scalar
            def _(act):
                def keep_pre(m, j):
                    act.wait_ge(z["projected"], m * 4 + j + 1)
                    act.copy(pre[:, j, :, PAD:], v3(f[j % 2][:, :], SEQ)).then_inc(z["pre_kept"], 1)

                def copy_x(m):
                    act.wait_ge(z["z_made"], m + 1)
                    act.wait_ge(z["convolved"], m + 1)
                    act.copy(xt[:, :, :], G.xT[:, :, dyn(m % NBLK, BLK)]).then_inc(z["copied"], 1)

                def decay(m):
                    act.wait_ge(z["decayed"], m + 1)
                    act.activation(E[:, :, :], v3(f[0][:, :], SEQ), ACT.Exp).then_inc(z["exped"], 1)

                def silu_conv(m):
                    act.wait_ge(z["convolved"], m + 2)
                    act.activation(conv[:, :, :], conv[:, :, :], ACT.Silu).then_inc(z["silued"], 1)
                    act.wait_ge(z["silued"], m + 1)
                    act.activation(sq[:, :, :], conv[:, 0:2, :], ACT.Square).then_inc(z["squared_qk"], 1)

                def silu_z(m):
                    act.wait_ge(z["z_made"], m + 2)
                    act.activation(zs[:, :, :], v3(w1[:, :], DV), ACT.Silu).then_inc(z["z_kept"], 1)

                def root_norms(m):
                    act.wait_ge(z["inverted"], m + 1)
                    act.activation(rt[:, :, :], ss[:, :, :], ACT.Sqrt).then_inc(z["rooted_qk"], 1)

                def keep_v(m):
                    act.wait_ge(z["rooted_qk"], m + 1)
                    act.wait_ge(z["v_turned"], m + 1)
                    for t in range(TPB):
                        last = act.activation(V[:, 2 * t:2 * t + 2, :], v3(w0[:, t * D:(t + 1) * D], DV), ACT.Copy,
                                              scale=rt[:, 0, TPB + t:TPB + t + 1])
                    last.then_inc(z["v_kept"], 1)

                def front_only():
                    copy_x(0)
                    for j in range(4):
                        keep_pre(0, j)
                    decay(0)
                    silu_conv(0)
                    root_norms(0)
                    keep_v(0)
                    silu_z(0)

                def body(n, m):
                    f_ = m is not None
                    if f_:
                        copy_x(m)
                        keep_pre(m, 0)
                        keep_pre(m, 1)
                    for l in range(1, LEVELS):
                        for g in range(GROUPS):
                            act.wait_ge(z[f"t_made{g}"], n * RL + l)
                            act.copy(Y[:, g * GP:(g + 1) * GP, :], v3(pT[g][:, 0:GP * SEQ], SEQ)).then_inc(z[f"t_kept{g}"], 1)
                        if f_ and l == 1:
                            keep_pre(m, 2)
                        if f_ and l == 2:
                            keep_pre(m, 3)
                        if f_ and l == 3:
                            decay(m)
                    if f_:
                        silu_conv(m)
                    act.wait_ge(z["w_made"], n + 1)
                    act.copy(U[:, :, :], v3(w0[:, :], DV)).then_inc(z["u_kept"], 1)
                    act.wait_ge(z["og_made"], n + 1)
                    act.activation(sq2[:, :, :], og[:, :, :], ACT.Square).then_inc(z["squared"], 1)
                    if f_:
                        root_norms(m)
                    act.wait_ge(z["var_ready"], n + 1)
                    act.activation(stat[:, :], stat[:, :], ACT.Sqrt).then_inc(z["rooted"], 1)
                    if f_:
                        keep_v(m)
                        silu_z(m)
                    act.wait_ge(z["o_turned"], n + 1)
                    act.copy(oT[:, :, :], v3(w0[:, :], P)).then_inc(z["ot_kept"], 1)

                passes(act, front_only, body)

            @block.vector
            def _(dve):
                prime(dve, z["done"], z["convolved"])
                step0 = Count(dve, z["set_up"])
                step0(dve.memset(pre[:, :, :, 0:PAD], 0.0))
                step0(dve.memset(G.y[:, :, :], 0.0))

                def of_pass(x, m):
                    return x[:, dyn(m, 1), :].rearrange("p o (j e) -> p (o j) e", e=1).to_broadcast([P, PROBS, SEQ])

                def gates(m):
                    if not isinstance(m, int):
                        dve.wait_ge(z["decayed"], m)
                    dve.tensor_tensor(gt[:, :, :], of_pass(g_all, m), rows(upto[:, :], PROBS), ALU.mult).then_inc(z["gt_ready"], 1)

                def convolve(m, step, pair, tap):
                    if pair == 0 and tap == 0:
                        dve.wait_ge(z["cw_here"], (m // NBLK) * 16 + 16)
                    if tap == 0:
                        dve.wait_ge(z["pre_kept"], m * 4 + 2 * pair + 2)
                    for j in (2 * pair, 2 * pair + 1):
                        out = v3(conv[:, j, :], SEQ)
                        src, scale = pre[:, j, :, tap:tap + SEQ], cw[:, j, tap:tap + 1]
                        if tap == 0:
                            last = dve.tensor_scalar(out, src, scale, None, ALU.mult)
                        else:
                            last = dve.scalar_tensor_tensor(out, src, scale, out, ALU.mult, ALU.add)
                    if pair == 1 and tap == TAPS - 1:
                        last.then_inc(z["convolved"], 1)
                    else:
                        step(last)

                def norms(m, step):
                    dve.wait_ge(z["normed"], m + 1)
                    step(dve.tensor_scalar(ss[:, 0, :], pn, EPS, None, ALU.add))
                    dve.reciprocal(ss[:, 1, :], ss[:, 0, :]).then_inc(z["inverted"], 1)

                def scale_decays(m, step):
                    dve.wait_ge(z["inverted"], m + 1)
                    step(dve.tensor_tensor(v3(bk[:, :], 2), b_all[:, dyn(m, 1), :].rearrange("p o (t h) -> p (o t) h", h=2),
                                           cols(ss[:, 1, TPB:PROBS], 2), ALU.mult))
                    dve.wait_ge(z["exped"], m + 1)
                    dve.tensor_tensor(E[:, :, :], E[:, :, :], cols(bk[:, :], SEQ), ALU.mult)
                    dve.wait_ge(z["kq_made"], m + 1)
                    b4 = f[1][:, :].rearrange("p (w t m) -> p w t m", w=2, m=SEQ)
                    dve.tensor_tensor(kq[:, :, :], b4[:, 0], rows(incl[:, :], TPB), ALU.mult)
                    step(dve.tensor_tensor(kk[:, :, :], b4[:, 1], rows(strict[:, :], TPB), ALU.mult))

                def matrices(m):
                    full = [P, TPB, 2, SEQ]
                    four = lambda ap: ap[:, :, :].rearrange("p (t h) m -> p t h m", h=2)
                    both = lambda ap: ap[:, :, :].rearrange("p t (o m) -> p t o m", o=1).to_broadcast(full)
                    dve.tensor_tensor(four(N), four(E), both(kk), ALU.mult).then_inc(z["n_ready"], 1)
                    dve.wait_ge(z["n_ready"], m + 1)
                    dve.tensor_tensor(C[:, 0, :, :], N[:, :, :], rows(level[:, 0, :], PROBS), ALU.mult).then_inc(z["c0_ready"], 1)
                    dve.tensor_tensor(four(A), four(E), both(kq), ALU.mult)
                    dve.wait_ge(z["c0_ready"], m + 1)
                    by_group = lambda ap: ap.rearrange("p (g j) n -> p g j n", g=GROUPS)
                    dve.tensor_tensor(RR[:, :, 0, :, :], by_group(rows(eye[:, :], PROBS)), by_group(C[:, 0, :, :]), ALU.subtract)

                def front_only():
                    step = Count(dve, z["front_step"], FRONT_STEPS, 0)
                    gates(0)
                    for pair in range(2):
                        for tap in range(TAPS):
                            convolve(0, step, pair, tap)
                    norms(0, step)
                    scale_decays(0, step)
                    matrices(0)

                def body(n, m):
                    f_ = m is not None
                    step = Count(dve, z["front_step"], FRONT_STEPS, m) if f_ else None
                    back = Count(dve, z["back_step"], BACK_STEPS, n)
                    dve.wait_ge(z["c_turned"], n + 1)
                    for g in range(GROUPS):
                        dve.tensor_tensor(RR[:, g, 1, :, :], rows(eye[:, :], GP), v3(pT[0][:, g * GP * SEQ:(g + 1) * GP * SEQ], SEQ),
                                          ALU.subtract).then_inc(z[f"r_ready{g}"], 1)
                    if f_:
                        gates(m)
                    for l in range(1, LEVELS):
                        for g in range(GROUPS):
                            dve.wait_ge(z[f"step_made{g}"], n * RL + l)
                            both = slice(0, 2 if l < RL else 1)
                            made = pRR[g].rearrange("p (w j n) -> p w j n", w=2, n=SEQ)
                            dve.tensor_tensor(RR[:, g, both], RR[:, g, both], made[:, both], ALU.subtract).then_inc(z[f"r_ready{g}"], 1)
                            unit = (l - 1) * GROUPS + g - 1
                            if f_ and 0 <= unit < 2 * TAPS:
                                convolve(m, step, unit // TAPS, unit % TAPS)
                    dve.wait_ge(z["o_made"], n + 1)
                    dve.tensor_tensor(og[:, :, :], v3(w1[:, :], DV), zs[:, :, :], ALU.mult).then_inc(z["og_made"], 1)
                    dve.tensor_copy(qs[:, 0, :], ss[:, 1, 0:TPB])
                    back(dve.tensor_copy(qs[:, 1, :], rt[:, 1, 0:TPB]))
                    if f_:
                        norms(m, step)
                    dve.wait_ge(z["squared"], n + 1)
                    by_tile = v3(stat[:, :], 2)
                    back(dve.tensor_reduce(stat[:, :], sq2[:, :, :], AX.X, ALU.add))
                    back(dve.tensor_tensor(by_tile, by_tile, cols(qs[:, 0, :], 2), ALU.mult))
                    dve.tensor_scalar(stat[:, :], stat[:, :], 1.0 / DV, EPS, ALU.mult, ALU.add).then_inc(z["var_ready"], 1)
                    dve.tensor_tensor(og[:, :, :], og[:, :, :], rows(gain[:, :], PROBS), ALU.mult)
                    if f_:
                        scale_decays(m, step)
                        matrices(m)
                        step.end()
                    dve.wait_ge(z["rooted"], n + 1)
                    back(dve.reciprocal(stat[:, :], stat[:, :]))
                    back(dve.tensor_tensor(by_tile, by_tile, cols(qs[:, 1, :], 2), ALU.mult))
                    dve.tensor_tensor(og[:, :, :], og[:, :, :], cols(stat[:, :], DV), ALU.mult).then_inc(z["og_ready"], 1)
                    back.end()
                    dve.wait_ge(z["y_made"], n + 2)
                    y = G.y[:, dyn(n % NBLK, TPB), :]
                    dve.tensor_tensor(y, y, v3(w1[:, :], D), ALU.add).then_inc(z["done"], 1)

                passes(dve, front_only, body)

            @block.tensor
            def _(pe):
                def each(out, lhsT, rhs, probs=range(PROBS)):
                    for j in probs:
                        for r in half:
                            last = pe.matmul(out(j, r), lhsT(j, r), rhs(j, r), start=True, stop=True)
                    return last

                bank = lambda b: lambda j, r: b[r, c64(j)]
                of = lambda x: lambda j, r: x[r, j, :]
                inv = lambda w: lambda j, r: RR[r, j // GP, w, j % GP, :]
                step_of = lambda w: lambda j, r: pRR[j // GP][r, c64(w * GP + j % GP)]

                def project(m, j):
                    if j == 0:
                        pe.wait_ge(z["w_here"], (m // NBLK) * 16 + 16)
                        pe.wait_ge(z["copied"], m + 1)
                    if j >= 2:
                        pe.wait_ge(z["pre_kept"], m * 4 + j - 1)
                    for k in range(KC):
                        last = pe.matmul(f[j % 2][:, :], w[:, k, j * P:(j + 1) * P], xt[:, k, :],
                                         start=(k == 0), stop=(k == KC - 1))
                    last.then_inc(z["projected"], 1)

                def decay_sums(m):
                    pe.wait_ge(z["pre_kept"], m * 4 + 3)
                    hold(pe, G, z["gt_ready"], m + 1, f[0][:, 0:1])
                    for r in half:
                        last = pe.matmul(f[0][r, :], after[r, :], gt[r, :, :], start=True, stop=True)
                    last.then_inc(z["decayed"], 1)

                def norm_sums(m):
                    pe.wait_ge(z["squared_qk"], m + 1)
                    for j in range(2):
                        for t in range(TPB):
                            last = pe.matmul(pn[:, j * TPB + t:j * TPB + t + 1], sq[:, j, t * P:(t + 1) * P], one[:, :],
                                             start=True, stop=True)
                    last.then_inc(z["normed"], 1)

                def key_products(m):
                    pe.wait_ge(z["pre_kept"], m * 4 + 4)
                    b4 = f[1][:, :].rearrange("p (w t m) -> p w t m", w=2, m=SEQ)
                    for t in range(TPB):
                        for s, r in enumerate(half):
                            c = c64(2 * t + s)
                            last = pe.matmul(b4[r, :, t, :], conv[:, 1, c], conv[:, 0:2, c], start=True, stop=True)
                    last.then_inc(z["kq_made"], 1)

                def project_z(m):
                    for t in range(TPB):
                        for k in range(KC):
                            last = pe.matmul(w1[:, t * D:(t + 1) * D], xt[:, k, t * P:(t + 1) * P], w[:, k, 4 * P:6 * P],
                                             start=(k == 0), stop=(k == KC - 1))
                    last.then_inc(z["z_made"], 1)

                def turn_v(m):
                    for t in range(TPB):
                        for h in range(2):
                            j = 2 * t + h
                            last = pe.transpose(w0[:, j * P:(j + 1) * P], conv[:, 2 + h, t * P:(t + 1) * P], G.ident[:, :])
                    last.then_inc(z["v_turned"], 1)

                def turn_level_0(m):
                    hold(pe, G, z["c0_ready"], m + 1, pT[0][:, 0:1])
                    each(bank(pT[0]), lambda j, r: C[r, 0, j, :], lambda j, r: eye[r, :]).then_inc(z["c_turned"], 1)

                def front_only():
                    prime(pe, z["z_made"], z["y_made"])
                    for j in range(4):
                        project(0, j)
                    decay_sums(0)
                    norm_sums(0)
                    key_products(0)
                    turn_v(0)
                    project_z(0)
                    turn_level_0(0)

                def body(n, m):
                    f_ = m is not None
                    if f_:
                        project(m, 0)
                        project(m, 1)
                    for l in range(1, LEVELS):
                        pe.wait_ge(z["c_ready"], n * RL + l)
                        if l == 1:
                            pe.wait_ge(z["r_ready1"], n * LEVELS + 1)
                        for g in range(GROUPS):
                            hold(pe, G, z[f"r_ready{g}"], n * LEVELS + l, pT[g][:, 0:1])
                            each(lambda j, r: pT[g][r, c64(j % GP)], lambda j, r: C[r, l, j, :], inv(1),
                                 range(g * GP, (g + 1) * GP)).then_inc(z[f"t_made{g}"], 1)
                        if f_ and l in (1, 2):
                            project(m, l + 1)
                        if f_ and l == 3:
                            decay_sums(m)
                        if l == 1:
                            pe.wait_ge(z["z_kept"], n + 1)
                            pe.wait_ge(z["done"], n + 1)
                        for g in range(GROUPS):
                            hold(pe, G, z[f"t_kept{g}"], n * RL + l, pRR[g][:, 0:1])
                            probs = range(g * GP, (g + 1) * GP)
                            last = each(step_of(0), of(Y), inv(0), probs)
                            if l < RL:
                                last = each(step_of(1), inv(0), of(Y), probs)
                            last.then_inc(z[f"step_made{g}"], 1)
                    pe.wait_ge(z["v_kept"], n + 1)
                    pe.wait_ge(z["r_ready1"], n * LEVELS + LEVELS)
                    hold(pe, G, z["r_ready0"], n * LEVELS + LEVELS, w0[:, 0:1])
                    each(lambda j, r: w0[r, j * DV:(j + 1) * DV], inv(0), of(V)).then_inc(z["w_made"], 1)
                    if f_:
                        norm_sums(m)
                    hold(pe, G, z["u_kept"], n + 1, w1[:, 0:1])
                    each(lambda j, r: w1[r, j * DV:(j + 1) * DV], of(A), of(U)).then_inc(z["o_made"], 1)
                    if f_:
                        key_products(m)
                        turn_v(m)
                        pe.wait_ge(z["og_made"], n + 1)
                        project_z(m)
                        turn_level_0(m)
                        pe.wait_ge(z["v_kept"], m + 1)
                    pe.wait_ge(z["og_ready"], n + 1)
                    for j in range(PROBS):
                        last = pe.transpose(w0[:, j * P:(j + 1) * P], og[:, j, :], G.ident[:, :])
                    last.then_inc(z["o_turned"], 1)
                    if f_:
                        pe.wait_ge(z["z_kept"], m + 1)
                    pe.wait_ge(z["wo_here"], (n // NBLK) * 16 + 16)
                    pe.wait_ge(z["ot_kept"], n + 1)
                    for t in range(TPB):
                        for h in range(2):
                            last = pe.matmul(w1[:, t * D:(t + 1) * D], oT[:, 2 * t + h, :], wo[:, h, :],
                                             start=(h == 0), stop=(h == 1))
                    last.then_inc(z["y_made"], 1)

                passes(pe, front_only, body)


def delta_layouts(a, i):
    NK = 16
    w = i["L1_attn_W_qkvz"].reshape(KC, P, NK, 6 * P)
    a["a1_w"] = np.ascontiguousarray(np.transpose(w, (2, 1, 0, 3)))
    a["a1_wo"] = np.ascontiguousarray(np.transpose(i["L1_attn_W_out"].reshape(NK, 2, P, D), (0, 2, 1, 3)))
    cw = i["L1_attn_conv_w"]
    qk = cw[:2 * NK * P].reshape(2, NK, P, 4)
    v = cw[2 * NK * P:].reshape(NK, 2, P, 4)
    a["a1_cw"] = np.ascontiguousarray(np.concatenate([np.transpose(qk, (1, 2, 0, 3)), np.transpose(v, (0, 2, 1, 3))], axis=2))
    ba = i["L1_attn_W_ba"].reshape(D, NK, 2, 2)
    a["a1_w_ba"] = in_rows(np.transpose(ba, (0, 2, 1, 3)).reshape(D, 64))
    a["a1_dt"], a["a1_a_log"] = i["L1_attn_dt_bias"].reshape(1, 32), i["L1_attn_A_log"].reshape(1, 32)
    a["a1_gain"] = i["L1_attn_norm_weight"].reshape(1, P)
    r, c = np.arange(P)[:, None] % SEQ, np.arange(SEQ)[None, :]
    f = lambda m: m.astype(np.float32)
    a["eye64"], a["upto64"], a["after64"], a["strict64"] = f(r == c), f(r <= c), f(r > c), f(r < c)
    a["incl64_scaled"] = f(r <= c) * np.float32(P ** -0.5)
    a["level64"] = np.ascontiguousarray(np.stack(
        [f((r >> (l + 1) == c >> (l + 1)) & (r >> l < c >> l)) for l in range(6)], axis=1))


MIXERS["a1"] = gated_delta


class Globals:
    pass


STAGES = ["a0", "x0", "f0", "a1", "x1", "f1", "a2", "x2", "f2", "a3", "x3", "f3"]


def decoder(nc, d, out):
    G = Globals()
    with Stage(nc, "g") as st:
        G.x_tok, G.y = st.sb("x_tok", [P, TILES, D]), st.sb("y", [P, TILES, D])
        G.xT = st.sb("xT", [P, KC, NTOK])
        G.ident, G.zero = st.sb("ident", [P, P]), st.sb("zero", [P, BLK])
        load(nc, [(G.x_tok[:, :, :], d["x_tok"]), (G.xT[:, :, :], d["xT"]), (G.ident[:, :], d["ident"]),
                  (G.zero[:, :], d["zero"])], st.sem("loaded"))
        for tag in STAGES:
            if tag in EXPERTS:
                gated_experts(nc, G, tag, d)
            else:
                MIXERS[tag](nc, G, tag, d)
            residual_norm(nc, G, tag)
        stored = st.sem("stored")
        with nc.Block() as block:
            @block.sync
            def _(sp):
                sp.dma_start(out, G.x_tok[:, :, :]).then_inc(stored, 16)
                sp.wait_ge(stored, 16)


def feature_major(w):
    return np.ascontiguousarray(np.transpose(w.reshape(w.shape[0], -1, P), (2, 1, 0)))


def in_rows(w):
    return np.ascontiguousarray(np.transpose(w.reshape(-1, P, w.shape[1]), (1, 0, 2)))


def pad_cols(w, n):
    return np.concatenate([w, np.zeros((w.shape[0], n - w.shape[1]), w.dtype)], axis=1)


def pack_experts(gate, up, down, owner):
    F = gate.shape[1]
    FT = -(-F // P)
    parts = []
    for w in (gate, up):
        w = pad_cols(w, FT * P).reshape(KC, P, FT, P)
        parts.append(np.transpose(w, (2, 1, 0, 3)))
    sel = np.zeros((P, FT * P), np.float32)
    sel[owner, np.arange(F)] = 1.0
    parts.append(np.transpose(sel.reshape(P, FT, 1, P), (1, 0, 2, 3)))
    down = np.concatenate([down, np.zeros((FT * P - F, D), down.dtype)], axis=0).reshape(FT, P, D)
    return np.ascontiguousarray(np.concatenate(parts, axis=2)), np.ascontiguousarray(down)


def owners(E, width, shared):
    return np.concatenate([np.repeat(np.arange(E), width), np.full(shared, E)])


def layouts(i):
    a = {}
    x = i["x"].reshape(TILES, P, D)
    a["x_tok"] = np.ascontiguousarray(np.transpose(x, (1, 0, 2)))
    a["xT"] = feature_major(i["x"].reshape(NTOK, D))
    a["ctx_tok"] = np.ascontiguousarray(np.transpose(i["ctx_2048"].reshape(TILES, P, D), (1, 0, 2)))
    a["ctxT"] = feature_major(i["ctx_2048"].reshape(NTOK, D))
    a["ident"] = np.eye(P, dtype=np.float32)
    a["zero"] = np.zeros((P, BLK), np.float32)
    for E in (4, 8, 16):
        a[f"before{E}"] = np.ascontiguousarray(np.broadcast_to(np.tri(E, k=-1, dtype=np.float32), (P, E, E)))
    I = 176
    gu = np.transpose(i["L0_ffn_w_gate_up"], (1, 0, 2))
    sh = i["L0_ffn_shared_gate_up"]
    a["f0_in_w"], a["f0_out_w"] = pack_experts(
        np.concatenate([gu[:, :, :I].reshape(D, -1), sh[:, :2 * I]], axis=1),
        np.concatenate([gu[:, :, I:].reshape(D, -1), sh[:, 2 * I:]], axis=1),
        np.concatenate([i["L0_ffn_w_down"].reshape(-1, D), i["L0_ffn_shared_down"]], axis=0), owners(16, I, 2 * I))
    a["f0_gate"] = feature_major(i["L0_ffn_gate_w"])
    gu = np.transpose(i["L2_ffn_gu_w"], (2, 0, 1))
    a["f2_in_w"], a["f2_out_w"] = pack_experts(
        np.concatenate([gu[:, :, :64].reshape(D, -1), i["L2_ffn_sh_gate_w"].T], axis=1),
        np.concatenate([gu[:, :, 64:].reshape(D, -1), i["L2_ffn_sh_up_w"].T], axis=1),
        np.concatenate([np.transpose(i["L2_ffn_dp_w"], (0, 2, 1)).reshape(-1, D), i["L2_ffn_sh_down_w"].T], axis=0),
        owners(64, 64, 64))
    a["f2_gate"] = feature_major(np.concatenate([i["L2_ffn_gate_w"], i["L2_ffn_sh_gate1_w"]], axis=0))
    a["f3_in_w"], a["f3_out_w"] = pack_experts(
        np.concatenate([np.transpose(i["L3_ffn_We_gate"], (1, 0, 2)).reshape(D, -1), i["L3_ffn_Ws_gate"]], axis=1),
        np.concatenate([np.transpose(i["L3_ffn_We_up"], (1, 0, 2)).reshape(D, -1), i["L3_ffn_Ws_up"]], axis=1),
        np.concatenate([i["L3_ffn_We_down"].reshape(-1, D), i["L3_ffn_Ws_down"]], axis=0), owners(8, I, 2 * I))
    a["f3_gate"] = in_rows(i["L3_ffn_W_router"])
    mixer_layouts(a, i)
    more_layouts(a, i)
    slot_layouts(a, i)
    delta_layouts(a, i)
    return a


def kernel(**inputs):
    import concourse.bacc as _bacc
    from concourse.bass_utils import run_bass_kernel_spmd as _run

    arrays = layouts({n: np.asarray(v) for n, v in inputs.items()})
    nc = _bacc.Bacc("TRN2", target_bir_lowering=False, num_devices=1)
    d = {n: nc.dram_tensor(f"in_{n}", arrays[n].shape, F32, kind="ExternalInput").ap() for n in arrays}
    out = nc.dram_tensor("out", (P, TILES, D), F32, kind="ExternalOutput").ap()
    decoder(nc, d, out)
    r = _run(nc, [{f"in_{n}": arrays[n] for n in arrays}], core_ids=[0])
    got = r.results[0]["out"]
    return np.ascontiguousarray(np.transpose(got, (1, 0, 2))).reshape(BATCH, SEQ, D)
```
